# Optimizing a Trainium2 kernel written in Bass

```python
import numpy as np
import jax
import jax.numpy as jnp

def _softmax(x, axis=-1):
    return jax.nn.softmax(x, axis=axis)

def _gelu(x):
    return jax.nn.gelu(x, approximate=True)

def _silu(x):
    return jax.nn.silu(x)

def _sigmoid(x):
    return jax.nn.sigmoid(x)

def _layernorm(x, axis=-1, eps=1e-05):
    m = jnp.mean(x, axis=axis, keepdims=True)
    v = jnp.var(x, axis=axis, keepdims=True)
    return (x - m) / jnp.sqrt(v + eps)

def _scatter_add(tgt, idx, src, axis=0):
    return tgt.at[idx].add(src)

def _segment_sum(src, seg, n):
    return jax.ops.segment_sum(src, seg, n)
kernel_name = 'mk_perceiver_d2_seqx_r8_d5acad'

def setup_inputs(seed: int=0):
    np.random.seed(seed)
    _w = jnp.asarray

    def _rec_inputs():
        import jax
        import jax.numpy as jnp
        _rk = jax.random.key(seed)
        x = 0.0002417 + 0.9998 * jax.random.normal(jax.random.fold_in(_rk, 1), (64, 32, 128), jnp.float32)
        _lenS = 32 - jax.random.randint(jax.random.fold_in(_rk, 7), (64,), 0, max(1, 32 // 4) + 1, jnp.int32)
        _lenS2 = 257 - jax.random.randint(jax.random.fold_in(_rk, 8), (64,), 0, max(1, 257 // 4) + 1, jnp.int32)
        _ctx_1024P = jax.random.normal(jax.random.fold_in(_rk, 11), (64, 16, 128), jnp.float32)
        _ctx_1024c = jax.random.dirichlet(jax.random.fold_in(_rk, 511), 0.3 * jnp.ones((16,), jnp.float32), (64, 257))
        _ctx_1024t = jnp.einsum('bsk,bkd->bsd', _ctx_1024c, _ctx_1024P)
        _ctx_1024t = _ctx_1024t * jax.lax.rsqrt(jnp.mean(jnp.square(_ctx_1024t)) + 1e-12) * 0.953939
        ctx_1024 = 7.22013e-05 + 1.00017 * (_ctx_1024t + 0.3 * jax.random.normal(jax.random.fold_in(_rk, 611), (64, 257, 128), jnp.float32))
        _validS = jnp.arange(32)[None, :] < _lenS[:, None]
        _validS2 = jnp.arange(257)[None, :] < _lenS2[:, None]
        _causal = jnp.tril(jnp.ones((32, 32), dtype=bool))
        mask_Bx1xSxS2_bk1 = jnp.broadcast_to(_validS2[:, None, None, :], (64, 1, 32, 257))
        return (x, ctx_1024, mask_Bx1xSxS2_bk1)
    x, ctx_1024, mask_Bx1xSxS2_bk1 = _rec_inputs()

    def _L0_xattn_setup():
        import jax, jax.numpy as jnp
        import numpy as np
        D_MODEL = 128
        B, S = (4, 256)
        key = jax.random.key(seed)
        ks = jax.random.split(key, 10)
        s = 1.0 / np.sqrt(D_MODEL)
        return {'k': jax.random.normal(ks[0], (B, S, D_MODEL), jnp.float32), 'v': jax.random.normal(ks[1], (B, S, D_MODEL), jnp.float32), 'q': jax.random.normal(ks[2], (B, S, D_MODEL), jnp.float32), 'Wk': jax.random.normal(ks[3], (D_MODEL, D_MODEL), jnp.float32) * s, 'Wv': jax.random.normal(ks[4], (D_MODEL, D_MODEL), jnp.float32) * s, 'bv': jnp.zeros((D_MODEL,), jnp.float32), 'Wq': jax.random.normal(ks[5], (D_MODEL, D_MODEL), jnp.float32) * s, 'bq': jnp.zeros((D_MODEL,), jnp.float32), 'Wo': jax.random.normal(ks[6], (D_MODEL, D_MODEL), jnp.float32) * s, 'bo': jnp.zeros((D_MODEL,), jnp.float32)}
    _L0_xattn_all = _L0_xattn_setup()
    _L0_xattn_in = {k: v for k, v in _L0_xattn_all.items() if k in ('Wk', 'Wv', 'bv', 'Wq', 'bq', 'Wo', 'bo')}
    del _L0_xattn_all

    def _L0_attn_setup():
        import jax, jax.numpy as jnp
        import numpy as np
        HIDDEN = 128
        STATE = 16
        BATCH = 4
        SEQ = 256
        LN_EPS = 1e-05

        def _selective_scan(x_ssm, dt, A, Bm, Cm):
            Bsz, L, D = x_ssm.shape
            N = A.shape[1]

            def step(h, inp):
                xt, dtt, bt, ct = inp
                dA = jnp.exp(A[None] * dtt[..., None])
                dB = dtt[..., None] * bt[:, None, :]
                h = dA * h + dB * xt[..., None]
                y = jnp.sum(h * ct[:, None, :], axis=-1)
                return (h, y)
            h0 = jnp.zeros((Bsz, D, N), x_ssm.dtype)
            xs = (jnp.swapaxes(x_ssm, 0, 1), jnp.swapaxes(dt, 0, 1), jnp.swapaxes(Bm, 0, 1), jnp.swapaxes(Cm, 0, 1))
            _, ys = jax.lax.scan(step, h0, xs)
            return jnp.swapaxes(ys, 0, 1)
        key = jax.random.key(seed)
        ks = jax.random.split(key, 16)
        D, N = (HIDDEN, STATE)
        s = 0.02
        return {'x': jax.random.normal(ks[0], (BATCH, SEQ, D), dtype=jnp.float32), 'w_in': jax.random.normal(ks[1], (2 * D, D), dtype=jnp.float32) * s, 'b_in': jnp.zeros((2 * D,), jnp.float32), 'w_dt': jax.random.normal(ks[2], (D, D), dtype=jnp.float32) * s, 'b_dt': jnp.zeros((D,), jnp.float32), 'A_log': jax.random.normal(ks[3], (D, N), dtype=jnp.float32), 'w_B': jax.random.normal(ks[4], (N, D), dtype=jnp.float32) * s, 'b_B': jnp.zeros((N,), jnp.float32), 'w_C': jax.random.normal(ks[5], (N, D), dtype=jnp.float32) * s, 'b_C': jnp.zeros((N,), jnp.float32), 'D': jnp.ones((D,), jnp.float32), 'w_out': jax.random.normal(ks[6], (D, D), dtype=jnp.float32) * s, 'b_out': jnp.zeros((D,), jnp.float32), 'gamma': jnp.ones((D,), jnp.float32), 'beta': jnp.zeros((D,), jnp.float32)}
    _L0_attn_all = _L0_attn_setup()
    _L0_attn_in = {k: v for k, v in _L0_attn_all.items() if k in ('w_in', 'b_in', 'w_dt', 'b_dt', 'A_log', 'w_B', 'b_B', 'w_C', 'b_C', 'D', 'w_out', 'b_out', 'gamma', 'beta')}
    del _L0_attn_all

    def _L0_ffn_setup():
        import jax, jax.numpy as jnp
        import numpy as np
        B, S, D_MODEL, D_HIDDEN = (4, 256, 128, 512)

        def act_quant(x):
            scale = 127.0 / jnp.clip(jnp.max(jnp.abs(x), axis=-1, keepdims=True), 1e-05)
            return jnp.clip(jnp.round(x * scale), -128, 127) / scale

        def weight_quant(w):
            scale = 1.0 / jnp.clip(jnp.mean(jnp.abs(w)), 1e-05)
            return jnp.clip(jnp.round(w * scale), -1, 1) / scale

        def bit_linear(x, w):
            xq = x + jax.lax.stop_gradient(act_quant(x) - x)
            wq = w + jax.lax.stop_gradient(weight_quant(w) - w)
            return jnp.einsum('bsd,hd->bsh', xq, wq)

        def depthwise_conv1d(x_bcl, w, b):
            y = jax.lax.conv_general_dilated(x_bcl, w, window_strides=(1,), padding=[(1, 1)], dimension_numbers=('NCH', 'OIH', 'NCH'), feature_group_count=x_bcl.shape[1])
            return y + b[None, :, None]
        key = jax.random.key(seed)
        ks = jax.random.split(key, 5)
        lim1 = 1.0 / np.sqrt(D_MODEL)
        lim2 = 1.0 / np.sqrt(D_HIDDEN)
        limc = 1.0 / np.sqrt(3.0)
        return {'x': jax.random.normal(ks[0], (B, S, D_MODEL), dtype=jnp.float32), 'w1': jax.random.uniform(ks[1], (D_HIDDEN, D_MODEL), jnp.float32, -lim1, lim1), 'conv_w': jax.random.uniform(ks[2], (D_HIDDEN, 1, 3), jnp.float32, -limc, limc), 'conv_b': jax.random.uniform(ks[3], (D_HIDDEN,), jnp.float32, -limc, limc), 'w2': jax.random.uniform(ks[4], (D_MODEL, D_HIDDEN), jnp.float32, -lim2, lim2)}
    _L0_ffn_all = _L0_ffn_setup()
    _L0_ffn_in = {k: v for k, v in _L0_ffn_all.items() if k in ('w1', 'conv_w', 'conv_b', 'w2')}
    del _L0_ffn_all

    def _L1_xattn_setup():
        import jax, jax.numpy as jnp
        import numpy as np
        D_MODEL = 128
        NUM_HEADS = 16
        D_K = D_MODEL // NUM_HEADS
        B, S = (2, 256)
        NEG = -1000000000.0

        def _split_heads(x):
            b, s, _ = x.shape
            return x.reshape(b, s, NUM_HEADS, D_K).transpose(0, 2, 1, 3)
        key = jax.random.key(seed)
        ks = jax.random.split(key, 12)
        scale = 1.0 / np.sqrt(D_MODEL)
        inp = {'q': jax.random.normal(ks[0], (B, S, D_MODEL), jnp.float32), 'k': jax.random.normal(ks[1], (B, S, D_MODEL), jnp.float32), 'v': jax.random.normal(ks[2], (B, S, D_MODEL), jnp.float32), 'mask': jax.random.randint(ks[3], (B, 1, S, S), 0, 2) == 1, 'w_q': jax.random.normal(ks[4], (D_MODEL, D_MODEL), jnp.float32) * scale, 'b_q': jnp.zeros((D_MODEL,), jnp.float32), 'w_k': jax.random.normal(ks[5], (D_MODEL, D_MODEL), jnp.float32) * scale, 'b_k': jnp.zeros((D_MODEL,), jnp.float32), 'w_v': jax.random.normal(ks[6], (D_MODEL, D_MODEL), jnp.float32) * scale, 'b_v': jnp.zeros((D_MODEL,), jnp.float32), 'w_o': jax.random.normal(ks[7], (D_MODEL, D_MODEL), jnp.float32) * scale, 'b_o': jnp.zeros((D_MODEL,), jnp.float32)}
        return inp
    _L1_xattn_all = _L1_xattn_setup()
    _L1_xattn_in = {k: v for k, v in _L1_xattn_all.items() if k in ('w_q', 'b_q', 'w_k', 'b_k', 'w_v', 'b_v', 'w_o', 'b_o')}
    del _L1_xattn_all

    def _L1_attn_setup():
        import jax, jax.numpy as jnp
        import numpy as np
        EPS = 1e-05

        def rwkv6_scan(q, k, v, w, u):
            B, H, T, K = q.shape
            V = v.shape[-1]
            h0 = jnp.zeros((B, H, K, V), jnp.float32)

            def step(h, xs):
                qi, ki, vi, wi = xs
                kv = ki[..., :, None] * vi[..., None, :]
                oi = jnp.einsum('bhk,bhkv->bhv', qi, h + u[None, :, :, None] * kv)
                h = h * jnp.exp(wi)[..., None] + kv
                return (h, oi)
            xs = tuple((jnp.moveaxis(a, 2, 0) for a in (q, k, v, w)))
            _, o = jax.lax.scan(step, h0, xs)
            return jnp.moveaxis(o, 0, 2)
        key = jax.random.key(seed)
        ks = jax.random.split(key, 20)
        B, T, D = (2, 256, 128)
        H, Dk, Dv = (4, 128, 32)
        KD, VD = (H * Dk, H * Dv)
        R5, LR = (5 * 32, 64)
        s = 0.02
        rn = lambda k, shp: jax.random.normal(k, shp, dtype=jnp.float32) * s
        return {'hidden_states': jax.random.normal(ks[0], (B, T, D), dtype=jnp.float32), 'xp_mu': rn(ks[1], (D,)), 'xp_W1': rn(ks[2], (R5, D)), 'xp_W2': rn(ks[3], (D, R5)), 'x_bias': rn(ks[4], (5, D)), 'r_W': rn(ks[5], (KD, D)), 'w_A': rn(ks[6], (LR, D)), 'w_B': rn(ks[7], (KD, LR)), 'w_b': rn(ks[8], (KD,)), 'k_W': rn(ks[9], (KD, D)), 'v_W': rn(ks[10], (VD, D)), 'g_A': rn(ks[11], (LR, D)), 'g_B': rn(ks[12], (VD, LR)), 'g_b': rn(ks[13], (VD,)), 'bonus': rn(ks[14], (H, Dk)), 'gn_w': jnp.ones((VD,), jnp.float32), 'gn_b': jnp.zeros((VD,), jnp.float32), 'o_W': rn(ks[15], (D, VD))}
    _L1_attn_all = _L1_attn_setup()
    _L1_attn_in = {k: v for k, v in _L1_attn_all.items() if k in ('xp_mu', 'xp_W1', 'xp_W2', 'x_bias', 'r_W', 'w_A', 'w_B', 'w_b', 'k_W', 'v_W', 'g_A', 'g_B', 'g_b', 'bonus', 'gn_w', 'gn_b', 'o_W')}
    del _L1_attn_all

    def _L1_ffn_setup():
        import jax, jax.numpy as jnp
        import numpy as np
        B, S, DIM, FFN, E = (4, 256, 128, 512, 8)
        key = jax.random.key(seed)
        k0, k1, k2, k3 = jax.random.split(key, 4)
        scale = 0.02
        return {'hidden_states': jax.random.normal(k0, (B, S, DIM), jnp.float32), 'router_w': jax.random.normal(k1, (DIM, E), jnp.float32) * scale, 'router_b': jnp.zeros((E,), jnp.float32), 'w1': jax.random.normal(k2, (E, DIM, 2 * FFN), jnp.float32) * scale, 'w2': jax.random.normal(k3, (E, FFN, DIM), jnp.float32) * scale}
    _L1_ffn_all = _L1_ffn_setup()
    _L1_ffn_in = {k: v for k, v in _L1_ffn_all.items() if k in ('router_w', 'router_b', 'w1', 'w2')}
    del _L1_ffn_all
    return {'x': x, 'ctx_1024': ctx_1024, 'mask_Bx1xSxS2_bk1': mask_Bx1xSxS2_bk1, 'L0_xattn_Wk': _L0_xattn_in['Wk'], 'L0_xattn_Wv': _L0_xattn_in['Wv'], 'L0_xattn_bv': _L0_xattn_in['bv'], 'L0_xattn_Wq': _L0_xattn_in['Wq'], 'L0_xattn_bq': _L0_xattn_in['bq'], 'L0_xattn_Wo': _L0_xattn_in['Wo'], 'L0_xattn_bo': _L0_xattn_in['bo'], 'L0_attn_w_in': _L0_attn_in['w_in'], 'L0_attn_b_in': _L0_attn_in['b_in'], 'L0_attn_w_dt': _L0_attn_in['w_dt'], 'L0_attn_b_dt': _L0_attn_in['b_dt'], 'L0_attn_A_log': _L0_attn_in['A_log'], 'L0_attn_w_B': _L0_attn_in['w_B'], 'L0_attn_b_B': _L0_attn_in['b_B'], 'L0_attn_w_C': _L0_attn_in['w_C'], 'L0_attn_b_C': _L0_attn_in['b_C'], 'L0_attn_D': _L0_attn_in['D'], 'L0_attn_w_out': _L0_attn_in['w_out'], 'L0_attn_b_out': _L0_attn_in['b_out'], 'L0_attn_gamma': _L0_attn_in['gamma'], 'L0_attn_beta': _L0_attn_in['beta'], 'L0_ffn_w1': _L0_ffn_in['w1'], 'L0_ffn_conv_w': _L0_ffn_in['conv_w'], 'L0_ffn_conv_b': _L0_ffn_in['conv_b'], 'L0_ffn_w2': _L0_ffn_in['w2'], 'L1_xattn_w_q': _L1_xattn_in['w_q'], 'L1_xattn_b_q': _L1_xattn_in['b_q'], 'L1_xattn_w_k': _L1_xattn_in['w_k'], 'L1_xattn_b_k': _L1_xattn_in['b_k'], 'L1_xattn_w_v': _L1_xattn_in['w_v'], 'L1_xattn_b_v': _L1_xattn_in['b_v'], 'L1_xattn_w_o': _L1_xattn_in['w_o'], 'L1_xattn_b_o': _L1_xattn_in['b_o'], 'L1_attn_xp_mu': _L1_attn_in['xp_mu'], 'L1_attn_xp_W1': _L1_attn_in['xp_W1'], 'L1_attn_xp_W2': _L1_attn_in['xp_W2'], 'L1_attn_x_bias': _L1_attn_in['x_bias'], 'L1_attn_r_W': _L1_attn_in['r_W'], 'L1_attn_w_A': _L1_attn_in['w_A'], 'L1_attn_w_B': _L1_attn_in['w_B'], 'L1_attn_w_b': _L1_attn_in['w_b'], 'L1_attn_k_W': _L1_attn_in['k_W'], 'L1_attn_v_W': _L1_attn_in['v_W'], 'L1_attn_g_A': _L1_attn_in['g_A'], 'L1_attn_g_B': _L1_attn_in['g_B'], 'L1_attn_g_b': _L1_attn_in['g_b'], 'L1_attn_bonus': _L1_attn_in['bonus'], 'L1_attn_gn_w': _L1_attn_in['gn_w'], 'L1_attn_gn_b': _L1_attn_in['gn_b'], 'L1_attn_o_W': _L1_attn_in['o_W'], 'L1_ffn_router_w': _L1_ffn_in['router_w'], 'L1_ffn_router_b': _L1_ffn_in['router_b'], 'L1_ffn_w1': _L1_ffn_in['w1'], 'L1_ffn_w2': _L1_ffn_in['w2']}

def reference(x, ctx_1024, mask_Bx1xSxS2_bk1, L0_xattn_Wk, L0_xattn_Wv, L0_xattn_bv, L0_xattn_Wq, L0_xattn_bq, L0_xattn_Wo, L0_xattn_bo, L0_attn_w_in, L0_attn_b_in, L0_attn_w_dt, L0_attn_b_dt, L0_attn_A_log, L0_attn_w_B, L0_attn_b_B, L0_attn_w_C, L0_attn_b_C, L0_attn_D, L0_attn_w_out, L0_attn_b_out, L0_attn_gamma, L0_attn_beta, L0_ffn_w1, L0_ffn_conv_w, L0_ffn_conv_b, L0_ffn_w2, L1_xattn_w_q, L1_xattn_b_q, L1_xattn_w_k, L1_xattn_b_k, L1_xattn_w_v, L1_xattn_b_v, L1_xattn_w_o, L1_xattn_b_o, L1_attn_xp_mu, L1_attn_xp_W1, L1_attn_xp_W2, L1_attn_x_bias, L1_attn_r_W, L1_attn_w_A, L1_attn_w_B, L1_attn_w_b, L1_attn_k_W, L1_attn_v_W, L1_attn_g_A, L1_attn_g_B, L1_attn_g_b, L1_attn_bonus, L1_attn_gn_w, L1_attn_gn_b, L1_attn_o_W, L1_ffn_router_w, L1_ffn_router_b, L1_ffn_w1, L1_ffn_w2):
    import jax
    import jax.numpy as jnp

    def _L0_xattn_ref(k, v, q, Wk, Wv, bv, Wq, bq, Wo, bo):
        import jax, jax.numpy as jnp
        import numpy as np
        D_MODEL = 128
        B, S = (4, 256)
        kp = jnp.einsum('bsd,ed->bse', k, Wk)
        vp = jnp.einsum('bsd,ed->bse', v, Wv) + bv
        qp = jnp.einsum('bsd,ed->bse', q, Wq) + bq
        scale = 1.0 / jnp.sqrt(jnp.float32(kp.shape[-1]))
        scores = jnp.einsum('bqd,bkd->bqk', qp, kp) * scale
        probs = jax.nn.softmax(scores, axis=-1)
        ctx = jnp.einsum('bqk,bkd->bqd', probs, vp)
        return jnp.einsum('bqd,ed->bqe', ctx, Wo) + bo

    def _L0_attn_ref(x, w_in, b_in, w_dt, b_dt, A_log, w_B, b_B, w_C, b_C, D, w_out, b_out, gamma, beta):
        import jax, jax.numpy as jnp
        import numpy as np
        HIDDEN = 128
        STATE = 16
        BATCH = 4
        SEQ = 256
        LN_EPS = 1e-05

        def _selective_scan(x_ssm, dt, A, Bm, Cm):
            Bsz, L, D = x_ssm.shape
            N = A.shape[1]

            def step(h, inp):
                xt, dtt, bt, ct = inp
                dA = jnp.exp(A[None] * dtt[..., None])
                dB = dtt[..., None] * bt[:, None, :]
                h = dA * h + dB * xt[..., None]
                y = jnp.sum(h * ct[:, None, :], axis=-1)
                return (h, y)
            h0 = jnp.zeros((Bsz, D, N), x_ssm.dtype)
            xs = (jnp.swapaxes(x_ssm, 0, 1), jnp.swapaxes(dt, 0, 1), jnp.swapaxes(Bm, 0, 1), jnp.swapaxes(Cm, 0, 1))
            _, ys = jax.lax.scan(step, h0, xs)
            return jnp.swapaxes(ys, 0, 1)
        residual = x
        xz = x @ w_in.T + b_in
        x_ssm, z = jnp.split(xz, 2, axis=-1)
        z = jax.nn.silu(z)
        dt = jax.nn.softplus(x_ssm @ w_dt.T + b_dt)
        Bm = x_ssm @ w_B.T + b_B
        Cm = x_ssm @ w_C.T + b_C
        A = -jnp.exp(A_log)
        y = _selective_scan(x_ssm, dt, A, Bm, Cm)
        y = y + D[None, None, :] * x_ssm
        y = y * z
        y = y @ w_out.T + b_out
        pre = y + residual
        mu = jnp.mean(pre, axis=-1, keepdims=True)
        var = jnp.mean(jnp.square(pre - mu), axis=-1, keepdims=True)
        return (pre - mu) * jax.lax.rsqrt(var + LN_EPS) * gamma + beta

    def _L0_ffn_ref(x, w1, conv_w, conv_b, w2):
        import jax, jax.numpy as jnp
        import numpy as np
        B, S, D_MODEL, D_HIDDEN = (4, 256, 128, 512)

        def act_quant(x):
            scale = 127.0 / jnp.clip(jnp.max(jnp.abs(x), axis=-1, keepdims=True), 1e-05)
            return jnp.clip(jnp.round(x * scale), -128, 127) / scale

        def weight_quant(w):
            scale = 1.0 / jnp.clip(jnp.mean(jnp.abs(w)), 1e-05)
            return jnp.clip(jnp.round(w * scale), -1, 1) / scale

        def bit_linear(x, w):
            xq = x + jax.lax.stop_gradient(act_quant(x) - x)
            wq = w + jax.lax.stop_gradient(weight_quant(w) - w)
            return jnp.einsum('bsd,hd->bsh', xq, wq)

        def depthwise_conv1d(x_bcl, w, b):
            y = jax.lax.conv_general_dilated(x_bcl, w, window_strides=(1,), padding=[(1, 1)], dimension_numbers=('NCH', 'OIH', 'NCH'), feature_group_count=x_bcl.shape[1])
            return y + b[None, :, None]
        h = bit_linear(x, w1)
        h = depthwise_conv1d(h.transpose(0, 2, 1), conv_w, conv_b)
        h = h.transpose(0, 2, 1)
        h = jax.nn.silu(h)
        return bit_linear(h, w2)

    def _L1_xattn_ref(q, k, v, mask, w_q, b_q, w_k, b_k, w_v, b_v, w_o, b_o):
        import jax, jax.numpy as jnp
        import numpy as np
        D_MODEL = 128
        NUM_HEADS = 16
        D_K = D_MODEL // NUM_HEADS
        B, S = (2, 256)
        NEG = -1000000000.0

        def _split_heads(x):
            b, s, _ = x.shape
            return x.reshape(b, s, NUM_HEADS, D_K).transpose(0, 2, 1, 3)
        qh = _split_heads(q @ w_q + b_q)
        kh = _split_heads(k @ w_k + b_k)
        vh = _split_heads(v @ w_v + b_v)
        scores = jnp.einsum('bhqd,bhkd->bhqk', qh, kh) / jnp.sqrt(jnp.asarray(D_K, jnp.float32))
        scores = jnp.where(mask, NEG, scores)
        attn = jax.nn.softmax(scores, axis=-1)
        out = jnp.einsum('bhqk,bhkd->bhqd', attn, vh)
        out = out.transpose(0, 2, 1, 3).reshape(q.shape[0], -1, D_MODEL)
        return out @ w_o + b_o

    def _L1_attn_ref(hidden_states, xp_mu, xp_W1, xp_W2, x_bias, r_W, w_A, w_B, w_b, k_W, v_W, g_A, g_B, g_b, bonus, gn_w, gn_b, o_W):
        import jax, jax.numpy as jnp
        import numpy as np
        EPS = 1e-05

        def rwkv6_scan(q, k, v, w, u):
            B, H, T, K = q.shape
            V = v.shape[-1]
            h0 = jnp.zeros((B, H, K, V), jnp.float32)

            def step(h, xs):
                qi, ki, vi, wi = xs
                kv = ki[..., :, None] * vi[..., None, :]
                oi = jnp.einsum('bhk,bhkv->bhv', qi, h + u[None, :, :, None] * kv)
                h = h * jnp.exp(wi)[..., None] + kv
                return (h, oi)
            xs = tuple((jnp.moveaxis(a, 2, 0) for a in (q, k, v, w)))
            _, o = jax.lax.scan(step, h0, xs)
            return jnp.moveaxis(o, 0, 2)
        B, T, D = hidden_states.shape
        H = bonus.shape[0]
        x = hidden_states
        shifted = jnp.pad(x, ((0, 0), (1, 0), (0, 0)))[:, :-1]
        delta = shifted - x
        xl = jnp.tanh((x + delta * xp_mu) @ xp_W1.T)
        xl = xl.reshape(B, T, 5, -1)
        W2 = xp_W2.reshape(D, 5, -1)
        x5 = jnp.einsum('blnr,hnr->blnh', xl, W2) + x_bias
        mur, muw, muk, muv, mug = (x5[:, :, i] for i in range(5))
        r = (x + delta * mur) @ r_W.T
        w = jnp.tanh((x + delta * muw) @ w_A.T) @ w_B.T + w_b
        k = (x + delta * muk) @ k_W.T
        v = (x + delta * muv) @ v_W.T
        g = jnp.tanh((x + delta * mug) @ g_A.T) @ g_B.T + g_b
        heads = lambda a: a.reshape(B, T, H, -1).transpose(0, 2, 1, 3)
        r, w, k, v = map(heads, (r, w, k, v))
        w = -jnp.exp(w)
        o = rwkv6_scan(r, k, v, w, bonus)
        o = o.transpose(0, 2, 1, 3).reshape(B, T, -1)
        mu = o.mean(-1, keepdims=True)
        var = ((o - mu) ** 2).mean(-1, keepdims=True)
        o = (o - mu) * jax.lax.rsqrt(var + EPS) * gn_w + gn_b
        o = o * (g * jax.nn.sigmoid(g))
        return o @ o_W.T

    def _L1_ffn_ref(hidden_states, router_w, router_b, w1, w2):
        import jax, jax.numpy as jnp
        import numpy as np
        B, S, DIM, FFN, E = (4, 256, 128, 512, 8)
        b, s, d = hidden_states.shape
        x = hidden_states.reshape(-1, d)
        logits = x @ router_w + router_b
        route = jax.nn.softmax(logits, axis=1)
        max_prob = jnp.max(route, axis=1, keepdims=True)
        max_ind = jnp.argmax(route, axis=1)
        out = jnp.zeros_like(x)
        num_experts = w1.shape[0]
        for e in range(num_experts):
            h = x @ w1[e]
            a, g = jnp.split(h, 2, axis=1)
            y = jax.nn.silu(a) * g @ w2[e]
            out = jnp.where((max_ind == e)[:, None], y, out)
        out = out * max_prob
        return out.reshape(b, s, d)
    x = x + _L0_xattn_ref(ctx_1024, ctx_1024, _layernorm(x, axis=-1), L0_xattn_Wk, L0_xattn_Wv, L0_xattn_bv, L0_xattn_Wq, L0_xattn_bq, L0_xattn_Wo, L0_xattn_bo)
    x = x + _L0_attn_ref(_layernorm(x, axis=-1), L0_attn_w_in, L0_attn_b_in, L0_attn_w_dt, L0_attn_b_dt, L0_attn_A_log, L0_attn_w_B, L0_attn_b_B, L0_attn_w_C, L0_attn_b_C, L0_attn_D, L0_attn_w_out, L0_attn_b_out, L0_attn_gamma, L0_attn_beta)
    x = x + _L0_ffn_ref(_layernorm(x, axis=-1), L0_ffn_w1, L0_ffn_conv_w, L0_ffn_conv_b, L0_ffn_w2)
    x = x + _L1_xattn_ref(_layernorm(x, axis=-1), ctx_1024, ctx_1024, mask_Bx1xSxS2_bk1, L1_xattn_w_q, L1_xattn_b_q, L1_xattn_w_k, L1_xattn_b_k, L1_xattn_w_v, L1_xattn_b_v, L1_xattn_w_o, L1_xattn_b_o)
    x = x + _L1_attn_ref(_layernorm(x, axis=-1), L1_attn_xp_mu, L1_attn_xp_W1, L1_attn_xp_W2, L1_attn_x_bias, L1_attn_r_W, L1_attn_w_A, L1_attn_w_B, L1_attn_w_b, L1_attn_k_W, L1_attn_v_W, L1_attn_g_A, L1_attn_g_B, L1_attn_g_b, L1_attn_bonus, L1_attn_gn_w, L1_attn_gn_b, L1_attn_o_W)
    x = x + _L1_ffn_ref(_layernorm(x, axis=-1), L1_ffn_router_w, L1_ffn_router_b, L1_ffn_w1, L1_ffn_w2)
    return x

_drawn_inputs = setup_inputs


def setup_inputs(seed=0):
    import zlib

    import numpy as np

    out = dict(_drawn_inputs(seed))
    spreads = {'L0_xattn_bv': (0.0, 0.1),
     'L0_xattn_bq': (0.0, 0.338),
     'L0_xattn_bo': (0.0, 0.1),
     'L0_attn_b_in': (0.0, 0.8),
     'L0_attn_b_dt': (0.0, 0.8),
     'L0_attn_b_B': (0.0, 0.8),
     'L0_attn_b_C': (0.0, 0.8),
     'L0_attn_D': (1.0, 0.6),
     'L0_attn_b_out': (0.0, 1.289),
     'L0_attn_gamma': (1.0, 0.2),
     'L0_attn_beta': (0.0, 0.1),
     'L1_xattn_b_q': (0.0, 0.734),
     'L1_xattn_b_k': (0.0, 2.0),
     'L1_xattn_b_v': (0.0, 0.1),
     'L1_xattn_b_o': (0.0, 0.1),
     'L1_attn_gn_w': (1.0, 0.6),
     'L1_attn_gn_b': (0.0, 0.8),
     'L1_ffn_router_b': (0.0, 0.8)}
    factors = {'L0_attn_w_in': 8.0,
     'L0_attn_w_dt': 8.0,
     'L0_attn_A_log': 8.0,
     'L0_attn_w_B': 8.0,
     'L0_attn_w_C': 8.0,
     'L0_attn_w_out': 8.0,
     'L1_attn_xp_mu': 8.0,
     'L1_attn_xp_W1': 8.0,
     'L1_attn_xp_W2': 8.0,
     'L1_attn_x_bias': 8.0,
     'L1_attn_r_W': 8.0,
     'L1_attn_w_A': 8.0,
     'L1_attn_w_B': 8.0,
     'L1_attn_w_b': 8.0,
     'L1_attn_k_W': 8.0,
     'L1_attn_v_W': 8.0,
     'L1_attn_g_A': 8.0,
     'L1_attn_g_B': 8.0,
     'L1_attn_g_b': 8.0,
     'L1_attn_bonus': 8.0,
     'L1_attn_o_W': 8.0,
     'L1_ffn_router_w': 8.0,
     'L1_ffn_w1': 8.0,
     'L1_ffn_w2': 8.0}
    for name, (base, spread) in spreads.items():
        noise = np.random.default_rng([zlib.crc32(name.encode()), seed]).standard_normal(out[name].shape)
        drawn = base * np.exp(spread * noise) if base else spread * noise
        out[name] = jnp.asarray(drawn.astype(out[name].dtype))
    for name, factor in factors.items():
        out[name] = (out[name] * factor).astype(out[name].dtype)
    return out
```

```python
from contextlib import ExitStack

import numpy as np

import concourse.bass as bass
from concourse import mybir

ALU = mybir.AluOpType
ACT = mybir.ActivationFunctionType
AX = mybir.AxisListType
F32 = mybir.dt.float32
BF16 = mybir.dt.bfloat16
U8 = mybir.dt.uint8

P = 128
B, S, D = 64, 32, 128
T = B * S
NT = T // P
CH = 512
NC = T // CH
TPC = CH // P
K2 = 257
K2P = 258
KW = 86
NSTATE = 16
HID = 512
NH, DK = 16, 8
RH = 4
NE = 8
EPS = 1e-5
MAGIC = 1.5 * 2.0 ** 23
NEG = -(2.0 ** 100)

WCOLS = [("wqT", 128), ("wk", 128), ("wvT", 128), ("woT", 128),
         ("winT", 256), ("wdtT", 128), ("wBT", 16), ("wCT", 16), ("woutT", 128),
         ("w1T", 512), ("w2T", 512),
         ("xq", 128), ("xk", 128), ("xv", 128), ("xo", 128),
         ("rW1T", 160), ("rW2Ta", 128), ("rW2Tb", 128), ("rrT", 512), ("rwAT", 64), ("rwBT", 512),
         ("rkT", 512), ("rvT", 128), ("rgAT", 64), ("rgBT", 128), ("roT", 128), ("router", 8)]
VCOLS = [("bq", 1), ("bv", 1), ("bin", 2), ("bdt", 1), ("alog", 16), ("Dskip", 1),
         ("convw", 12), ("convb", 4),
         ("xbq", 1), ("xbk", 1), ("xbv", 1),
         ("mu", 1), ("xbias", 5), ("wb", 4), ("gb", 1), ("bonus", 4), ("gnw", 1), ("gnb", 1)]
RCOLS = [("bo", 128), ("bout", 128), ("gamma", 128), ("beta", 128), ("xbo", 128),
         ("bB", 16), ("bC", 16), ("rb", 8)]
CCOLS = [("ident", 128), ("headsel", 128), ("negsel", 128), ("levels", 5 * 64), ("expert", 9 * 128), ("evals", 8), ("ones", 32)]


def columns(cols):
    at, out = 0, {}
    for name, n in cols:
        out[name] = (at, n)
        at += n
    return out, at


WAT, WN = columns(WCOLS)
VAT, VN = columns(VCOLS)
RAT, RN = columns(RCOLS)
CAT, CN = columns(CCOLS)
LEVELS = [1, 2, 4, 8, 16]


def shape_constants():
    c = np.zeros((P, CN), np.float32)
    at = lambda n: slice(CAT[n][0], CAT[n][0] + CAT[n][1])
    p = np.arange(P)
    c[:, at("ident")] = np.eye(P)
    c[:, at("headsel")] = (p[:, None] // DK % 4 == p[None, :] // S)
    c[:, at("negsel")] = np.where(p[:, None] % S == p[None, :] % S, NEG, 0.0)
    c[:, at("levels")] = np.concatenate([p[:, None] // n == 2 * (np.arange(64)[None, :] // n) for n in LEVELS], 1)
    e = np.zeros((P, NE + 1, P), np.float32)
    for i in range(NE):
        e[i, i, :] = 1.0
    c[:, at("expert")] = e.reshape(P, -1)
    c[:, at("ones")] = 1.0
    c[:, at("evals")] = NE - np.arange(NE)
    return c


def build_program(nc, x_d, ctxn_d, ctxT_d, mask_d, w_d, v_d, r_d, c_d, we_d, out_d, stop="F"):
    with ExitStack() as ctx:
        def sb(name, shape, dt=F32):
            return ctx.enter_context(nc.sbuf_tensor(name, shape, dt))

        sems = {}

        def sem(name):
            if name not in sems:
                sems[name] = ctx.enter_context(nc.semaphore(name))
            return sems[name]

        psum = ctx.enter_context(nc.psum_tensor("psum", [P, 8 * CH], F32))
        bank = [psum[:, i * CH:(i + 1) * CH] for i in range(8)]

        def banks(i, n):
            return psum[:, i * CH:(i + n) * CH]

        W = sb("weights", [P, WN])
        V = sb("vectors", [P, VN])
        R = sb("rows", [P, RN])
        C = sb("constants", [P, CN])
        x_tok = sb("x_tok", [P, NT, D])
        xn_tok = sb("xn_tok", [P, NT, D])
        xnT = sb("xnT", [P, T])
        ln_st = sb("ln_st", [P, NT, 6])
        ln_mv = sb("ln_mv", [P, NT, 2])
        ln_var = sb("ln_var", [P, NT])
        ln_rstd = sb("ln_rstd", [P, NT])
        zeros = sb("zeros", [P, CH], BF16)
        neg_half = sb("neg_half", [P, TPC])
        AR = 28800
        arena = sb("arena", [P, AR])
        ring = sb("ring", [P, 4, 4 * 3 * D])
        RING_AT = AR - 4 * 4 * K2P
        ctxT_ring = [arena[:, RING_AT + j * 4 * K2P:RING_AT + (j + 1) * 4 * K2P] for j in range(4)]

        def w(name, lo=0, hi=None, rows=P):
            a, n = WAT[name]
            return W[0:rows, a + lo:a + (n if hi is None else hi)]

        def vec(name, j=0):
            return V[:, VAT[name][0] + j:VAT[name][0] + j + 1]

        def row(name):
            return R[:, RAT[name][0]:RAT[name][0] + RAT[name][1]]

        def const(name, lo=0, hi=None):
            a, n = CAT[name]
            return C[:, a + lo:a + (n if hi is None else hi)]

        ident = const("ident")

        class Room:

            def __init__(self, at=0):
                self.at = at

            def take(self, n, dt=F32):
                words = n if dt == F32 else (n + 1) // 2
                a = arena[:, self.at:self.at + words]
                self.at += words
                assert self.at <= AR, self.at
                return a if dt == F32 else a.bitcast(dt)

        chain = {"dve": 0, "act": 0, "pool": 0}

        def link(eng, name, ins):
            chain[name] += 1
            ins.then_inc(sem(name + "_chain"), 1)
            eng.wait_ge(sem(name + "_chain"), chain[name])

        def ln_dve(dve, k, src, ready):
            for c in range(NC):
                ready(c)
                for t in range(4 * c, 4 * c + 4):
                    ins = dve.bn_stats(ln_st[:, t, :], src[:, t, :])
                link(dve, "dve", ins)
                for t in range(4 * c, 4 * c + 4):
                    ins = dve.bn_aggr(ln_mv[:, t, :], ln_st[:, t, :])
                link(dve, "dve", ins)
                dve.tensor_scalar(ln_var[:, 4 * c:4 * c + 4], ln_mv[:, 4 * c:4 * c + 4, 1], EPS, None,
                                  ALU.add).then_inc(sem("ln_var"), 1)
            for c in range(NC):
                dve.wait_ge(sem("ln_rstd"), NC * k + c + 1)
                for t in range(4 * c, 4 * c + 4):
                    ins = dve.tensor_scalar(xn_tok[:, t, :], src[:, t, :], ln_mv[:, t, 0:1],
                                            ln_rstd[:, t:t + 1], ALU.subtract, ALU.mult)
                ins.then_inc(sem("ln_xn"), 1)

        def ln_pool(pool, k):
            for c in range(NC):
                pool.wait_ge(sem("ln_var"), NC * k + c + 1)
                pool.tensor_tensor(ln_rstd[:, 4 * c:4 * c + 4], ln_var[:, 4 * c:4 * c + 4], neg_half[:, :],
                                   ALU.pow).then_inc(sem("ln_rstd"), 1)

        def ln_pe(pe, k, kt):
            for c in range(NC):
                pe.wait_ge(sem("ln_xn"), NC * k + c + 1)
                if c >= 2:
                    pe.wait_ge(sem("ln_T"), NC * kt + c - 1)
                for t in range(4):
                    ins = pe.transpose(bank[6 + c % 2][:, t * P:(t + 1) * P], xn_tok[:, 4 * c + t, :], ident)
                ins.then_inc(sem("ln_tr"), 1)

        def ln_act(act, kt):
            for c in range(NC):
                act.wait_ge(sem("ln_tr"), NC * kt + c + 1)
                act.activation(xnT[:, c * CH:(c + 1) * CH], bank[6 + c % 2][:, :], ACT.Copy)\
                   .then_inc(sem("ln_T"), 1)

        ra = Room()
        a_qT = ra.take(T)
        a_ctxn = [ring[:, j, :].rearrange("p (b k d) -> p b k d", b=4, k=3) for j in range(4)]
        a_ctxT = ctxT_ring
        a_qk = [ra.take(P) for _ in range(2)]
        a_nmax = [ra.take(1) for _ in range(2)]
        a_sum = [ra.take(1) for _ in range(2)]
        a_rs = [ra.take(1) for _ in range(2)]
        a_p = [ra.take(3 * KW) for _ in range(2)]
        a_pn = [ra.take(3 * KW) for _ in range(2)]
        a_pT = [ra.take(3 * P).rearrange("p (k n) -> p k n", k=3) for _ in range(2)]
        a_cx = [ra.take(P) for _ in range(2)]
        a_av = [ra.take(P) for _ in range(2)]

        def a_load(sp, j, g):
            sp.dma_start(a_ctxn[j][0:KW], ctxn_d[bass.ds(g, 1), :, :].rearrange("g p (b k d) -> p (g b) k d", b=4, k=3))\
              .then_inc(sem(f"a_ctx{j}"), 16)
            sp.dma_start(a_ctxT[j], ctxT_d[bass.ds(g, 1), :, :].rearrange("g p k -> p (g k)"))\
              .then_inc(sem(f"a_ctx{j}"), 16)

        def a_sp(sp):
            for j in range(4):
                a_load(sp, j, j)
            with sp.Fori(0, NT // 4 - 1) as r:
                i = r * 4
                for j in range(4):
                    sp.wait_ge(sem("a_pv"), i + j + 1)
                    a_load(sp, j, i + 4 + j)

        def a_pe(pe):
            ln_pe(pe, 0, 0)
            for c in range(NC):
                pe.wait_ge(sem("ln_T"), c + 1)
                pe.matmul(bank[c][:, :], w("wqT"), xnT[:, c * CH:(c + 1) * CH], start=True, stop=True)\
                  .then_inc(sem("a_qproj"), 1)
            pe.wait_ge(sem("a_qT"), NC)
            with pe.Fori(0, NT // 4) as r:
                i = r * 4
                for pair in (0, 2):
                    pe.wait_ge(sem("a_x"), i + pair + 1)
                    for u in (0, 1):
                        pe.matmul(bank[6 + u][:, 0:P], w("wk"), a_qT[:, bass.ds((i + pair + u) * P, P)],
                                  start=True, stop=True).then_inc(sem("a_q"), 1)
                    for u in (0, 1):
                        j = pair + u
                        pe.wait_ge(sem(f"a_ctx{j}"), i * 8 + 32)
                        pe.wait_ge(sem("a_qk"), i + j + 1)
                        for b in range(4):
                            ins = pe.matmul(bank[u][32 * b:32 * b + 32, 0:K2], a_qk[u][:, 32 * b:32 * b + 32],
                                            a_ctxT[j][:, b * K2P:b * K2P + K2], start=True, stop=True)
                        ins.then_inc(sem("a_s"), 1)
                    for u in (0, 1):
                        pe.wait_ge(sem("a_pn"), i + pair + u + 1)
                        for k in range(3):
                            ins = pe.transpose(bank[2 + u][0:KW, k * P:(k + 1) * P],
                                               a_pn[u][:, k * KW:(k + 1) * KW], ident)
                        ins.then_inc(sem("a_t"), 1)
                    for u in (0, 1):
                        j = pair + u
                        pe.wait_ge(sem("a_pT"), i + j + 1)
                        for b in range(4):
                            for k in range(3):
                                ins = pe.matmul(bank[4 + u][:, 32 * b:32 * b + 32], a_ctxn[j][0:KW, b, k, :],
                                                a_pT[u][0:KW, k, 32 * b:32 * b + 32], start=(k == 0), stop=(k == 2))
                        ins.then_inc(sem("a_pv"), 1)
                    for u in (0, 1):
                        pe.wait_ge(sem("a_cx"), i + pair + u + 1)
                        pe.matmul(bank[6 + u][:, P:2 * P], w("wvT"), a_cx[u], start=True, stop=True)\
                          .then_inc(sem("a_v"), 1)
                    for u in (0, 1):
                        pe.wait_ge(sem("a_av"), i + pair + u + 1)
                        pe.matmul(bank[6 + u][:, 2 * P:3 * P], a_av[u], w("woT"), start=True, stop=True)\
                          .then_inc(sem("a_o"), 1)

        def a_act(act):
            ln_act(act, 0)
            for c in range(NC):
                act.wait_ge(sem("a_qproj"), c + 1)
                act.activation(a_qT[:, c * CH:(c + 1) * CH], bank[c][:, :], ACT.Identity, bias=vec("bq"))\
                   .then_inc(sem("a_qT"), 1)
            with act.Fori(0, NT // 2) as r:
                i = r * 2
                for u in (0, 1):
                    act.wait_ge(sem("a_q"), i + u + 1)
                    act.activation(a_qk[u], bank[6 + u][:, 0:P], ACT.Copy, scale=float(D) ** -0.5)\
                       .then_inc(sem("a_qk"), 1)
                for u in (0, 1):
                    act.wait_ge(sem("a_max"), i + u + 1)
                    act.activation(a_p[u][:, 0:K2], bank[u][:, 0:K2], ACT.Exp, bias=a_nmax[u],
                                   accum_out=a_sum[u]).then_inc(sem("a_exp"), 1)
                for u in (0, 1):
                    act.wait_ge(sem("a_t"), i + u + 1)
                    act.activation(a_pT[u][0:KW], bank[2 + u][0:KW, 0:3 * P].rearrange("p (k n) -> p k n", k=3),
                                   ACT.Copy).then_inc(sem("a_pT"), 1)
                for u in (0, 1):
                    act.wait_ge(sem("a_v"), i + u + 1)
                    act.activation(a_av[u], bank[6 + u][:, P:2 * P], ACT.Identity, bias=vec("bv"))\
                       .then_inc(sem("a_av"), 1)

        def a_pool(pool):
            ln_pool(pool, 0)

        def a_dve(dve):
            dve.wait_ge(sem("x_load"), 16)
            ln_dve(dve, 0, x_tok, lambda c: None)
            for u in (0, 1):
                ins = dve.memset(a_pn[u][:, K2:3 * KW], 0.0)
            link(dve, "dve", ins)
            dve.wait_ge(sem("row_load"), 16)
            link(dve, "dve", dve.tensor_tensor(x_tok[:, :, :], x_tok[:, :, :],
                                               row("bo").unsqueeze(1).broadcast_to([P, NT, D]), ALU.add))
            dve.nop().then_inc(sem("a_x"), 1)
            with dve.Fori(0, NT // 2) as r:
                i = r * 2
                for u in (0, 1):
                    dve.wait_ge(sem("a_s"), i + u + 1)
                    dve.tensor_reduce(a_nmax[u], bank[u][:, 0:K2], AX.X, ALU.max, negate=True)\
                       .then_inc(sem("a_max"), 1)
                for u in (0, 1):
                    dve.wait_ge(sem("a_exp"), i + u + 1)
                    dve.reciprocal(a_rs[u], a_sum[u]).then_inc(sem("a_rs"), 1)
                for u in (0, 1):
                    dve.wait_ge(sem("a_rs"), i + u + 1)
                    dve.tensor_scalar(a_pn[u][:, 0:K2], a_p[u][:, 0:K2], a_rs[u], None, ALU.mult)\
                       .then_inc(sem("a_pn"), 1)
                for u in (0, 1):
                    dve.wait_ge(sem("a_pv"), i + u + 1)
                    dve.tensor_copy(a_cx[u], bank[4 + u][:, 0:P]).then_inc(sem("a_cx"), 1)
                for u in (0, 1):
                    dve.wait_ge(sem("a_o"), i + u + 1)
                    xt = x_tok[:, bass.ds(i + u, 1), :].rearrange("p a d -> p (a d)")
                    dve.tensor_tensor(xt, bank[6 + u][:, 2 * P:3 * P], xt, ALU.add)\
                       .then_inc(sem("a_x"), 1)

        rb_ = Room()
        b_xs, b_z, b_dt, b_dtx, b_y = (rb_.take(T) for _ in range(5))
        b_t1, b_t2 = (rb_.take(T) for _ in range(2))
        b_a = [rb_.take(T) for _ in range(2)]
        HT = T // 2
        b_u = [rb_.take(HT) for _ in range(2)]
        b_h = [rb_.take(HT) for _ in range(2)]
        b_hc = [rb_.take(HT) for _ in range(4)]
        b_aneg = rb_.take(NSTATE)
        b_aexp = rb_.take(NSTATE)
        b_pre = b_t1.rearrange("p (t d) -> p t d", d=D)

        def steps(a):
            return a.rearrange("p (b s) -> p b s", s=S)

        def b_pool(pool):
            ln_pool(pool, 1)
            pool.wait_ge(sem("ln_xn"), 2 * NC)
            pool.wait_ge(sem("ln_T"), 2 * NC)
            pool.tensor_tensor(xn_tok[:, :, :], xn_tok[:, :, :],
                               row("bout").unsqueeze(1).broadcast_to([P, NT, D]), ALU.add)\
                .then_inc(sem("b_res"), 1)
            pool.tensor_tensor(x_tok[:, :, :], x_tok[:, :, :],
                               row("beta").unsqueeze(1).broadcast_to([P, NT, D]), ALU.add)\
                .then_inc(sem("b_res"), 1)
            pool.wait_ge(sem("b_skip"), 1)
            for q in range(2 * NSTATE):
                hf = q % 2
                y = b_y[:, hf * HT:(hf + 1) * HT]
                pool.wait_ge(sem("b_hc"), q + 1)
                if q >= 2:
                    pool.wait_ge(sem("b_yadd"), q - 1)
                pool.tensor_tensor(y, y, b_hc[q % 4], ALU.add).then_inc(sem("b_yadd"), 1)
            ln_pool(pool, 2)

        def b_pe(pe):
            ln_pe(pe, 1, 1)
            for c in range(NC):
                pe.wait_ge(sem("ln_T"), NC + c + 1)
                xc = xnT[:, c * CH:(c + 1) * CH]
                pe.matmul(bank[c], w("winT", 0, D), xc, start=True, stop=True).then_inc(sem("b_xsp"), 1)
                if c >= 2:
                    pe.wait_ge(sem("b_z"), c - 1)
                pe.matmul(bank[4 + c % 2], w("winT", D, 2 * D), xc, start=True, stop=True)\
                  .then_inc(sem("b_zp"), 1)
            for c in range(NC):
                pe.wait_ge(sem("b_xs"), c + 1)
                pe.matmul(bank[c], w("wdtT"), b_xs[:, c * CH:(c + 1) * CH], start=True, stop=True)\
                  .then_inc(sem("b_dtp"), 1)
            pe.wait_ge(sem("b_relu"), NC)
            pe.wait_ge(sem("b_abs"), NC)
            pe.wait_ge(sem("b_z"), NC)
            for q in range(2 * NSTATE):
                n, hf = q // 2, q % 2
                for which, name, used, done in ((0, "wBT", "b_u", "b_B"), (2, "wCT", "b_hc", "b_C")):
                    if q >= 2:
                        pe.wait_ge(sem(used), q - 1)
                    for c in range(2):
                        at = hf * HT + c * CH
                        ins = pe.matmul(bank[4 * hf + which + c], w(name, n, n + 1).broadcast_to([P, P]),
                                        b_xs[:, at:at + CH], start=True, stop=True)
                    ins.then_inc(sem(done), 1)
            for c in range(NC):
                if c < 2:
                    pe.wait_ge(sem("b_yz"), c + 1)
                for t in range(4):
                    tt = 4 * c + t
                    ins = pe.matmul(bank[c][:, t * P:(t + 1) * P], b_y[:, tt * P:(tt + 1) * P], w("woutT"),
                                    start=True, stop=True)
                ins.then_inc(sem("b_out"), 1)

        def b_act(act):
            ln_act(act, 1)
            for c in range(NC):
                act.wait_ge(sem("b_xsp"), c + 1)
                act.activation(b_xs[:, c * CH:(c + 1) * CH], bank[c], ACT.Identity, bias=vec("bin", 0))\
                   .then_inc(sem("b_xs"), 1)
                act.wait_ge(sem("b_zp"), c + 1)
                act.activation(b_z[:, c * CH:(c + 1) * CH], bank[4 + c % 2], ACT.Silu, bias=vec("bin", 1))\
                   .then_inc(sem("b_z"), 1)
            for c in range(NC):
                act.wait_ge(sem("b_relu"), c + 1)
                act.activation(b_t1[:, c * CH:(c + 1) * CH], bank[c], ACT.Abs, bias=vec("bdt"))\
                   .then_inc(sem("b_abs"), 1)
            act.activation(b_aexp, V[:, VAT["alog"][0]:VAT["alog"][0] + NSTATE], ACT.Exp)\
               .then_inc(sem("b_aexp"), 1)
            act.wait_ge(sem("b_abs"), NC)
            link(act, "act", act.activation(b_t2, b_t1, ACT.Exp, scale=-1.0))
            act.activation(b_t1, b_t2, ACT.Ln, bias=1.0).then_inc(sem("b_log1p"), 1)
            act.wait_ge(sem("b_dt"), 1)
            act.wait_ge(sem("b_azero"), 1)
            for n in range(NSTATE):
                if n >= 2:
                    act.wait_ge(sem("b_scan"), 2 * (n - 1))
                act.activation(steps(b_a[n % 2])[:, :, 1:S], steps(b_dt)[:, :, 1:S], ACT.Exp,
                               scale=b_aneg[:, n:n + 1]).then_inc(sem("b_a"), 1)

        def b_dve(dve):
            ln_dve(dve, 1, x_tok, lambda c: dve.wait_ge(sem("a_x"), TPC * (c + 1) + 1))
            for j in range(2):
                ins = dve.memset(steps(b_a[j])[:, :, 0], 0.0)
            ins.then_inc(sem("b_azero"), 1)
            for c in range(NC):
                dve.wait_ge(sem("b_dtp"), c + 1)
                dve.tensor_scalar(b_dt[:, c * CH:(c + 1) * CH], bank[c], vec("bdt"), 0.0, ALU.add, ALU.max)\
                   .then_inc(sem("b_relu"), 1)
            dve.wait_ge(sem("b_aexp"), 1)
            link(dve, "dve", dve.tensor_scalar(b_aneg, b_aexp, -1.0, None, ALU.mult))
            dve.wait_ge(sem("b_log1p"), 1)
            link(dve, "dve", dve.tensor_tensor(b_dt, b_dt, b_t1, ALU.add))
            dve.tensor_tensor(b_dtx, b_dt, b_xs, ALU.mult).then_inc(sem("b_dt"), 1)
            dve.tensor_scalar(b_y, b_xs, vec("Dskip"), None, ALU.mult).then_inc(sem("b_skip"), 1)
            dve.wait_ge(sem("b_dt"), 1)
            dve.wait_ge(sem("row_load"), 16)
            bB, bC = row("bB"), row("bC")
            for n in range(NSTATE):
                for hf in (0, 1):
                    q = 2 * n + hf
                    half = slice(hf * HT, (hf + 1) * HT)
                    dve.wait_ge(sem("b_B"), q + 1)
                    if q >= 2:
                        dve.wait_ge(sem("b_scan"), q - 1)
                    dve.scalar_tensor_tensor(out=b_u[hf], in0=banks(4 * hf, 2), scalar=bB[:, n:n + 1],
                                             in1=b_dtx[:, half], op0=ALU.add, op1=ALU.mult)\
                       .then_inc(sem("b_u"), 1)
                for hf in (0, 1):
                    q = 2 * n + hf
                    half = slice(hf * HT, (hf + 1) * HT)
                    dve.wait_ge(sem("b_a"), n + 1)
                    dve.wait_ge(sem("b_u"), q + 1)
                    dve.tensor_tensor_scan(b_h[hf], b_a[n % 2][:, half], b_u[hf], 0.0, ALU.mult, ALU.add)\
                       .then_inc(sem("b_scan"), 1)
                for hf in (0, 1):
                    q = 2 * n + hf
                    dve.wait_ge(sem("b_C"), q + 1)
                    dve.wait_ge(sem("b_scan"), q + 1)
                    if q >= 4:
                        dve.wait_ge(sem("b_yadd"), q - 3)
                    dve.scalar_tensor_tensor(out=b_hc[q % 4], in0=banks(4 * hf + 2, 2), scalar=bC[:, n:n + 1],
                                             in1=b_h[hf], op0=ALU.add, op1=ALU.mult)\
                       .then_inc(sem("b_hc"), 1)
            for hf in (0, 1):
                dve.wait_ge(sem("b_yadd"), 2 * NSTATE - 1 + hf)
                y = b_y[:, hf * HT:(hf + 1) * HT]
                dve.tensor_tensor(y, y, b_z[:, hf * HT:(hf + 1) * HT], ALU.mult).then_inc(sem("b_yz"), 1)
            dve.wait_ge(sem("b_res"), 2)
            for c in range(NC):
                dve.wait_ge(sem("b_out"), c + 1)
                dve.tensor_tensor(b_pre[:, 4 * c:4 * c + 4, :], bank[c].rearrange("p (t d) -> p t d", d=D),
                                  xn_tok[:, 4 * c:4 * c + 4, :], ALU.add).then_inc(sem("b_pre"), 1)
            ln_dve(dve, 2, b_pre, lambda c: dve.wait_ge(sem("b_pre"), c + 1))
            for c in range(NC):
                tiles = slice(4 * c, 4 * c + 4)
                dve.wait_ge(sem("ln_xn"), 2 * NC + c + 1)
                dve.tensor_tensor(b_pre[:, tiles, :], xn_tok[:, tiles, :],
                                  row("gamma").unsqueeze(1).broadcast_to([P, TPC, D]), ALU.mult)\
                   .then_inc(sem("b_gam"), 1)
            for c in range(NC):
                tiles = slice(4 * c, 4 * c + 4)
                dve.wait_ge(sem("b_gam"), c + 1)
                dve.tensor_tensor(x_tok[:, tiles, :], x_tok[:, tiles, :], b_pre[:, tiles, :], ALU.add)\
                   .then_inc(sem("x_done"), 1)

        rc = Room()
        c_w1f, c_w2f = rc.take(HID), rc.take(HID)
        c_w1q, c_w2q = rc.take(HID, BF16), rc.take(HID, BF16)
        c_identb = rc.take(P, BF16)
        c_wsum, c_wmean, c_winv = rc.take(2), rc.take(2), rc.take(2)
        c_ones = rc.take(P)
        c_q = rc.take(T, BF16).rearrange("p (t d) -> p t d", d=D)
        c_qT = rc.take(T, BF16)
        c_m, c_s, c_dq = rc.take(2 * NT), rc.take(2 * NT), rc.take(2 * NT)
        c_R = rc.take(T)
        c_hp = [rc.take(B * (S + 2)).rearrange("p (b s) -> p b s", s=S + 2) for _ in range(2)]
        c_t = [rc.take(T) for _ in range(2)]
        c_hs = [rc.take(T) for _ in range(4)]
        c_qf = c_t[0].rearrange("p (t d) -> p t d", d=D)
        c_q2f = [rc.take(HID) for _ in range(4)]
        c_q2 = [rc.take(HID, BF16) for _ in range(4)]
        c_q2T = [rc.take(HID, BF16).rearrange("p (k n) -> p k n", k=4) for _ in range(4)]

        def quant_scales(dve, at, n, which):
            m, s, d = c_m[:, at:at + n], c_s[:, at:at + n], c_dq[:, at:at + n]
            link(dve, "dve", dve.tensor_scalar(m, m, 1e-5, None, ALU.max))
            link(dve, "dve", dve.reciprocal(s, m))
            dve.tensor_scalar(d, m, 1.0 / 127.0, c_wmean[:, which:which + 1], ALU.mult, ALU.mult)
            link(dve, "dve", dve.tensor_scalar(s, s, 127.0, None, ALU.mult))

        def c_pool(pool):
            ln_pool(pool, 3)

        def c_dve(dve):
            link(dve, "dve", dve.memset(c_ones, 1.0))
            for k, name in enumerate(("w1T", "w2T")):
                ins = dve.tensor_reduce(c_wsum[:, k:k + 1], w(name), AX.X, ALU.add, apply_absolute_value=True)
            ins.then_inc(sem("c_wsum"), 1)
            for j in range(2):
                dve.memset(c_hp[j][:, :, 0], 0.0)
                ins = dve.memset(c_hp[j][:, :, S + 1], 0.0)
            link(dve, "dve", ins)
            dve.tensor_copy(c_identb, ident).then_inc(sem("c_identb"), 1)
            dve.wait_ge(sem("c_wtot"), 1)
            link(dve, "dve", dve.tensor_scalar(c_wmean, bank[0][:, 0:2], 1.0 / (D * HID), 1e-5, ALU.mult, ALU.max))
            link(dve, "dve", dve.reciprocal(c_winv, c_wmean))
            for k, (name, f, q) in enumerate((("w1T", c_w1f, c_w1q), ("w2T", c_w2f, c_w2q))):
                link(dve, "dve", dve.tensor_scalar(f, w(name), c_winv[:, k:k + 1], MAGIC, ALU.mult, ALU.add))
                link(dve, "dve", dve.tensor_scalar(f, f, MAGIC, 1.0, ALU.subtract, ALU.min))
                dve.tensor_scalar(q, f, -1.0, None, ALU.max).then_inc(sem("c_wq"), 1)
            ln_dve(dve, 3, x_tok, lambda c: dve.wait_ge(sem("x_done"), c + 1))
            for c in range(NC):
                tiles = slice(4 * c, 4 * c + 4)
                dve.wait_ge(sem("ln_xn"), 3 * NC + c + 1)
                link(dve, "dve", dve.tensor_reduce(c_m[:, tiles], xn_tok[:, tiles, :], AX.X, ALU.max,
                                                   apply_absolute_value=True))
                quant_scales(dve, 4 * c, 4, 0)
                dve.nop().then_inc(sem("c_scale"), 1)
                for t in range(4 * c, 4 * c + 4):
                    ins = dve.tensor_scalar(c_qf[:, t, :], xn_tok[:, t, :], c_s[:, t:t + 1], MAGIC, ALU.mult, ALU.add)
                link(dve, "dve", ins)
                dve.tensor_scalar(c_q[:, tiles, :], c_qf[:, tiles, :], MAGIC, None, ALU.subtract)\
                   .then_inc(sem("c_q"), 1)
            def conv(j):
                for n, (tap, lo) in enumerate(((0, 0), (2, 2))):
                    dve.wait_ge(sem("c_mid"), j + 1)
                    if n:
                        dve.wait_ge(sem("c_left"), j + 1)
                    dve.scalar_tensor_tensor(out=steps(c_t[j % 2]), in0=c_hp[j % 2][:, :, lo:lo + S],
                                             scalar=vec("convw", 3 * j + tap), in1=steps(c_t[j % 2]),
                                             op0=ALU.mult, op1=ALU.add)\
                       .then_inc(sem("c_right" if n else "c_left"), 1)

            for j in range(4):
                for c in range(NC):
                    k = 4 * j + c
                    dve.wait_ge(sem("c_h"), k + 1)
                    dve.wait_ge(sem("c_R"), c + 1)
                    if j >= 2:
                        dve.wait_ge(sem("c_right"), j - 1)
                    dve.tensor_tensor(c_hp[j % 2][:, 16 * c:16 * c + 16, 1:S + 1], steps(bank[k % 4]),
                                      steps(c_R[:, c * CH:(c + 1) * CH]), ALU.mult).then_inc(sem("c_hp"), 1)
                if j >= 1:
                    conv(j - 1)
            conv(3)
            for g in range(NC):
                for t in range(4):
                    dve.wait_ge(sem("c_ht"), 4 * g + t + 1)
                    ins = dve.tensor_reduce(c_m[:, NT + 4 * g + t:NT + 4 * g + t + 1], bank[t], AX.X, ALU.max,
                                            apply_absolute_value=True)
                link(dve, "dve", ins)
                quant_scales(dve, NT + 4 * g, 4, 1)
                dve.nop().then_inc(sem("c_scale2"), 1)
                for t in range(4):
                    dve.wait_ge(sem("c_q2f"), 4 * g + t + 1)
                    if g >= 1:
                        dve.wait_ge(sem("c_q2t"), 4 * (g - 1) + t + 1)
                    dve.tensor_scalar(c_q2[t], c_q2f[t], MAGIC, None, ALU.subtract).then_inc(sem("c_q2"), 1)
                for t in range(4):
                    tt = 4 * g + t
                    dve.wait_ge(sem("c_o"), tt + 1)
                    ins = dve.scalar_tensor_tensor(out=x_tok[:, tt, :], in0=bank[6 + t % 2][:, 0:D],
                                                   scalar=c_dq[:, NT + tt:NT + tt + 1], in1=x_tok[:, tt, :],
                                                   op0=ALU.mult, op1=ALU.add)
                    ins.then_inc(sem("c_x"), 1)
                dve.wait_ge(sem("c_x"), 4 * g + 4)
                dve.nop().then_inc(sem("x_done"), 1)

        def c_pe(pe):
            pe.wait_ge(sem("c_wsum"), 1)
            pe.matmul(bank[0][:, 0:2], c_ones, c_wsum, start=True, stop=True).then_inc(sem("c_wtot"), 1)
            pe.wait_ge(sem("c_identb"), 1)
            for c in range(NC):
                pe.wait_ge(sem("c_scale"), c + 1)
                for t in range(4):
                    ins = pe.matmul(bank[4 + c % 2][:, t * P:(t + 1) * P],
                                    c_dq[:, 4 * c + t:4 * c + t + 1].broadcast_to([P, P]), ident,
                                    start=True, stop=True)
                ins.then_inc(sem("c_Rp"), 1)
                pe.wait_ge(sem("c_q"), c + 1)
                for t in range(4):
                    ins = pe.transpose(bank[6 + c % 2][:, t * 64:(t + 1) * 64].bitcast(BF16), c_q[:, 4 * c + t, :],
                                       c_identb)
                ins.then_inc(sem("c_qt"), 1)
                if c >= 1:
                    pe.wait_ge(sem("c_R"), c)
                    pe.wait_ge(sem("c_qT"), c)
            pe.wait_ge(sem("c_wq"), 2)
            for k in range(16):
                j, c = k // 4, k % 4
                pe.wait_ge(sem("c_qT"), c + 1)
                if k >= 4:
                    pe.wait_ge(sem("c_hp"), k - 3)
                pe.matmul(bank[k % 4], c_w1q[:, j * P:(j + 1) * P], c_qT[:, c * CH:(c + 1) * CH],
                          start=True, stop=True).then_inc(sem("c_h"), 1)
            pe.wait_ge(sem("c_hp"), 16)
            pe.wait_ge(sem("c_hs"), 4)

            def to_tokens(tt):
                for j in range(4):
                    ins = pe.transpose(bank[tt % 4][:, j * P:(j + 1) * P], c_hs[j][:, tt * P:(tt + 1) * P], ident)
                ins.then_inc(sem("c_ht"), 1)

            for tt in range(4):
                to_tokens(tt)
            for tt in range(NT):
                pe.wait_ge(sem("c_q2"), tt + 1)
                if tt >= 2:
                    pe.wait_ge(sem("c_q2T"), tt - 1)
                for j in range(4):
                    ins = pe.transpose(bank[4 + tt % 2][:, j * 64:(j + 1) * 64].bitcast(BF16),
                                       c_q2[tt % 4][:, j * P:(j + 1) * P], c_identb)
                ins.then_inc(sem("c_q2t"), 1)
                pe.wait_ge(sem("c_q2T"), tt + 1)
                if tt >= 2:
                    pe.wait_ge(sem("c_x"), tt - 1)
                for j in range(4):
                    ins = pe.matmul(bank[6 + tt % 2][:, 0:D], c_q2T[tt % 4][:, j, :], c_w2q[:, j * P:(j + 1) * P],
                                    start=(j == 0), stop=(j == 3))
                ins.then_inc(sem("c_o"), 1)
                if tt + 4 < NT:
                    to_tokens(tt + 4)

        def c_act(act):
            for c in range(NC):
                act.wait_ge(sem("c_Rp"), c + 1)
                act.activation(c_R[:, c * CH:(c + 1) * CH], bank[4 + c % 2], ACT.Copy).then_inc(sem("c_R"), 1)
                act.wait_ge(sem("c_qt"), c + 1)
                act.activation(c_qT[:, c * CH:(c + 1) * CH], bank[6 + c % 2][:, 0:CH // 2].bitcast(BF16), ACT.Copy)\
                   .then_inc(sem("c_qT"), 1)

            def silu(j):
                act.wait_ge(sem("c_right"), j + 1)
                act.activation(c_hs[j], c_t[j % 2], ACT.Silu).then_inc(sem("c_hs"), 1)

            for j in range(4):
                if j >= 2:
                    silu(j - 2)
                    act.wait_ge(sem("c_hs"), j - 1)
                act.wait_ge(sem("c_hp"), 4 * j + 4)
                act.activation(steps(c_t[j % 2]), c_hp[j % 2][:, :, 1:S + 1], ACT.Identity,
                               scale=vec("convw", 3 * j + 1), bias=vec("convb", j)).then_inc(sem("c_mid"), 1)
            silu(2)
            silu(3)
            for g in range(NC):
                act.wait_ge(sem("c_scale2"), g + 1)
                for t in range(4):
                    tt = 4 * g + t
                    if g >= 1:
                        act.wait_ge(sem("c_q2"), tt - 3)
                    act.activation(c_q2f[t], bank[t], ACT.Copy, scale=c_s[:, NT + tt:NT + tt + 1], bias=MAGIC)\
                       .then_inc(sem("c_q2f"), 1)
                for t in range(4):
                    tt = 4 * g + t
                    act.wait_ge(sem("c_q2t"), tt + 1)
                    act.activation(c_q2T[t], bank[4 + tt % 2][:, 0:CH // 2].bitcast(BF16)
                                   .rearrange("p (k n) -> p k n", k=4), ACT.Copy).then_inc(sem("c_q2T"), 1)


        rd = Room()
        d_qT, d_aT = rd.take(T), rd.take(T)
        d_qb = [rd.take(P) for _ in range(2)]
        d_mb = [rd.take(K2 + 1, BF16) for _ in range(2)]
        d_neg = rd.take(P, BF16)
        d_kT = [rd.take(K2P) for _ in range(2)]
        d_v = [rd.take(3 * P).rearrange("p (k n) -> p k n", k=3) for _ in range(2)]
        d_p = [rd.take(4 * K2P).rearrange("p (c k) -> p c k", c=4) for _ in range(2)]
        d_nmax = [rd.take(4) for _ in range(2)]
        d_sum = [rd.take(4) for _ in range(2)]
        d_rs = [rd.take(4) for _ in range(2)]
        d_pT = rd.take(4 * 3 * P).rearrange("p (c k n) -> p c k n", c=4, k=3)
        d_tmp = rd.take(P)
        d_msk = [rd.take(68).bitcast(U8) for _ in range(4)]
        assert rd.at <= RING_AT
        STEPS = B // 4 - 1

        def d_load(sp, j, r):
            sp.dma_start(ctxT_ring[j][:, 0:K2P],
                         ctxT_d[bass.ds(r, 1), :, j * K2P:(j + 1) * K2P].rearrange("g p k -> p (g k)"))\
              .then_inc(sem(f"d_ctx{j}"), 16)
            for c in range(4):
                sp.dma_start(d_msk[j][32 * c:32 * c + 32, 0:K2],
                             mask_d[bass.ds(4 * r + j, 1), :, :].rearrange("g s k -> s (g k)"))\
                  .then_inc(sem(f"d_ctx{j}"), 16)

        def d_sp(sp):
            sp.wait_ge(sem("x_done"), 2 * NC)
            for j in range(4):
                d_load(sp, j, 0)
            with sp.Fori(0, STEPS) as r:
                for j in range(4):
                    sp.wait_ge(sem("d_vp"), r * 4 + j + 1)
                    sp.wait_ge(sem("d_mb"), r * 4 + j + 1)
                    d_load(sp, j, r + 1)

        def d_pool(pool):
            ln_pool(pool, 4)
            pool.wait_ge(sem("ln_xn"), 5 * NC)
            pool.tensor_tensor(x_tok[:, :, :], x_tok[:, :, :],
                               row("xbo").unsqueeze(1).broadcast_to([P, NT, D]), ALU.add)\
                .then_inc(sem("d_xbo"), 1)
            pool.wait_ge(sem("d_qT"), NC)

            def operands(b, j, r):
                pool.wait_ge(sem(f"d_ctx{j}"), r * 80 + 80)
                pool.tensor_tensor(d_qb[j % 2].rearrange("p (h s) -> p h s", h=4),
                                   const("headsel").rearrange("p (h s) -> p h s", h=4),
                                   d_qT[:, bass.ds(b * S, S)].unsqueeze(1).broadcast_to([P, 4, S]),
                                   ALU.mult)
                pool.tensor_copy(d_mb[j % 2][:, 0:K2], d_msk[j][:, 0:K2]).then_inc(sem("d_mb"), 1)

            operands(0, 0, 0)
            operands(1, 1, 0)
            with pool.Fori(0, STEPS) as r:
                for j in range(4):
                    pool.wait_ge(sem("d_s"), r * 8 + 2 * j + 2)
                    operands(r * 4 + j + 2, (j + 2) % 4, r + (j + 2) // 4)
            for j in range(2):
                pool.wait_ge(sem("d_s"), STEPS * 8 + 2 * j + 2)
                operands(STEPS * 4 + j + 2, j + 2, STEPS)

        def d_pe(pe):
            ln_pe(pe, 4, 2)
            for c in range(NC):
                pe.wait_ge(sem("ln_T"), 2 * NC + c + 1)
                pe.matmul(bank[c], w("xq"), xnT[:, c * CH:(c + 1) * CH], start=True, stop=True)\
                  .then_inc(sem("d_qp"), 1)
            pe.wait_ge(sem("d_neg"), 1)
            pe.wait_ge(sem("d_qT"), NC)

            def project_k(b, j, r):
                pe.wait_ge(sem(f"d_ctx{j}"), r * 80 + 80)
                pe.wait_ge(sem("d_v"), b)
                pe.matmul(bank[7][:, 0:K2P], w("xk"), ctxT_ring[j][:, 0:K2P], start=True, stop=True)\
                  .then_inc(sem("d_kp"), 1)

            def project_v(b, j):
                pe.wait_ge(sem("d_kT"), b + 1)
                for k in range(3):
                    ins = pe.matmul(bank[7][0:KW, k * P:(k + 1) * P], ctxT_ring[j][:, k * KW:(k + 1) * KW],
                                    w("xv"), start=True, stop=True)
                ins.then_inc(sem("d_vp"), 1)

            def scores(b, j, half, first=False):
                if half == 0:
                    pe.wait_ge(sem("d_mb"), b + 1)
                if not first:
                    pe.wait_ge(sem("d_exp"), b * 2 - 1 + half)
                for c in (2 * half, 2 * half + 1):
                    rows = slice(32 * c, 32 * c + 32)
                    pe.matmul(bank[c][:, 0:K2], d_qb[j % 2][rows, :], d_kT[j % 2][rows, 0:K2], start=True, stop=False)
                    ins = pe.matmul(bank[c][:, 0:K2], d_neg[rows, :], d_mb[j % 2][rows, 0:K2], start=False, stop=True)
                ins.then_inc(sem("d_s"), 1)

            def transposed(b, j, c):
                if c % 2 == 0:
                    pe.wait_ge(sem("d_pn"), b * 2 + 1 + c // 2)
                if c >= 2:
                    pe.wait_ge(sem("d_pT"), b * 3 + c - 1)
                for k in range(3):
                    ins = pe.transpose(bank[4 + c % 2][0:KW, k * P:(k + 1) * P],
                                       d_p[j % 2][:, c, k * KW:(k + 1) * KW], ident)
                ins.then_inc(sem("d_t"), 1)

            def averages(b, j):
                pe.wait_ge(sem("d_pT"), b * 3 + 3)
                pe.wait_ge(sem("d_pT3"), b + 1)
                pe.wait_ge(sem("d_diag"), b + 1)
                for k in range(3):
                    for c in range(4):
                        ins = pe.matmul(bank[6][32 * c:32 * c + 32, 0:P], d_v[j % 2][0:KW, k, 32 * c:32 * c + 32],
                                        d_pT[0:KW, c, k, :], start=(k == 0), stop=(k == 2))
                ins.then_inc(sem("d_pv"), 1)

            def step(b, j, r, last=False):
                n, jn, rn = b + 1, (j + 1) % 4, r + (j + 1) // 4
                if not last:
                    project_k(n, jn, rn)
                transposed(b, j, 0)
                transposed(b, j, 1)
                if not last:
                    project_v(n, jn)
                transposed(b, j, 2)
                if not last:
                    scores(n, jn, 0)
                transposed(b, j, 3)
                averages(b, j)
                if not last:
                    scores(n, jn, 1)

            project_k(0, 0, 0)
            project_v(0, 0)
            scores(0, 0, 0, first=True)
            scores(0, 0, 1, first=True)
            with pe.Fori(0, STEPS) as r:
                for j in range(4):
                    step(r * 4 + j, j, r)
            for j in range(4):
                step(STEPS * 4 + j, j, STEPS, last=(j == 3))
            pe.wait_ge(sem("d_aT"), B)
            for c in range(NC):
                for t in range(4):
                    tt = 4 * c + t
                    ins = pe.matmul(bank[c][:, t * P:(t + 1) * P], d_aT[:, tt * P:(tt + 1) * P], w("xo"),
                                    start=True, stop=True)
                ins.then_inc(sem("d_out"), 1)

        def d_act(act):
            ln_act(act, 2)

            def projections(b, j):
                act.wait_ge(sem("d_kp"), b + 1)
                act.activation(d_kT[j % 2], bank[7][:, 0:K2P], ACT.Identity, bias=vec("xbk")).then_inc(sem("d_kT"), 1)
                act.wait_ge(sem("d_vp"), b + 1)
                act.activation(d_v[j % 2][0:KW], bank[7][0:KW, 0:3 * P].rearrange("p (k n) -> p k n", k=3), ACT.Copy)\
                   .then_inc(sem("d_v"), 1)

            def exps(b, j, half):
                act.wait_ge(sem("d_max"), b * 2 + 1 + half)
                for c in (2 * half, 2 * half + 1):
                    ins = act.activation(d_p[j % 2][:, c, 0:K2], bank[c][:, 0:K2], ACT.Exp,
                                         bias=d_nmax[j % 2][:, c:c + 1], accum_out=d_sum[j % 2][:, c:c + 1])
                ins.then_inc(sem("d_exp"), 1)

            def step(b, j, last=False):
                if not last:
                    projections(b + 1, (j + 1) % 4)
                act.wait_ge(sem("d_t"), b * 4 + 4)
                act.activation(d_pT[0:KW, 3], bank[5][0:KW, 0:3 * P].rearrange("p (k n) -> p k n", k=3), ACT.Copy)\
                   .then_inc(sem("d_pT3"), 1)
                if not last:
                    exps(b + 1, (j + 1) % 4, 0)
                    exps(b + 1, (j + 1) % 4, 1)

            projections(0, 0)
            exps(0, 0, 0)
            exps(0, 0, 1)
            with act.Fori(0, STEPS) as r:
                for j in range(4):
                    step(r * 4 + j, j)
            for j in range(4):
                step(STEPS * 4 + j, j, last=(j == 3))

        def d_dve(dve):
            ln_dve(dve, 4, x_tok, lambda c: dve.wait_ge(sem("x_done"), NC + c + 1))
            dve.tensor_copy(d_neg, const("negsel")).then_inc(sem("d_neg"), 1)
            for u in range(2):
                ins = dve.memset(d_p[u][:, :, K2], 0.0)
            link(dve, "dve", ins)
            for c in range(NC):
                dve.wait_ge(sem("d_qp"), c + 1)
                dve.tensor_scalar(d_qT[:, c * CH:(c + 1) * CH], bank[c], vec("xbq"), float(DK) ** -0.5,
                                  ALU.add, ALU.mult).then_inc(sem("d_qT"), 1)

            def maxima(b, j, half):
                dve.wait_ge(sem("d_s"), b * 2 + 1 + half)
                cs = slice(2 * half, 2 * half + 2)
                dve.tensor_reduce(d_nmax[j % 2][:, cs],
                                  banks(2 * half, 2).rearrange("p (c k) -> p c k", c=2)[:, :, 0:K2],
                                  AX.X, ALU.max, negate=True).then_inc(sem("d_max"), 1)

            def normalised(b, j, half):
                cs = slice(2 * half, 2 * half + 2)
                dve.wait_ge(sem("d_exp"), b * 2 + 1 + half)
                dve.reciprocal(d_rs[j % 2][:, cs], d_sum[j % 2][:, cs]).then_inc(sem("d_rs"), 1)
                dve.wait_ge(sem("d_rs"), b * 2 + 1 + half)
                for c in (2 * half, 2 * half + 1):
                    ins = dve.tensor_scalar(d_p[j % 2][:, c, 0:K2], d_p[j % 2][:, c, 0:K2],
                                            d_rs[j % 2][:, c:c + 1], None, ALU.mult)
                ins.then_inc(sem("d_pn"), 1)

            def step(b, j, last=False):
                for c in range(3):
                    dve.wait_ge(sem("d_t"), b * 4 + c + 1)
                    dve.tensor_copy(d_pT[0:KW, c], bank[4 + c % 2][0:KW, 0:3 * P]
                                    .rearrange("p (k n) -> p k n", k=3)).then_inc(sem("d_pT"), 1)
                if not last:
                    maxima(b + 1, (j + 1) % 4, 0)
                dve.wait_ge(sem("d_pv"), b + 1)
                dve.scalar_tensor_tensor(out=d_tmp, in0=bank[6][:, 0:P], scalar=vec("xbv"), in1=const("headsel"),
                                         op0=ALU.add, op1=ALU.mult).then_inc(sem("d_diag"), 1)
                if not last:
                    maxima(b + 1, (j + 1) % 4, 1)
                    normalised(b + 1, (j + 1) % 4, 0)
                dve.wait_ge(sem("d_diag"), b + 2)
                dve.tensor_reduce(d_aT[:, bass.ds(b * S, S)], d_tmp.rearrange("p (h s) -> p s h", h=4),
                                  AX.X, ALU.add).then_inc(sem("d_aT"), 1)
                if not last:
                    normalised(b + 1, (j + 1) % 4, 1)

            dve.nop().then_inc(sem("d_diag"), 1)
            maxima(0, 0, 0)
            maxima(0, 0, 1)
            normalised(0, 0, 0)
            normalised(0, 0, 1)
            with dve.Fori(0, STEPS) as r:
                for j in range(4):
                    step(r * 4 + j, j)
            for j in range(4):
                step(STEPS * 4 + j, j, last=(j == 3))
            dve.wait_ge(sem("d_xbo"), 1)
            for c in range(NC):
                dve.wait_ge(sem("d_out"), c + 1)
                dve.tensor_tensor(x_tok[:, 4 * c:4 * c + 4, :], bank[c].rearrange("p (t d) -> p t d", d=D),
                                  x_tok[:, 4 * c:4 * c + 4, :], ALU.add).then_inc(sem("x_done"), 1)

        re_ = Room()
        e_r, e_k, e_e = (re_.take(RH * T) for _ in range(3))
        e_vT, e_sg = re_.take(T), re_.take(T)
        flat = ring[:, :, :].rearrange("p a b -> p (a b)")
        e_delta, e_xlA = flat[:, 0:T], flat[:, T:2 * T]
        e_xi = [flat[:, 2 * T + i * CH:2 * T + (i + 1) * CH] for i in range(2)]
        e_tan = [flat[0:64, 2 * T + (2 + i) * CH:2 * T + (3 + i) * CH] for i in range(2)]
        e_xlB = xn_tok[:, :, :].rearrange("p t d -> p (t d)")
        e_at = [flat[:, i * HT:(i + 1) * HT] for i in range(2)]
        e_vt = flat[:, T:2 * T]
        e_ruk = [e_xlB, flat[:, 2 * T:3 * T]]
        e_w = xnT[:, :]
        MIX = ("r", "w", "k", "v", "g")
        units = [(c, n) for c in range(NC) for n in range(5)]
        outs = []
        for q, (c, n) in enumerate(units):
            if MIX[n] == "r":
                outs += [(q, "r", h, "act") for h in range(RH)]
            elif MIX[n] == "k":
                outs += [(q, "k", h, "dve") for h in range(RH)]
            elif MIX[n] == "w":
                outs += [(q, "wA", 0, "act")] + [(q, "w", h, "act") for h in range(RH)]
            elif MIX[n] == "v":
                outs += [(q, "v", 0, "dve")]
            else:
                outs += [(q, "gA", 0, "act"), (q, "g", 0, "act")]
        out_count = []
        seen = {"act": 0, "dve": 0}
        for o in outs:
            seen[o[3]] += 1
            out_count.append((o[3], seen[o[3]]))
        tan_index = {}
        for q, kind, _, _ in outs:
            if kind in ("wA", "gA"):
                tan_index[q] = len(tan_index)

        def chunk(a, c):
            return a[:, c * CH:(c + 1) * CH]

        def head_chunk(a, h, c):
            return a[:, h * T + c * CH:h * T + (c + 1) * CH]

        def sides(a, n):
            return a.rearrange("p (b s n) -> p b s n", s=2, n=n)

        jobs = [(l, h) for l in range(len(LEVELS)) for h in range(RH)]

        def e_pool(pool):
            ln_pool(pool, 5)
            for l in range(len(LEVELS) - 1):
                n = LEVELS[l]
                for h in range(RH):
                    i = l * RH + h
                    k = sides(e_k[:, h * T:(h + 1) * T], n)
                    e = sides(e_e[:, h * T:(h + 1) * T], n)
                    pool.wait_ge(sem("e_a"), i + 1)
                    if l:
                        pool.wait_ge(sem("e_T"), i - RH + 1)
                        pool.wait_ge(sem("e_K"), i - RH + 1)
                    pool.tensor_tensor(k[:, :, 0, :], k[:, :, 0, :],
                                       e[:, :, 1, 0:1].broadcast_to([P, T // 2 // n, n]), ALU.mult)\
                        .then_inc(sem("e_K"), 1)
                    pool.wait_ge(sem("e_R"), i + 1)
                    pool.wait_ge(sem("e_K"), i + 1)
                    pool.tensor_tensor(e[:, :, 0, 0], e[:, :, 0, 0], e[:, :, 1, 0], ALU.mult)\
                        .then_inc(sem("e_T"), 1)
            ln_pool(pool, 6)

        def e_pe(pe):
            ln_pe(pe, 5, 3)
            o = [0]

            def product(lhsT, rhs, m=P):
                if o[0] >= 6:
                    e, n = out_count[o[0] - 6]
                    pe.wait_ge(sem("e_left_" + e), n)
                ins = pe.matmul(bank[2 + o[0] % 6][0:m, :], lhsT, rhs, start=True, stop=True)
                ins.then_inc(sem("e_out"), 1)
                o[0] += 1

            pe.wait_ge(sem("ln_T"), 4 * NC)
            for c in range(NC):
                pe.wait_ge(sem("e_xm"), c + 1)
                if c >= 1:
                    pe.wait_ge(sem("e_xl"), c)
                pe.matmul(bank[0], w("rW1T", 0, P), e_xi[c % 2], start=True, stop=True)
                pe.matmul(bank[1][0:32, :], w("rW1T", P, 160), e_xi[c % 2], start=True, stop=True)\
                  .then_inc(sem("e_xlp"), 1)
            pe.wait_ge(sem("e_xl"), NC)

            def mixing(q):
                c, n = units[q]
                if q >= 2:
                    pe.wait_ge(sem("e_m"), q - 1)
                if n < 4:
                    rows = slice(32 * n, 32 * n + 32)
                    pe.matmul(bank[q % 2], W[rows, WAT["rW2Ta"][0]:WAT["rW2Ta"][0] + P], chunk(e_xlA, c)[rows, :],
                              start=True, stop=True).then_inc(sem("e_x5"), 1)
                else:
                    pe.matmul(bank[q % 2], w("rW2Tb", rows=32), chunk(e_xlB, c)[0:32, :],
                              start=True, stop=True).then_inc(sem("e_x5"), 1)

            mixing(0)
            for q, (c, n) in enumerate(units):
                if q + 1 < len(units):
                    mixing(q + 1)
                pe.wait_ge(sem("e_xi"), q + 1)
                xi = e_xi[q % 2]
                kind = MIX[n]
                if kind in "rk":
                    for h in range(RH):
                        product(w("rrT" if kind == "r" else "rkT", h * P, (h + 1) * P), xi)
                elif kind == "v":
                    product(w("rvT"), xi)
                else:
                    product(w("rwAT" if kind == "w" else "rgAT"), xi, 64)
                if kind in "wg":
                    pe.wait_ge(sem("e_left_act"), out_count[o[0] - 1][1])
                    tan = e_tan[tan_index[q] % 2]
                    if kind == "w":
                        for h in range(RH):
                            product(w("rwBT", h * P, (h + 1) * P, rows=64), tan)
                    else:
                        product(w("rgBT", rows=64), tan)
            pe.wait_ge(sem("e_left_act"), seen["act"])
            pe.wait_ge(sem("e_left_dve"), seen["dve"])
            for h in range(RH):
                pe.wait_ge(sem("e_ruk"), h + 1)
                for c in range(NC):
                    ins = pe.matmul(bank[c][32 * h:32 * h + 32, :], const("ones", 0, 32), chunk(e_ruk[h % 2], c),
                                    start=True, stop=True)
                ins.then_inc(sem("e_diag"), 1)
            for tt in range(NT):
                ins = pe.transpose(banks(4, 4)[:, tt * P:(tt + 1) * P], e_vT[:, tt * P:(tt + 1) * P], ident)
            ins.then_inc(sem("e_vtp"), 1)
            pe.wait_ge(sem("zeros"), 1)
            pe.wait_ge(sem("e_vt"), 1)
            for c in range(NC):
                pe.matmul(bank[4 + c], zeros[:, 0:P], zeros[:, :], start=True, stop=False, skip_group_check=True)
            pe.wait_ge(sem("e_dg"), 1)

            def decayed(m):
                l, h = jobs[m]
                if m >= 2:
                    pe.wait_ge(sem("e_at"), m - 1)
                if l:
                    pe.wait_ge(sem("e_K"), m - RH + 1)
                    pe.wait_ge(sem("e_R"), m - RH + 1)
                for g in range(NT):
                    tokens = slice(h * T + g * P, h * T + (g + 1) * P)
                    ins = pe.matmul(banks(2 * (m % 2), 2)[:, g * 64:(g + 1) * 64], e_k[:, tokens],
                                    sides(e_r[:, tokens], LEVELS[l])[:, :, 1, :], start=True, stop=True)
                ins.then_inc(sem("e_a"), 1)

            def outputs(m):
                l, h = jobs[m]
                pe.wait_ge(sem("e_at"), m + 1)
                for g in range(NT):
                    out = sides(banks(4, 4)[32 * h:32 * h + 32, g * P:(g + 1) * P], LEVELS[l])[:, :, 1, :]
                    ins = pe.matmul(out, e_vt[:, g * P + 32 * h:g * P + 32 * h + 32],
                                    e_at[m % 2][:, g * 64:(g + 1) * 64],
                                    start=False, stop=(l == len(LEVELS) - 1), skip_group_check=True)
                ins.then_inc(sem("e_o"), 1)

            for m in range(len(jobs)):
                decayed(m)
                if m >= 1:
                    outputs(m - 1)
            outputs(len(jobs) - 1)
            for c in range(NC):
                pe.wait_ge(sem("e_oT"), c + 1)
                for t in range(4):
                    tt = 4 * c + t
                    ins = pe.transpose(bank[c][:, t * P:(t + 1) * P], e_w[:, tt * P:(tt + 1) * P], ident)
                ins.then_inc(sem("e_ot"), 1)
            pe.wait_ge(sem("e_oT"), NC)
            ln_pe(pe, 6, 4)
            for c in range(NC):
                pe.wait_ge(sem("e_gated"), c + 1)
                for t in range(4):
                    tt = 4 * c + t
                    ins = pe.matmul(bank[c][:, t * P:(t + 1) * P], e_w[:, tt * P:(tt + 1) * P], w("roT"),
                                    start=True, stop=True)
                ins.then_inc(sem("e_proj"), 1)

        def e_act(act):
            ln_act(act, 3)
            for c in range(NC):
                act.wait_ge(sem("e_xlp"), c + 1)
                act.activation(chunk(e_xlA, c), bank[0], ACT.Tanh)
                act.activation(chunk(e_xlB, c)[0:32, :], bank[1][0:32, :], ACT.Tanh).then_inc(sem("e_xl"), 1)
            for o, (q, kind, h, e) in enumerate(outs):
                if e != "act":
                    continue
                c = units[q][0]
                src = bank[2 + o % 6]
                act.wait_ge(sem("e_out"), o + 1)
                if kind == "r":
                    act.activation(head_chunk(e_r, h, c), src, ACT.Copy).then_inc(sem("e_left_act"), 1)
                elif kind in ("wA", "gA"):
                    act.activation(e_tan[tan_index[q] % 2], src[0:64, :], ACT.Tanh).then_inc(sem("e_left_act"), 1)
                elif kind == "w":
                    act.activation(head_chunk(e_e, h, c), src, ACT.Exp, bias=vec("wb", h))\
                       .then_inc(sem("e_left_act"), 1)
                else:
                    act.activation(chunk(e_sg, c), src, ACT.Identity, bias=vec("gb")).then_inc(sem("e_left_act"), 1)
            act.wait_ge(sem("e_left_act"), seen["act"])
            for h in range(RH):
                act.activation(e_e[:, h * T:(h + 1) * T], e_e[:, h * T:(h + 1) * T], ACT.Exp, scale=-1.0)\
                   .then_inc(sem("e_decay"), 1)
            act.activation(e_sg, e_sg, ACT.Silu).then_inc(sem("e_sg"), 1)
            act.wait_ge(sem("e_vtp"), 1)
            act.activation(e_vt, banks(4, 4), ACT.Copy).then_inc(sem("e_vt"), 1)
            for c in range(NC):
                act.wait_ge(sem("ln_tr"), 4 * NC + c + 1)
                act.activation(chunk(e_w, c), bank[6 + c % 2], ACT.Identity, scale=vec("gnw"), bias=vec("gnb"))\
                   .then_inc(sem("ln_T"), 1)

        def e_dve(dve):
            dve.memset(zeros[:, :], 0.0).then_inc(sem("zeros"), 1)
            ln_dve(dve, 5, x_tok, lambda c: dve.wait_ge(sem("x_done"), 2 * NC + c + 1))
            dve.wait_ge(sem("ln_T"), 4 * NC)
            xs_, ds_ = steps(xnT[:, :]), steps(e_delta)
            dve.tensor_tensor(ds_[:, :, 1:S], xs_[:, :, 0:S - 1], xs_[:, :, 1:S], ALU.subtract)
            link(dve, "dve", dve.tensor_scalar(ds_[:, :, 0], xs_[:, :, 0], -1.0, None, ALU.mult))
            for c in range(NC):
                if c >= 2:
                    dve.wait_ge(sem("e_xlp"), c - 1)
                dve.scalar_tensor_tensor(out=e_xi[c % 2], in0=chunk(e_delta, c), scalar=vec("mu"),
                                         in1=chunk(xnT, c), op0=ALU.mult, op1=ALU.add).then_inc(sem("e_xm"), 1)
            dve.wait_ge(sem("e_xlp"), NC)
            last_out = {q: o for o, (q, kind, _, _) in enumerate(outs) if kind not in ("w", "g")}

            def evacuate(q):
                for o, (q2, kind, h, e) in enumerate(outs):
                    if q2 != q or e != "dve":
                        continue
                    c = units[q][0]
                    dve.wait_ge(sem("e_out"), o + 1)
                    dst = head_chunk(e_k, h, c) if kind == "k" else chunk(e_vT, c)
                    dve.tensor_copy(dst, bank[2 + o % 6]).then_inc(sem("e_left_dve"), 1)

            for q, (c, n) in enumerate(units):
                dve.wait_ge(sem("e_x5"), q + 1)
                if q >= 2:
                    dve.wait_ge(sem("e_out"), last_out[q - 2] + 1)
                dve.scalar_tensor_tensor(out=e_xi[q % 2], in0=bank[q % 2], scalar=vec("xbias", n),
                                         in1=chunk(e_delta, c), op0=ALU.add, op1=ALU.mult).then_inc(sem("e_m"), 1)
                dve.wait_ge(sem("e_m"), q + 1)
                dve.tensor_tensor(e_xi[q % 2], e_xi[q % 2], chunk(xnT, c), ALU.add).then_inc(sem("e_xi"), 1)
                if q >= 1:
                    evacuate(q - 1)
            evacuate(len(units) - 1)
            dve.wait_ge(sem("e_left_dve"), seen["dve"])
            dve.wait_ge(sem("e_left_act"), seen["act"])
            dve.wait_ge(sem("e_out"), len(outs))
            for h in range(RH):
                if h >= 2:
                    dve.wait_ge(sem("e_diag"), h - 1)
                dve.scalar_tensor_tensor(out=e_ruk[h % 2], in0=e_r[:, h * T:(h + 1) * T], scalar=vec("bonus", h),
                                         in1=e_k[:, h * T:(h + 1) * T], op0=ALU.mult, op1=ALU.mult)\
                   .then_inc(sem("e_ruk"), 1)
            dve.wait_ge(sem("e_diag"), RH)
            dve.tensor_tensor(e_w, banks(0, 4), e_vT, ALU.mult).then_inc(sem("e_dg"), 1)
            dve.wait_ge(sem("e_decay"), RH)
            for m, (l, h) in enumerate(jobs):
                i, n = m, LEVELS[l]
                dve.wait_ge(sem("e_a"), i + 1)
                if i >= 2:
                    dve.wait_ge(sem("e_o"), i - 1)
                mask = const("levels", l * 64, (l + 1) * 64).unsqueeze(1).broadcast_to([P, NT, 64])
                dve.tensor_tensor(e_at[i % 2].rearrange("p (g t) -> p g t", g=NT),
                                  banks(2 * (m % 2), 2).rearrange("p (g t) -> p g t", g=NT), mask, ALU.mult)\
                   .then_inc(sem("e_at"), 1)
                if l < len(LEVELS) - 1:
                    r = sides(e_r[:, h * T:(h + 1) * T], n)
                    e = sides(e_e[:, h * T:(h + 1) * T], n)
                    if l:
                        dve.wait_ge(sem("e_T"), i - RH + 1)
                        dve.wait_ge(sem("e_R"), i - RH + 1)
                    dve.tensor_tensor(r[:, :, 1, :], r[:, :, 1, :],
                                      e[:, :, 0, 0:1].broadcast_to([P, T // 2 // n, n]), ALU.mult)\
                       .then_inc(sem("e_R"), 1)
            dve.wait_ge(sem("e_o"), len(LEVELS) * RH)
            for c in range(NC):
                dve.tensor_tensor(chunk(e_w, c), bank[4 + c], chunk(e_w, c), ALU.add).then_inc(sem("e_oT"), 1)
            ln_dve(dve, 6, banks(0, 4).rearrange("p (t d) -> p t d", d=D), lambda c: dve.wait_ge(sem("e_ot"), c + 1))
            dve.wait_ge(sem("e_sg"), 1)
            for c in range(NC):
                dve.wait_ge(sem("ln_T"), 4 * NC + c + 1)
                dve.tensor_tensor(chunk(e_w, c), chunk(e_w, c), chunk(e_sg, c), ALU.mult).then_inc(sem("e_gated"), 1)
            for c in range(NC):
                dve.wait_ge(sem("e_proj"), c + 1)
                dve.tensor_tensor(x_tok[:, 4 * c:4 * c + 4, :], bank[c].rearrange("p (t d) -> p t d", d=D),
                                  x_tok[:, 4 * c:4 * c + 4, :], ALU.add).then_inc(sem("x_done"), 1)

        rf = Room()
        f_ind = rf.take(NT * NE).rearrange("p (t e) -> p t e", e=NE)
        f_lg = rf.take(NT * NE).rearrange("p (t e) -> p t e", e=NE)
        f_ex = rf.take(NT * NE).rearrange("p (t e) -> p t e", e=NE)
        f_mx, f_se, f_mp, f_top = (rf.take(NT) for _ in range(4))
        f_indT = rf.take(T, BF16)
        f_sel = rf.take((NE + 1) * P, BF16)
        f_xe = [rf.take(CH) for _ in range(2)]
        f_sa = [rf.take(CH) for _ in range(4)]
        f_h = [rf.take(CH) for _ in range(4)]
        JOBS = 5
        TURNS = NE // 2

        def over_experts(a):
            return a.unsqueeze(2).broadcast_to([P, NT, NE])

        def f_sp(sp):
            sp.wait_ge(sem("e_o"), len(LEVELS) * RH)
            for s in range(2):
                sp.dma_start(ring[:, s, :], we_d[s, :, :]).then_inc(sem(f"f_w{s}"), 16)
            with sp.Fori(0, TURNS - 1) as r:
                for s in range(2):
                    sp.wait_ge(sem("f_y"), r * 8 + 4 * s + 4)
                    sp.dma_start(ring[:, s, :], we_d[bass.ds(r * 2 + 2 + s, 1), :, :]
                                 .rearrange("e p n -> p (e n)")).then_inc(sem(f"f_w{s}"), 16)

        def f_pool(pool):
            ln_pool(pool, 7)

        def f_pe(pe):
            ln_pe(pe, 7, 5)
            for c in range(NC):
                pe.wait_ge(sem("ln_T"), 5 * NC + c + 1)
                for t in range(4):
                    tt = 4 * c + t
                    ins = pe.matmul(bank[0][:, tt * NE:(tt + 1) * NE], xnT[:, tt * P:(tt + 1) * P], w("router"),
                                    start=True, stop=True)
            ins.then_inc(sem("f_logits"), 1)
            for c in range(NC):
                pe.matmul(bank[4 + c], zeros[:, 0:P], zeros[:, :], start=True, stop=False, skip_group_check=True)
            pe.wait_ge(sem("f_ind"), 1)
            for tt in range(NT):
                ins = pe.transpose(banks(0, 4)[0:NE, tt * P:(tt + 1) * P], f_ind[:, tt, :], ident)
            ins.then_inc(sem("f_indp"), 1)
            pe.wait_ge(sem("f_indT"), 1)

            def token_mask(e, c, pair):
                pe.matmul(bank[2 * pair], f_sel[:, bass.ds(e * P, P)], chunk(f_indT, c), start=True, stop=True)\
                  .then_inc(sem("f_bc"), 1)

            def hidden(u, v, c, slot, j, pair):
                m = u * JOBS + 1 + j
                pe.wait_ge(sem("f_left"), m)
                weights = ring[:, slot, :]
                pe.matmul(bank[2 * pair], weights[:, j * P:(j + 1) * P], f_xe[v % 2], start=True, stop=True)\
                  .then_inc(sem("f_A"), 1)
                pe.matmul(bank[2 * pair + 1], weights[:, HID + j * P:HID + (j + 1) * P], f_xe[v % 2],
                          start=True, stop=True).then_inc(sem("f_G"), 1)

            def down(u, c, slot, j, last=False):
                pe.wait_ge(sem("f_left"), u * JOBS + 3 + j)
                for t in range(4):
                    ins = pe.matmul(bank[4 + c][:, t * P:(t + 1) * P], f_h[j][:, t * P:(t + 1) * P],
                                    ring[:, slot, 2 * HID + j * P:2 * HID + (j + 1) * P],
                                    start=False, stop=(j == 3), skip_group_check=True)
                if j == 3:
                    ins.then_inc(sem("f_y"), 1)

            token_mask(0, 0, 0)
            with pe.Fori(0, TURNS) as r:
                for v in range(8):
                    slot, c = v // 4, v % 4
                    u = r * 8 + v
                    pair = lambda j: (v * JOBS + 1 + j) % 2
                    if c == 0:
                        pe.wait_ge(sem(f"f_w{slot}"), r * 16 + 16)
                    pe.wait_ge(sem("f_left"), u * JOBS + 2)
                    hidden(u, v, c, slot, 0, pair(0))
                    for j in range(1, 4):
                        hidden(u, v, c, slot, j, pair(j))
                        down(u, c, slot, j - 1)
                    pe.wait_ge(sem("f_left"), u * JOBS + 5)
                    token_mask(r * 2 + (v + 1) // 4, (c + 1) % 4, pair(4))
                    down(u, c, slot, 3)

        def f_act(act):
            ln_act(act, 5)
            act.wait_ge(sem("f_rel"), 1)
            act.activation(f_ex, f_lg, ACT.Exp).then_inc(sem("f_ex"), 1)
            with act.Fori(0, TURNS * 4) as r:
                for v in range(2):
                    for j in range(4):
                        act.wait_ge(sem("f_A"), r * 8 + 4 * v + j + 1)
                        act.activation(f_sa[j], bank[2 * ((v * JOBS + 1 + j) % 2)], ACT.Silu)\
                           .then_inc(sem("f_sa"), 1)

        def f_dve(dve):
            dve.tensor_copy(f_sel, const("expert")).then_inc(sem("f_sel"), 1)
            link(dve, "dve", dve.memset(f_indT, 0.0))
            ln_dve(dve, 7, x_tok, lambda c: dve.wait_ge(sem("x_done"), 3 * NC + c + 1))
            dve.wait_ge(sem("f_logits"), 1)
            logits = bank[0][:, 0:NT * NE].rearrange("p (t e) -> p t e", e=NE)
            link(dve, "dve", dve.tensor_tensor(f_lg, logits, row("rb").unsqueeze(1).broadcast_to([P, NT, NE]), ALU.add))
            link(dve, "dve", dve.tensor_reduce(f_mx, f_lg, AX.X, ALU.max))
            dve.tensor_tensor(f_lg, f_lg, over_experts(f_mx), ALU.subtract).then_inc(sem("f_rel"), 1)
            dve.wait_ge(sem("f_ex"), 1)
            dve.tensor_reduce(f_se, f_ex, AX.X, ALU.add)
            link(dve, "dve", dve.tensor_reduce(f_top, f_ex, AX.X, ALU.max))
            link(dve, "dve", dve.reciprocal(f_se, f_se))
            link(dve, "dve", dve.tensor_tensor(f_mp, f_top, f_se, ALU.mult))
            link(dve, "dve", dve.tensor_tensor(f_lg, f_ex, over_experts(f_top), ALU.is_equal))
            link(dve, "dve", dve.tensor_tensor(f_lg, f_lg, const("evals").unsqueeze(1).broadcast_to([P, NT, NE]),
                                               ALU.mult))
            link(dve, "dve", dve.tensor_reduce(f_mx, f_lg, AX.X, ALU.max))
            dve.tensor_tensor(f_ind, f_lg, over_experts(f_mx), ALU.is_equal).then_inc(sem("f_ind"), 1)
            dve.wait_ge(sem("f_indp"), 1)
            dve.tensor_copy(f_indT[0:NE, :], banks(0, 4)[0:NE, :]).then_inc(sem("f_indT"), 1)

            def tokens(count, c, v, pair):
                dve.wait_ge(sem("f_bc"), count)
                dve.tensor_tensor(f_xe[v % 2], bank[2 * pair], chunk(xnT, c), ALU.mult).then_inc(sem("f_left"), 1)

            dve.nop().then_inc(sem("f_left"), 1)
            tokens(1, 0, 0, 0)
            with dve.Fori(0, TURNS) as r:
                for v in range(8):
                    u = r * 8 + v
                    for j in range(4):
                        dve.wait_ge(sem("f_G"), u * 4 + j + 1)
                        dve.wait_ge(sem("f_sa"), u * 4 + j + 1)
                        dve.tensor_tensor(f_h[j], bank[2 * ((v * JOBS + 1 + j) % 2) + 1], f_sa[j], ALU.mult)\
                           .then_inc(sem("f_left"), 1)
                    tokens(u + 2, (v + 1) % 4, v + 1, (v * JOBS + 5) % 2)
            dve.wait_ge(sem("f_y"), TURNS * 8)
            for c in range(NC):
                for t in range(4):
                    tt = 4 * c + t
                    ins = dve.scalar_tensor_tensor(out=x_tok[:, tt, :], in0=bank[4 + c][:, t * P:(t + 1) * P],
                                                   scalar=f_mp[:, tt:tt + 1], in1=x_tok[:, tt, :],
                                                   op0=ALU.mult, op1=ALU.add)
                ins.then_inc(sem("x_done"), 1)

        stages = "ABCDEF"[:"ABCDEF".index(stop) + 1]
        programs = {k: v for k, v in locals().items()}

        def run(eng, name):
            for s in stages:
                f = programs.get(f"{s.lower()}_{name}")
                if f is not None:
                    f(eng)

        block = ctx.enter_context(nc.Block())

        @block.sync
        def _(sp):
            sp.dma_start(x_tok[:, :, :], x_d.rearrange("(t p) d -> p t d", p=P)).then_inc(sem("x_load"), 16)
            sp.dma_start(C[:, :], c_d).then_inc(sem("c_load"), 16)
            sp.dma_start(V[:, :], v_d).then_inc(sem("w_load"), 16)
            sp.dma_start(R[:, :], r_d.broadcast_to([P, RN])).then_inc(sem("row_load"), 16)
            sp.dma_start(W[:, 0:512], w_d[:, 0:512]).then_inc(sem("w_load"), 16)
            sp.dma_start(W[:, 512:WN], w_d[:, 512:WN]).then_inc(sem("w_load"), 16)
            run(sp, "sp")
            sp.wait_ge(sem("a_x"), NT + 1)
            sp.wait_ge(sem("x_done"), NC * (len(stages) - 1))
            sp.dma_start(out_d.rearrange("(t p) d -> p t d", p=P), x_tok[:, :, :]).then_inc(sem("stored"), 16)
            sp.wait_ge(sem("stored"), 16)

        @block.tensor
        def _(pe):
            pe.wait_ge(sem("c_load"), 16)
            pe.wait_ge(sem("w_load"), 48)
            run(pe, "pe")

        @block.scalar
        def _(act):
            act.wait_ge(sem("w_load"), 48)
            run(act, "act")

        @block.vector
        def _(dve):
            dve.memset(neg_half[:, :], -0.5).then_inc(sem("half"), 1)
            run(dve, "dve")

        @block.gpsimd
        def _(pool):
            pool.wait_ge(sem("half"), 1)
            run(pool, "pool")


def packed(cols, rows, parts):
    at, n = columns(cols)
    out = np.zeros((rows, n), np.float32)
    for name, a in parts.items():
        lo, k = at[name]
        out[:a.shape[0], lo:lo + k] = a
    assert set(parts) == {c for c, _ in cols}
    return out


def arranged(i):
    g = {k: np.asarray(v) for k, v in i.items()}
    col = lambda a, n=1: a.reshape(n, P).T
    W = packed(WCOLS, P, {
        "wqT": g["L0_xattn_Wq"].T, "wk": g["L0_xattn_Wk"], "wvT": g["L0_xattn_Wv"].T, "woT": g["L0_xattn_Wo"].T,
        "winT": g["L0_attn_w_in"].T, "wdtT": g["L0_attn_w_dt"].T, "wBT": g["L0_attn_w_B"].T,
        "wCT": g["L0_attn_w_C"].T, "woutT": g["L0_attn_w_out"].T,
        "w1T": g["L0_ffn_w1"].T, "w2T": g["L0_ffn_w2"].T.reshape(4, P, D).transpose(1, 0, 2).reshape(P, 512),
        "xq": g["L1_xattn_w_q"], "xk": g["L1_xattn_w_k"], "xv": g["L1_xattn_w_v"], "xo": g["L1_xattn_w_o"],
        "rW1T": g["L1_attn_xp_W1"].T, "rW2Ta": g["L1_attn_xp_W2"].T[0:128], "rW2Tb": g["L1_attn_xp_W2"].T[128:160],
        "rrT": g["L1_attn_r_W"].T, "rwAT": g["L1_attn_w_A"].T, "rwBT": g["L1_attn_w_B"].T,
        "rkT": g["L1_attn_k_W"].T, "rvT": g["L1_attn_v_W"].T, "rgAT": g["L1_attn_g_A"].T,
        "rgBT": g["L1_attn_g_B"].T, "roT": g["L1_attn_o_W"].T, "router": g["L1_ffn_router_w"]})
    V = packed(VCOLS, P, {
        "bq": col(g["L0_xattn_bq"]), "bv": col(g["L0_xattn_bv"]), "bin": col(g["L0_attn_b_in"], 2),
        "bdt": col(g["L0_attn_b_dt"]), "alog": g["L0_attn_A_log"], "Dskip": col(g["L0_attn_D"]),
        "convw": g["L0_ffn_conv_w"].reshape(4, P, 3).transpose(1, 0, 2).reshape(P, 12),
        "convb": col(g["L0_ffn_conv_b"], 4),
        "xbq": col(g["L1_xattn_b_q"]), "xbk": col(g["L1_xattn_b_k"]), "xbv": col(g["L1_xattn_b_v"]),
        "mu": col(g["L1_attn_xp_mu"]), "xbias": g["L1_attn_x_bias"].T, "wb": col(g["L1_attn_w_b"], 4),
        "gb": col(g["L1_attn_g_b"]), "bonus": g["L1_attn_bonus"].T, "gnw": col(g["L1_attn_gn_w"]),
        "gnb": col(g["L1_attn_gn_b"])})
    R = packed(RCOLS, 1, {n: g[k].reshape(1, -1) for n, k in (
        ("bo", "L0_xattn_bo"), ("bout", "L0_attn_b_out"), ("gamma", "L0_attn_gamma"), ("beta", "L0_attn_beta"),
        ("xbo", "L1_xattn_b_o"), ("bB", "L0_attn_b_B"), ("bC", "L0_attn_b_C"), ("rb", "L1_ffn_router_b"))})
    ctxn = np.zeros((B, 3 * KW, D), np.float32)
    ctxn[:, 0:K2] = g["ctx_1024"]
    ctxT = ctxn.reshape(NT, 4, K2P, D).transpose(0, 3, 1, 2).reshape(NT, D, 4 * K2P)
    ctxn = ctxn.reshape(NT, 4, 3, KW, D).transpose(0, 3, 1, 2, 4).reshape(NT, KW, 4 * 3 * D)
    return {
        "x": g["x"].reshape(T, D), "ctxn": ctxn, "ctxT": ctxT,
        "mask": g["mask_Bx1xSxS2_bk1"].reshape(B, S, K2),
        "w": W, "v": V, "r": R, "c": shape_constants(),
        "we": np.concatenate([g["L1_ffn_w1"], g["L1_ffn_w2"].reshape(NE, 4, P, D).transpose(0, 2, 1, 3)
                              .reshape(NE, P, HID)], 2)}


def kernel(**inputs):
    import concourse.bacc as bacc
    from concourse.bass_utils import run_bass_kernel_spmd

    nc = bacc.Bacc("TRN2", target_bir_lowering=False, num_devices=1)
    arrays, args = {}, []
    for name, a in arranged(inputs).items():
        a = np.ascontiguousarray(a)
        arrays[f"in_{name}"] = a
        args.append(nc.dram_tensor(f"in_{name}", a.shape, mybir.dt.from_np(a.dtype), kind="ExternalInput").ap())
    args.append(nc.dram_tensor("out", (T, D), F32, kind="ExternalOutput").ap())
    build_program(nc, *args)
    r = run_bass_kernel_spmd(nc, [arrays], core_ids=[0])
    return r.results[0]["out"].reshape(B, S, D)
```

```python
from contextlib import ExitStack

import numpy as np

import concourse.bass as bass
from concourse import mybir

ALU = mybir.AluOpType
ACT = mybir.ActivationFunctionType
AX = mybir.AxisListType
F32 = mybir.dt.float32
BF16 = mybir.dt.bfloat16
U8 = mybir.dt.uint8

P = 128
B, S, D = 64, 32, 128
T = B * S
NT = T // P
CH = 512
NC = T // CH
TPC = CH // P
K2 = 257
K2P = 258
KW = 86
NSTATE = 16
HID = 512
NH, DK = 16, 8
RH = 4
NE = 8
EPS = 1e-5
MAGIC = 1.5 * 2.0 ** 23
NEG = -(2.0 ** 100)

WCOLS = [("wq", 128), ("wk", 128), ("wv", 128), ("woT", 128),
         ("winT", 256), ("wdtT", 128), ("wBT", 16), ("wCT", 16), ("woutT", 128),
         ("w1T", 512), ("w2T", 512),
         ("xq", 128), ("xk", 128), ("xv", 128), ("xo", 128),
         ("rW1T", 160), ("rW2Ta", 128), ("rW2Tb", 128), ("rrT", 512), ("rwAT", 64), ("rwBT", 512),
         ("rkT", 512), ("rvT", 128), ("rgAT", 64), ("rgBT", 128), ("roT", 128), ("router", 8)]
VCOLS = [("bq", 1), ("bv", 1), ("bin", 2), ("bdt", 1), ("alog", 16), ("Dskip", 1),
         ("convw", 12), ("convb", 4),
         ("xbq", 1), ("xbk", 1), ("xbv", 1),
         ("mu", 1), ("xbias", 5), ("wb", 4), ("gb", 1), ("bonus", 4), ("gnw", 1), ("gnb", 1)]
RCOLS = [("bo", 128), ("bout", 128), ("gamma", 128), ("beta", 128), ("xbo", 128),
         ("bB", 16), ("bC", 16), ("rb", 8)]
CCOLS = [("ident", 128), ("headsel", 128), ("heads", NH * 32), ("negsel", 128), ("levels", 5 * 64), ("expert", 9 * 128), ("evals", 8), ("ones", 32)]


def columns(cols):
    at, out = 0, {}
    for name, n in cols:
        out[name] = (at, n)
        at += n
    return out, at


WAT, WN = columns(WCOLS)
VAT, VN = columns(VCOLS)
RAT, RN = columns(RCOLS)
CAT, CN = columns(CCOLS)
LEVELS = [1, 2, 4, 8, 16]


def shape_constants():
    c = np.zeros((P, CN), np.float32)
    at = lambda n: slice(CAT[n][0], CAT[n][0] + CAT[n][1])
    p = np.arange(P)
    c[:, at("ident")] = np.eye(P)
    c[:, at("headsel")] = (p[:, None] // DK % 4 == p[None, :] // S)
    c[:, at("heads")] = (p[:, None] // DK == np.arange(NH * S)[None, :] // S)
    c[:, at("negsel")] = np.where(p[:, None] % S == p[None, :] % S, NEG / 4, 0.0)
    c[:, at("levels")] = np.concatenate([p[:, None] // n == 2 * (np.arange(64)[None, :] // n) for n in LEVELS], 1)
    e = np.zeros((P, NE + 1, P), np.float32)
    for i in range(NE):
        e[i, i, :] = 1.0
    c[:, at("expert")] = e.reshape(P, -1)
    c[:, at("ones")] = 1.0
    c[:, at("evals")] = NE - np.arange(NE)
    return c


def build_program(nc, x_d, ctxn_d, ctxT_d, mask_d, w_d, v_d, r_d, c_d, we_d, out_d, stop="F"):
    with ExitStack() as ctx:
        def sb(name, shape, dt=F32):
            return ctx.enter_context(nc.sbuf_tensor(name, shape, dt))

        sems = {}

        def sem(name):
            if name not in sems:
                sems[name] = ctx.enter_context(nc.semaphore(name))
            return sems[name]

        psum = ctx.enter_context(nc.psum_tensor("psum", [P, 8 * CH], F32))
        bank = [psum[:, i * CH:(i + 1) * CH] for i in range(8)]

        def banks(i, n):
            return psum[:, i * CH:(i + n) * CH]

        W = sb("weights", [P, WN])
        V = sb("vectors", [P, VN])
        R = sb("rows", [P, RN])
        C = sb("constants", [P, CN])
        x_tok = sb("x_tok", [P, NT, D])
        xn_tok = sb("xn_tok", [P, NT, D])
        xnT = sb("xnT", [P, T])
        ln_st = sb("ln_st", [P, NT, 6])
        ln_mv = sb("ln_mv", [P, NT, 2])
        ln_var = sb("ln_var", [P, NT])
        ln_rstd = sb("ln_rstd", [P, NT])
        zeros = sb("zeros", [P, CH], BF16)
        neg_half = sb("neg_half", [P, TPC])
        AR = 28800
        arena = sb("arena", [P, AR])
        ring = sb("ring", [P, 4, 4 * 3 * D])
        RING_AT = AR - 4 * 4 * K2P
        ctxT_ring = [arena[:, RING_AT + j * 4 * K2P:RING_AT + (j + 1) * 4 * K2P] for j in range(4)]

        def w(name, lo=0, hi=None, rows=P):
            a, n = WAT[name]
            return W[0:rows, a + lo:a + (n if hi is None else hi)]

        def vec(name, j=0):
            return V[:, VAT[name][0] + j:VAT[name][0] + j + 1]

        def row(name):
            return R[:, RAT[name][0]:RAT[name][0] + RAT[name][1]]

        def const(name, lo=0, hi=None):
            a, n = CAT[name]
            return C[:, a + lo:a + (n if hi is None else hi)]

        ident = const("ident")

        class Room:

            def __init__(self, at=0):
                self.at = at

            def take(self, n, dt=F32):
                words = n if dt == F32 else (n + 1) // 2
                a = arena[:, self.at:self.at + words]
                self.at += words
                assert self.at <= AR, self.at
                return a if dt == F32 else a.bitcast(dt)

        chain = {"dve": 0, "act": 0, "pool": 0}

        def link(eng, name, ins):
            chain[name] += 1
            ins.then_inc(sem(name + "_chain"), 1)
            eng.wait_ge(sem(name + "_chain"), chain[name])

        def ln_dve(dve, k, src, ready):
            for c in range(NC):
                ready(c)
                for t in range(4 * c, 4 * c + 4):
                    ins = dve.bn_stats(ln_st[:, t, :], src[:, t, :])
                link(dve, "dve", ins)
                for t in range(4 * c, 4 * c + 4):
                    ins = dve.bn_aggr(ln_mv[:, t, :], ln_st[:, t, :])
                link(dve, "dve", ins)
                dve.tensor_scalar(ln_var[:, 4 * c:4 * c + 4], ln_mv[:, 4 * c:4 * c + 4, 1], EPS, None,
                                  ALU.add).then_inc(sem("ln_var"), 1)
            for c in range(NC):
                dve.wait_ge(sem("ln_rstd"), NC * k + c + 1)
                for t in range(4 * c, 4 * c + 4):
                    ins = dve.tensor_scalar(xn_tok[:, t, :], src[:, t, :], ln_mv[:, t, 0:1],
                                            ln_rstd[:, t:t + 1], ALU.subtract, ALU.mult)
                ins.then_inc(sem("ln_xn"), 1)

        def ln_pool(pool, k):
            for c in range(NC):
                pool.wait_ge(sem("ln_var"), NC * k + c + 1)
                pool.tensor_tensor(ln_rstd[:, 4 * c:4 * c + 4], ln_var[:, 4 * c:4 * c + 4], neg_half[:, :],
                                   ALU.pow).then_inc(sem("ln_rstd"), 1)

        def ln_pe(pe, k, kt):
            for c in range(NC):
                pe.wait_ge(sem("ln_xn"), NC * k + c + 1)
                if c >= 2:
                    pe.wait_ge(sem("ln_T"), NC * kt + c - 1)
                for t in range(4):
                    ins = pe.transpose(bank[6 + c % 2][:, t * P:(t + 1) * P], xn_tok[:, 4 * c + t, :], ident)
                ins.then_inc(sem("ln_tr"), 1)

        def ln_act(act, kt):
            for c in range(NC):
                act.wait_ge(sem("ln_tr"), NC * kt + c + 1)
                act.activation(xnT[:, c * CH:(c + 1) * CH], bank[6 + c % 2][:, :], ACT.Copy)\
                   .then_inc(sem("ln_T"), 1)

        ra = Room()
        a_ctxn = [ring[:, j, :].rearrange("p (b k d) -> p b k d", b=4, k=3) for j in range(4)]
        a_ctxT = ctxT_ring
        a_wqk, a_wvo, a_bias = ra.take(P), ra.take(P), ra.take(P)
        a_qb = ra.take(1)
        a_qk = [ra.take(P) for _ in range(2)]
        a_nmax = [ra.take(1) for _ in range(2)]
        a_sum = [ra.take(1) for _ in range(2)]
        a_rs = [ra.take(1) for _ in range(2)]
        a_p = [ra.take(3 * KW) for _ in range(2)]
        a_pn = [ra.take(3 * KW) for _ in range(2)]
        a_pT = [ra.take(3 * P).rearrange("p (k n) -> p k n", k=3) for _ in range(2)]
        a_cx = [ra.take(P) for _ in range(2)]
        a_cxT = [ra.take(P) for _ in range(2)]
        A_SCALE = float(D) ** -0.5
        A_LAG = 4

        def a_steps(eng, step):
            def edge(ts):
                for t in ts:
                    step(t, t % 4, t // 4, lambda lag: 0 <= t - lag < NT)

            edge(range(A_LAG))
            with eng.Fori(1, NT // 4 - 1) as r:
                for j in range(4):
                    step(r * 4 + j, j, r, lambda lag: True)
            edge(range(NT - 4, NT + A_LAG))

        def a_load(sp, j, g):
            sp.dma_start(a_ctxT[j], ctxT_d[bass.ds(g, 1), :, :].rearrange("g p k -> p (g k)"))\
              .then_inc(sem(f"a_ctx{j}"), 16)
            sp.dma_start(a_ctxn[j][0:KW], ctxn_d[bass.ds(g, 1), :, :].rearrange("g p (b k d) -> p (g b) k d", b=4, k=3))\
              .then_inc(sem(f"a_ctx{j}"), 16)

        def a_sp(sp):
            with sp.Fori(0, NT // 4 - 1) as r:
                i = r * 4
                for j in range(4):
                    sp.wait_ge(sem("a_pv"), i + j + 1)
                    a_load(sp, j, i + 4 + j)

        def a_pe(pe):
            pe.wait_ge(sem("ident_load"), 16)
            ln_pe(pe, 0, 0)
            pe.wait_ge(sem("wa_load"), 32)
            pe.matmul(bank[0][:, 0:P], w("wq"), w("wk"), start=True, stop=True)
            pe.matmul(bank[0][:, P:P + 1], w("wk"), vec("bq"), start=True, stop=True).then_inc(sem("a_wqk_p"), 1)
            pe.matmul(bank[1][:, 0:P], w("wv"), w("woT"), start=True, stop=True)
            pe.matmul(bank[1][:, P:2 * P], vec("bv").broadcast_to([P, P]), w("woT"), start=True, stop=True)\
              .then_inc(sem("a_wvo_p"), 1)
            pe.wait_ge(sem("a_w"), 3)
            pe.wait_ge(sem("a_bias"), 1)
            pe.wait_ge(sem("ln_T"), NC)
            pe.matmul(bank[4][:, 0:P], a_wqk, xnT[:, 0:P], start=True, stop=True).then_inc(sem("a_q"), 1)

            def step(t, j, turn, has):
                if has(-1):
                    pe.wait_ge(sem("a_qk"), t + 1)
                    pe.matmul(bank[4][:, 0:P], a_wqk, xnT[:, bass.ds((t + 1) * P, P)], start=True, stop=True)\
                      .then_inc(sem("a_q"), 1)
                if has(0):
                    pe.wait_ge(sem(f"a_ctx{j}"), turn * 32 + 32)
                    pe.wait_ge(sem("a_qk"), t + 1)
                    if has(2):
                        pe.wait_ge(sem("a_exp"), t - 1)
                    for b in range(4):
                        ins = pe.matmul(bank[j % 2][32 * b:32 * b + 32, 0:K2], a_qk[j % 2][:, 32 * b:32 * b + 32],
                                        a_ctxT[j][:, b * K2P:b * K2P + K2], start=True, stop=True)
                    ins.then_inc(sem("a_s"), 1)
                if has(2):
                    pe.wait_ge(sem("a_pT"), t - 1)
                    if has(3):
                        pe.wait_ge(sem("a_cx"), t - 2)
                    for k in range(3):
                        for b in range(4):
                            ins = pe.matmul(bank[3][32 * b:32 * b + 32, 0:P], a_pT[j % 2][0:KW, k, 32 * b:32 * b + 32],
                                            a_ctxn[(j - 2) % 4][0:KW, b, k, :], start=(k == 0), stop=(k == 2))
                    ins.then_inc(sem("a_pv"), 1)
                if has(1):
                    pe.wait_ge(sem("a_pn"), t)
                    if has(2):
                        pe.wait_ge(sem("a_pT"), t - 1)
                    for k in range(3):
                        ins = pe.transpose(bank[2][0:KW, k * P:(k + 1) * P],
                                           a_pn[(j - 1) % 2][:, k * KW:(k + 1) * KW], ident)
                    ins.then_inc(sem("a_t"), 1)
                if has(3):
                    pe.wait_ge(sem("a_cx"), t - 2)
                    if has(4):
                        pe.wait_ge(sem("a_cxT"), t - 3)
                    pe.transpose(bank[5][:, 0:P], a_cx[(j - 3) % 2], ident).then_inc(sem("a_ct"), 1)
                if has(4):
                    pe.wait_ge(sem("a_cxT"), t - 3)
                    if has(5):
                        pe.wait_ge(sem("a_x"), t - 4)
                    pe.matmul(bank[6][:, 0:P], a_cxT[j % 2], a_wvo, start=True, stop=True).then_inc(sem("a_o"), 1)

            a_steps(pe, step)

        def a_act(act):
            ln_act(act, 0)
            act.wait_ge(sem("a_wqk_p"), 1)
            act.activation(a_wqk, bank[0][:, 0:P], ACT.Copy).then_inc(sem("a_w"), 1)
            act.activation(a_qb, bank[0][:, P:P + 1], ACT.Copy, scale=A_SCALE).then_inc(sem("a_w"), 1)
            act.wait_ge(sem("a_wvo_p"), 1)
            act.activation(a_wvo, bank[1][:, 0:P], ACT.Copy).then_inc(sem("a_w"), 1)

            def queries(t, j):
                act.wait_ge(sem("a_q"), t + 1)
                act.activation(a_qk[j % 2], bank[4][:, 0:P], ACT.Identity, bias=a_qb, scale=A_SCALE)\
                   .then_inc(sem("a_qk"), 1)

            act.wait_ge(sem("a_w"), 3)
            queries(0, 0)

            def step(t, j, turn, has):
                if has(-1):
                    queries(t + 1, j + 1)
                if has(0):
                    act.wait_ge(sem("a_max"), t + 1)
                    act.activation(a_p[j % 2][:, 0:K2], bank[j % 2][:, 0:K2], ACT.Exp, bias=a_nmax[j % 2],
                                   accum_out=a_sum[j % 2]).then_inc(sem("a_exp"), 1)
                if has(1):
                    act.wait_ge(sem("a_t"), t)
                    act.activation(a_pT[(j - 1) % 2][0:KW], bank[2][0:KW, 0:3 * P].rearrange("p (k n) -> p k n", k=3),
                                   ACT.Copy).then_inc(sem("a_pT"), 1)
                if has(3):
                    act.wait_ge(sem("a_ct"), t - 2)
                    act.activation(a_cxT[(j - 3) % 2], bank[5][:, 0:P], ACT.Copy).then_inc(sem("a_cxT"), 1)

            a_steps(act, step)

        def a_pool(pool):
            ln_pool(pool, 0)
            pool.wait_ge(sem("a_bias"), 1)
            for c in range(NC):
                tiles = slice(4 * c, 4 * c + 4)
                pool.wait_ge(sem("ln_xn"), c + 1)
                pool.tensor_tensor(x_tok[:, tiles, :], x_tok[:, tiles, :],
                                   a_bias.unsqueeze(1).broadcast_to([P, TPC, D]), ALU.add)\
                    .then_inc(sem("a_biased"), 1)

        def a_dve(dve):
            for u in (0, 1):
                dve.memset(a_pn[u][:, K2:3 * KW], 0.0)
            ln_dve(dve, 0, x_tok, lambda c: dve.wait_ge(sem(f"x_load{c}"), 16))
            dve.wait_ge(sem("row_load"), 16)
            dve.wait_ge(sem("a_w"), 3)
            dve.tensor_tensor(a_bias, bank[1][:, P:2 * P], row("bo"), ALU.add).then_inc(sem("a_bias"), 1)

            def step(t, j, turn, has):
                if has(0):
                    dve.wait_ge(sem("a_s"), t + 1)
                    dve.tensor_reduce(a_nmax[j % 2], bank[j % 2][:, 0:K2], AX.X, ALU.max, negate=True)\
                       .then_inc(sem("a_max"), 1)
                if has(2):
                    dve.wait_ge(sem("a_pv"), t - 1)
                    dve.tensor_copy(a_cx[j % 2], bank[3][:, 0:P]).then_inc(sem("a_cx"), 1)
                if has(0):
                    dve.wait_ge(sem("a_exp"), t + 1)
                    dve.reciprocal(a_rs[j % 2], a_sum[j % 2]).then_inc(sem("a_rs"), 1)
                    dve.wait_ge(sem("a_rs"), t + 1)
                    dve.tensor_scalar(a_pn[j % 2][:, 0:K2], a_p[j % 2][:, 0:K2], a_rs[j % 2], None, ALU.mult)\
                       .then_inc(sem("a_pn"), 1)
                if has(4):
                    dve.wait_ge(sem("a_o"), t - 3)
                    xt = x_tok[:, bass.ds(t - 4, 1), :].rearrange("p a d -> p (a d)")
                    dve.tensor_tensor(xt, bank[6][:, 0:P], xt, ALU.add).then_inc(sem("a_x"), 1)

            dve.wait_ge(sem("a_biased"), NC)
            a_steps(dve, step)

        rb_ = Room()
        b_xs, b_z, b_dt, b_dtx, b_y = (rb_.take(T) for _ in range(5))
        b_t1, b_t2 = (rb_.take(T) for _ in range(2))
        b_a = [rb_.take(T) for _ in range(2)]
        HT = T // 2
        b_u = [rb_.take(HT) for _ in range(2)]
        b_h = [rb_.take(HT) for _ in range(2)]
        b_hc = [rb_.take(HT) for _ in range(4)]
        b_aneg = rb_.take(NSTATE)
        b_aexp = rb_.take(NSTATE)
        b_pre = b_t1.rearrange("p (t d) -> p t d", d=D)

        def steps(a):
            return a.rearrange("p (b s) -> p b s", s=S)

        def b_pool(pool):
            ln_pool(pool, 1)
            pool.wait_ge(sem("ln_xn"), 2 * NC)
            pool.wait_ge(sem("ln_T"), 2 * NC)
            pool.tensor_tensor(xn_tok[:, :, :], xn_tok[:, :, :],
                               row("bout").unsqueeze(1).broadcast_to([P, NT, D]), ALU.add)\
                .then_inc(sem("b_res"), 1)
            pool.tensor_tensor(x_tok[:, :, :], x_tok[:, :, :],
                               row("beta").unsqueeze(1).broadcast_to([P, NT, D]), ALU.add)\
                .then_inc(sem("b_res"), 1)
            pool.wait_ge(sem("b_skip"), 1)
            for q in range(2 * NSTATE):
                hf = q % 2
                y = b_y[:, hf * HT:(hf + 1) * HT]
                pool.wait_ge(sem("b_hc"), q + 1)
                if q >= 2:
                    pool.wait_ge(sem("b_yadd"), q - 1)
                pool.tensor_tensor(y, y, b_hc[q % 4], ALU.add).then_inc(sem("b_yadd"), 1)
            ln_pool(pool, 2)

        def b_pe(pe):
            ln_pe(pe, 1, 1)
            for c in range(NC):
                pe.wait_ge(sem("ln_T"), NC + c + 1)
                xc = xnT[:, c * CH:(c + 1) * CH]
                pe.matmul(bank[c], w("winT", 0, D), xc, start=True, stop=True).then_inc(sem("b_xsp"), 1)
                if c >= 2:
                    pe.wait_ge(sem("b_z"), c - 1)
                pe.matmul(bank[4 + c % 2], w("winT", D, 2 * D), xc, start=True, stop=True)\
                  .then_inc(sem("b_zp"), 1)
            for c in range(NC):
                pe.wait_ge(sem("b_xs"), c + 1)
                pe.matmul(bank[c], w("wdtT"), b_xs[:, c * CH:(c + 1) * CH], start=True, stop=True)\
                  .then_inc(sem("b_dtp"), 1)
            pe.wait_ge(sem("b_relu"), NC)
            pe.wait_ge(sem("b_abs"), NC)
            pe.wait_ge(sem("b_z"), NC)
            for q in range(2 * NSTATE):
                n, hf = q // 2, q % 2
                for which, name, used, done in ((0, "wBT", "b_u", "b_B"), (2, "wCT", "b_hc", "b_C")):
                    if q >= 2:
                        pe.wait_ge(sem(used), q - 1)
                    for c in range(2):
                        at = hf * HT + c * CH
                        ins = pe.matmul(bank[4 * hf + which + c], w(name, n, n + 1).broadcast_to([P, P]),
                                        b_xs[:, at:at + CH], start=True, stop=True)
                    ins.then_inc(sem(done), 1)
            for c in range(NC):
                if c < 2:
                    pe.wait_ge(sem("b_yz"), c + 1)
                for t in range(4):
                    tt = 4 * c + t
                    ins = pe.matmul(bank[c][:, t * P:(t + 1) * P], b_y[:, tt * P:(tt + 1) * P], w("woutT"),
                                    start=True, stop=True)
                ins.then_inc(sem("b_out"), 1)

        def b_act(act):
            ln_act(act, 1)
            for c in range(NC):
                act.wait_ge(sem("b_xsp"), c + 1)
                act.activation(b_xs[:, c * CH:(c + 1) * CH], bank[c], ACT.Identity, bias=vec("bin", 0))\
                   .then_inc(sem("b_xs"), 1)
                act.wait_ge(sem("b_zp"), c + 1)
                act.activation(b_z[:, c * CH:(c + 1) * CH], bank[4 + c % 2], ACT.Silu, bias=vec("bin", 1))\
                   .then_inc(sem("b_z"), 1)
            for c in range(NC):
                act.wait_ge(sem("b_relu"), c + 1)
                act.activation(b_t1[:, c * CH:(c + 1) * CH], bank[c], ACT.Abs, bias=vec("bdt"))\
                   .then_inc(sem("b_abs"), 1)
            act.activation(b_aexp, V[:, VAT["alog"][0]:VAT["alog"][0] + NSTATE], ACT.Exp)\
               .then_inc(sem("b_aexp"), 1)
            act.wait_ge(sem("b_abs"), NC)
            link(act, "act", act.activation(b_t2, b_t1, ACT.Exp, scale=-1.0))
            act.activation(b_t1, b_t2, ACT.Ln, bias=1.0).then_inc(sem("b_log1p"), 1)
            act.wait_ge(sem("b_dt"), 1)
            act.wait_ge(sem("b_azero"), 1)
            for n in range(NSTATE):
                if n >= 2:
                    act.wait_ge(sem("b_scan"), 2 * (n - 1))
                act.activation(steps(b_a[n % 2])[:, :, 1:S], steps(b_dt)[:, :, 1:S], ACT.Exp,
                               scale=b_aneg[:, n:n + 1]).then_inc(sem("b_a"), 1)

        def b_dve(dve):
            ln_dve(dve, 1, x_tok, lambda c: dve.wait_ge(sem("a_x"), TPC * (c + 1)))
            for j in range(2):
                ins = dve.memset(steps(b_a[j])[:, :, 0], 0.0)
            ins.then_inc(sem("b_azero"), 1)
            for c in range(NC):
                dve.wait_ge(sem("b_dtp"), c + 1)
                dve.tensor_scalar(b_dt[:, c * CH:(c + 1) * CH], bank[c], vec("bdt"), 0.0, ALU.add, ALU.max)\
                   .then_inc(sem("b_relu"), 1)
            dve.wait_ge(sem("b_aexp"), 1)
            link(dve, "dve", dve.tensor_scalar(b_aneg, b_aexp, -1.0, None, ALU.mult))
            dve.wait_ge(sem("b_log1p"), 1)
            link(dve, "dve", dve.tensor_tensor(b_dt, b_dt, b_t1, ALU.add))
            dve.tensor_tensor(b_dtx, b_dt, b_xs, ALU.mult).then_inc(sem("b_dt"), 1)
            dve.tensor_scalar(b_y, b_xs, vec("Dskip"), None, ALU.mult).then_inc(sem("b_skip"), 1)
            dve.wait_ge(sem("b_dt"), 1)
            dve.wait_ge(sem("row_load"), 16)
            bB, bC = row("bB"), row("bC")
            for n in range(NSTATE):
                for hf in (0, 1):
                    q = 2 * n + hf
                    half = slice(hf * HT, (hf + 1) * HT)
                    dve.wait_ge(sem("b_B"), q + 1)
                    if q >= 2:
                        dve.wait_ge(sem("b_scan"), q - 1)
                    dve.scalar_tensor_tensor(out=b_u[hf], in0=banks(4 * hf, 2), scalar=bB[:, n:n + 1],
                                             in1=b_dtx[:, half], op0=ALU.add, op1=ALU.mult)\
                       .then_inc(sem("b_u"), 1)
                for hf in (0, 1):
                    q = 2 * n + hf
                    half = slice(hf * HT, (hf + 1) * HT)
                    dve.wait_ge(sem("b_a"), n + 1)
                    dve.wait_ge(sem("b_u"), q + 1)
                    dve.tensor_tensor_scan(b_h[hf], b_a[n % 2][:, half], b_u[hf], 0.0, ALU.mult, ALU.add)\
                       .then_inc(sem("b_scan"), 1)
                for hf in (0, 1):
                    q = 2 * n + hf
                    dve.wait_ge(sem("b_C"), q + 1)
                    dve.wait_ge(sem("b_scan"), q + 1)
                    if q >= 4:
                        dve.wait_ge(sem("b_yadd"), q - 3)
                    dve.scalar_tensor_tensor(out=b_hc[q % 4], in0=banks(4 * hf + 2, 2), scalar=bC[:, n:n + 1],
                                             in1=b_h[hf], op0=ALU.add, op1=ALU.mult)\
                       .then_inc(sem("b_hc"), 1)
            for hf in (0, 1):
                dve.wait_ge(sem("b_yadd"), 2 * NSTATE - 1 + hf)
                y = b_y[:, hf * HT:(hf + 1) * HT]
                dve.tensor_tensor(y, y, b_z[:, hf * HT:(hf + 1) * HT], ALU.mult).then_inc(sem("b_yz"), 1)
            dve.wait_ge(sem("b_res"), 2)
            for c in range(NC):
                dve.wait_ge(sem("b_out"), c + 1)
                dve.tensor_tensor(b_pre[:, 4 * c:4 * c + 4, :], bank[c].rearrange("p (t d) -> p t d", d=D),
                                  xn_tok[:, 4 * c:4 * c + 4, :], ALU.add).then_inc(sem("b_pre"), 1)
            ln_dve(dve, 2, b_pre, lambda c: dve.wait_ge(sem("b_pre"), c + 1))
            for c in range(NC):
                tiles = slice(4 * c, 4 * c + 4)
                dve.wait_ge(sem("ln_xn"), 2 * NC + c + 1)
                dve.tensor_tensor(b_pre[:, tiles, :], xn_tok[:, tiles, :],
                                  row("gamma").unsqueeze(1).broadcast_to([P, TPC, D]), ALU.mult)\
                   .then_inc(sem("b_gam"), 1)
            for c in range(NC):
                tiles = slice(4 * c, 4 * c + 4)
                dve.wait_ge(sem("b_gam"), c + 1)
                dve.tensor_tensor(x_tok[:, tiles, :], x_tok[:, tiles, :], b_pre[:, tiles, :], ALU.add)\
                   .then_inc(sem("x_done"), 1)

        rc = Room()
        c_w1f, c_w2f = rc.take(HID), rc.take(HID)
        c_w1q, c_w2q = rc.take(HID, BF16), rc.take(HID, BF16)
        c_identb = rc.take(P, BF16)
        c_wsum, c_wmean, c_winv = rc.take(2), rc.take(2), rc.take(2)
        c_ones = rc.take(P)
        c_q = rc.take(T, BF16).rearrange("p (t d) -> p t d", d=D)
        c_qT = rc.take(T, BF16)
        c_m, c_s, c_dq = rc.take(2 * NT), rc.take(2 * NT), rc.take(2 * NT)
        c_R = rc.take(T)
        c_hp = [rc.take(B * (S + 2)).rearrange("p (b s) -> p b s", s=S + 2) for _ in range(2)]
        c_t = [rc.take(T) for _ in range(2)]
        c_hs = [rc.take(T) for _ in range(4)]
        c_qf = c_t[0].rearrange("p (t d) -> p t d", d=D)
        c_q2f = [rc.take(HID) for _ in range(4)]
        c_q2 = [rc.take(HID, BF16) for _ in range(4)]
        c_q2T = [rc.take(HID, BF16).rearrange("p (k n) -> p k n", k=4) for _ in range(4)]

        def quant_scales(dve, at, n, which):
            m, s, d = c_m[:, at:at + n], c_s[:, at:at + n], c_dq[:, at:at + n]
            link(dve, "dve", dve.tensor_scalar(m, m, 1e-5, None, ALU.max))
            link(dve, "dve", dve.reciprocal(s, m))
            dve.tensor_scalar(d, m, 1.0 / 127.0, c_wmean[:, which:which + 1], ALU.mult, ALU.mult)
            link(dve, "dve", dve.tensor_scalar(s, s, 127.0, None, ALU.mult))

        def c_pool(pool):
            ln_pool(pool, 3)

        def c_dve(dve):
            link(dve, "dve", dve.memset(c_ones, 1.0))
            for k, name in enumerate(("w1T", "w2T")):
                ins = dve.tensor_reduce(c_wsum[:, k:k + 1], w(name), AX.X, ALU.add, apply_absolute_value=True)
            ins.then_inc(sem("c_wsum"), 1)
            for j in range(2):
                dve.memset(c_hp[j][:, :, 0], 0.0)
                ins = dve.memset(c_hp[j][:, :, S + 1], 0.0)
            link(dve, "dve", ins)
            dve.tensor_copy(c_identb, ident).then_inc(sem("c_identb"), 1)
            dve.wait_ge(sem("c_wtot"), 1)
            link(dve, "dve", dve.tensor_scalar(c_wmean, bank[0][:, 0:2], 1.0 / (D * HID), 1e-5, ALU.mult, ALU.max))
            link(dve, "dve", dve.reciprocal(c_winv, c_wmean))
            for k, (name, f, q) in enumerate((("w1T", c_w1f, c_w1q), ("w2T", c_w2f, c_w2q))):
                link(dve, "dve", dve.tensor_scalar(f, w(name), c_winv[:, k:k + 1], MAGIC, ALU.mult, ALU.add))
                link(dve, "dve", dve.tensor_scalar(f, f, MAGIC, 1.0, ALU.subtract, ALU.min))
                dve.tensor_scalar(q, f, -1.0, None, ALU.max).then_inc(sem("c_wq"), 1)
            ln_dve(dve, 3, x_tok, lambda c: dve.wait_ge(sem("x_done"), c + 1))
            for c in range(NC):
                tiles = slice(4 * c, 4 * c + 4)
                dve.wait_ge(sem("ln_xn"), 3 * NC + c + 1)
                link(dve, "dve", dve.tensor_reduce(c_m[:, tiles], xn_tok[:, tiles, :], AX.X, ALU.max,
                                                   apply_absolute_value=True))
                quant_scales(dve, 4 * c, 4, 0)
                dve.nop().then_inc(sem("c_scale"), 1)
                for t in range(4 * c, 4 * c + 4):
                    ins = dve.tensor_scalar(c_qf[:, t, :], xn_tok[:, t, :], c_s[:, t:t + 1], MAGIC, ALU.mult, ALU.add)
                link(dve, "dve", ins)
                dve.tensor_scalar(c_q[:, tiles, :], c_qf[:, tiles, :], MAGIC, None, ALU.subtract)\
                   .then_inc(sem("c_q"), 1)
            def conv(j):
                for n, (tap, lo) in enumerate(((0, 0), (2, 2))):
                    dve.wait_ge(sem("c_mid"), j + 1)
                    if n:
                        dve.wait_ge(sem("c_left"), j + 1)
                    dve.scalar_tensor_tensor(out=steps(c_t[j % 2]), in0=c_hp[j % 2][:, :, lo:lo + S],
                                             scalar=vec("convw", 3 * j + tap), in1=steps(c_t[j % 2]),
                                             op0=ALU.mult, op1=ALU.add)\
                       .then_inc(sem("c_right" if n else "c_left"), 1)

            for j in range(4):
                for c in range(NC):
                    k = 4 * j + c
                    dve.wait_ge(sem("c_h"), k + 1)
                    dve.wait_ge(sem("c_R"), c + 1)
                    if j >= 2:
                        dve.wait_ge(sem("c_right"), j - 1)
                    dve.tensor_tensor(c_hp[j % 2][:, 16 * c:16 * c + 16, 1:S + 1], steps(bank[k % 4]),
                                      steps(c_R[:, c * CH:(c + 1) * CH]), ALU.mult).then_inc(sem("c_hp"), 1)
                if j >= 1:
                    conv(j - 1)
            conv(3)
            for g in range(NC):
                for t in range(4):
                    dve.wait_ge(sem("c_ht"), 4 * g + t + 1)
                    ins = dve.tensor_reduce(c_m[:, NT + 4 * g + t:NT + 4 * g + t + 1], bank[t], AX.X, ALU.max,
                                            apply_absolute_value=True)
                link(dve, "dve", ins)
                quant_scales(dve, NT + 4 * g, 4, 1)
                dve.nop().then_inc(sem("c_scale2"), 1)
                for t in range(4):
                    dve.wait_ge(sem("c_q2f"), 4 * g + t + 1)
                    if g >= 1:
                        dve.wait_ge(sem("c_q2t"), 4 * (g - 1) + t + 1)
                    dve.tensor_scalar(c_q2[t], c_q2f[t], MAGIC, None, ALU.subtract).then_inc(sem("c_q2"), 1)
                for t in range(4):
                    tt = 4 * g + t
                    dve.wait_ge(sem("c_o"), tt + 1)
                    ins = dve.scalar_tensor_tensor(out=x_tok[:, tt, :], in0=bank[6 + t % 2][:, 0:D],
                                                   scalar=c_dq[:, NT + tt:NT + tt + 1], in1=x_tok[:, tt, :],
                                                   op0=ALU.mult, op1=ALU.add)
                    ins.then_inc(sem("c_x"), 1)
                dve.wait_ge(sem("c_x"), 4 * g + 4)
                dve.nop().then_inc(sem("x_done"), 1)

        def c_pe(pe):
            pe.wait_ge(sem("c_wsum"), 1)
            pe.matmul(bank[0][:, 0:2], c_ones, c_wsum, start=True, stop=True).then_inc(sem("c_wtot"), 1)
            pe.wait_ge(sem("c_identb"), 1)
            for c in range(NC):
                pe.wait_ge(sem("c_scale"), c + 1)
                for t in range(4):
                    ins = pe.matmul(bank[4 + c % 2][:, t * P:(t + 1) * P],
                                    c_dq[:, 4 * c + t:4 * c + t + 1].broadcast_to([P, P]), ident,
                                    start=True, stop=True)
                ins.then_inc(sem("c_Rp"), 1)
                pe.wait_ge(sem("c_q"), c + 1)
                for t in range(4):
                    ins = pe.transpose(bank[6 + c % 2][:, t * 64:(t + 1) * 64].bitcast(BF16), c_q[:, 4 * c + t, :],
                                       c_identb)
                ins.then_inc(sem("c_qt"), 1)
                if c >= 1:
                    pe.wait_ge(sem("c_R"), c)
                    pe.wait_ge(sem("c_qT"), c)
            pe.wait_ge(sem("c_wq"), 2)
            for k in range(16):
                j, c = k // 4, k % 4
                pe.wait_ge(sem("c_qT"), c + 1)
                if k >= 4:
                    pe.wait_ge(sem("c_hp"), k - 3)
                pe.matmul(bank[k % 4], c_w1q[:, j * P:(j + 1) * P], c_qT[:, c * CH:(c + 1) * CH],
                          start=True, stop=True).then_inc(sem("c_h"), 1)
            pe.wait_ge(sem("c_hp"), 16)
            pe.wait_ge(sem("c_hs"), 4)

            def to_tokens(tt):
                for j in range(4):
                    ins = pe.transpose(bank[tt % 4][:, j * P:(j + 1) * P], c_hs[j][:, tt * P:(tt + 1) * P], ident)
                ins.then_inc(sem("c_ht"), 1)

            for tt in range(4):
                to_tokens(tt)
            for tt in range(NT):
                pe.wait_ge(sem("c_q2"), tt + 1)
                if tt >= 2:
                    pe.wait_ge(sem("c_q2T"), tt - 1)
                for j in range(4):
                    ins = pe.transpose(bank[4 + tt % 2][:, j * 64:(j + 1) * 64].bitcast(BF16),
                                       c_q2[tt % 4][:, j * P:(j + 1) * P], c_identb)
                ins.then_inc(sem("c_q2t"), 1)
                pe.wait_ge(sem("c_q2T"), tt + 1)
                if tt >= 2:
                    pe.wait_ge(sem("c_x"), tt - 1)
                for j in range(4):
                    ins = pe.matmul(bank[6 + tt % 2][:, 0:D], c_q2T[tt % 4][:, j, :], c_w2q[:, j * P:(j + 1) * P],
                                    start=(j == 0), stop=(j == 3))
                ins.then_inc(sem("c_o"), 1)
                if tt + 4 < NT:
                    to_tokens(tt + 4)

        def c_act(act):
            for c in range(NC):
                act.wait_ge(sem("c_Rp"), c + 1)
                act.activation(c_R[:, c * CH:(c + 1) * CH], bank[4 + c % 2], ACT.Copy).then_inc(sem("c_R"), 1)
                act.wait_ge(sem("c_qt"), c + 1)
                act.activation(c_qT[:, c * CH:(c + 1) * CH], bank[6 + c % 2][:, 0:CH // 2].bitcast(BF16), ACT.Copy)\
                   .then_inc(sem("c_qT"), 1)

            def silu(j):
                act.wait_ge(sem("c_right"), j + 1)
                act.activation(c_hs[j], c_t[j % 2], ACT.Silu).then_inc(sem("c_hs"), 1)

            for j in range(4):
                if j >= 2:
                    silu(j - 2)
                    act.wait_ge(sem("c_hs"), j - 1)
                act.wait_ge(sem("c_hp"), 4 * j + 4)
                act.activation(steps(c_t[j % 2]), c_hp[j % 2][:, :, 1:S + 1], ACT.Identity,
                               scale=vec("convw", 3 * j + 1), bias=vec("convb", j)).then_inc(sem("c_mid"), 1)
            silu(2)
            silu(3)
            for g in range(NC):
                act.wait_ge(sem("c_scale2"), g + 1)
                for t in range(4):
                    tt = 4 * g + t
                    if g >= 1:
                        act.wait_ge(sem("c_q2"), tt - 3)
                    act.activation(c_q2f[t], bank[t], ACT.Copy, scale=c_s[:, NT + tt:NT + tt + 1], bias=MAGIC)\
                       .then_inc(sem("c_q2f"), 1)
                for t in range(4):
                    tt = 4 * g + t
                    act.wait_ge(sem("c_q2t"), tt + 1)
                    act.activation(c_q2T[t], bank[4 + tt % 2][:, 0:CH // 2].bitcast(BF16)
                                   .rearrange("p (k n) -> p k n", k=4), ACT.Copy).then_inc(sem("c_q2T"), 1)


        rd = Room()
        d_qT, d_aT = rd.take(T), rd.take(T)
        d_qb = [rd.take(4 * P) for _ in range(4)]
        d_mb = [rd.take(K2 + 1, BF16) for _ in range(4)]
        d_neg = rd.take(P, BF16)
        d_kT = [rd.take(K2P) for _ in range(2)]
        d_v = [rd.take(3 * P).rearrange("p (k n) -> p k n", k=3) for _ in range(2)]
        d_p = [rd.take(4 * K2P).rearrange("p (c k) -> p c k", c=4) for _ in range(2)]
        d_nmax = [rd.take(4) for _ in range(2)]
        d_sum = [rd.take(4) for _ in range(2)]
        d_rs = [rd.take(4) for _ in range(2)]
        d_pT = [rd.take(4 * 3 * P).rearrange("p (c k n) -> p c k n", c=4, k=3) for _ in range(2)]
        d_tmp = rd.take(P)
        d_msk = [rd.take(68).bitcast(U8) for _ in range(4)]
        d_keys = bank[6][:, P:P + K2P]
        assert rd.at <= RING_AT
        STEPS = B // 4 - 1

        def d_load(sp, j, r):
            sp.dma_start(ctxT_ring[j][:, 0:K2P],
                         ctxT_d[bass.ds(r, 1), :, j * K2P:(j + 1) * K2P].rearrange("g p k -> p (g k)"))\
              .then_inc(sem(f"d_ctx{j}"), 16)
            for c in range(4):
                sp.dma_start(d_msk[j][32 * c:32 * c + 32, 0:K2],
                             mask_d[bass.ds(4 * r + j, 1), :, :].rearrange("g s k -> s (g k)"))\
                  .then_inc(sem(f"d_ctx{j}"), 16)

        def d_sp(sp):
            sp.wait_ge(sem("x_done"), 2 * NC)
            for j in range(4):
                d_load(sp, j, 0)
            with sp.Fori(0, STEPS) as r:
                for j in range(4):
                    sp.wait_ge(sem("d_vp"), r * 4 + j + 1)
                    sp.wait_ge(sem("d_mb"), r * 4 + j + 1)
                    d_load(sp, j, r + 1)

        def d_pool(pool):
            ln_pool(pool, 4)
            pool.wait_ge(sem("ln_xn"), 5 * NC)
            pool.tensor_tensor(x_tok[:, :, :], x_tok[:, :, :],
                               row("xbo").unsqueeze(1).broadcast_to([P, NT, D]), ALU.add)\
                .then_inc(sem("d_xbo"), 1)
            pool.wait_ge(sem("d_qT"), NC)

            def operands(b, j, r):
                pool.wait_ge(sem(f"d_ctx{j}"), r * 80 + 80)
                pool.tensor_tensor(d_qb[j].rearrange("p (h s) -> p h s", h=NH),
                                   const("heads").rearrange("p (h s) -> p h s", h=NH),
                                   d_qT[:, bass.ds(b * S, S)].unsqueeze(1).broadcast_to([P, NH, S]),
                                   ALU.mult)
                pool.tensor_copy(d_mb[j][:, 0:K2], d_msk[j][:, 0:K2]).then_inc(sem("d_mb"), 1)

            operands(0, 0, 0)
            operands(1, 1, 0)
            operands(2, 2, 0)
            with pool.Fori(0, STEPS) as r:
                for j in range(4):
                    pool.wait_ge(sem("d_s"), r * 8 + 2 * j + 2)
                    operands(r * 4 + j + 3, (j + 3) % 4, r + (j + 3) // 4)
            pool.wait_ge(sem("d_s"), STEPS * 8 + 2)
            operands(STEPS * 4 + 3, 3, STEPS)

        def d_pe(pe):
            ln_pe(pe, 4, 2)
            for c in range(NC):
                pe.wait_ge(sem("ln_T"), 2 * NC + c + 1)
                pe.matmul(bank[c], w("xq"), xnT[:, c * CH:(c + 1) * CH], start=True, stop=True)\
                  .then_inc(sem("d_qp"), 1)
            pe.wait_ge(sem("d_neg"), 1)
            pe.wait_ge(sem("d_qT"), NC)

            def project_k(b, j, r, first=False):
                pe.wait_ge(sem(f"d_ctx{j}"), r * 80 + 80)
                if not first:
                    pe.wait_ge(sem("d_diag"), b - 1)
                pe.matmul(d_keys, w("xk"), ctxT_ring[j][:, 0:K2P], start=True, stop=True)\
                  .then_inc(sem("d_kp"), 1)

            def project_v(b, j, first=False):
                if not first:
                    pe.wait_ge(sem("d_v"), b)
                for k in range(3):
                    ins = pe.matmul(bank[7][0:KW, k * P:(k + 1) * P], ctxT_ring[j][:, k * KW:(k + 1) * KW],
                                    w("xv"), start=True, stop=True)
                ins.then_inc(sem("d_vp"), 1)

            def scores(b, j, half, first=False):
                if half == 0:
                    pe.wait_ge(sem("d_mb"), b + 1)
                    pe.wait_ge(sem("d_kT"), b + 1)
                if not first:
                    pe.wait_ge(sem("d_exp"), b * 2 - 1 + half)
                for c in (2 * half, 2 * half + 1):
                    pe.matmul(bank[c][:, 0:K2], d_qb[j][:, c * P:(c + 1) * P], d_kT[j % 2][:, 0:K2],
                              start=True, stop=False)
                    ins = pe.matmul(bank[c][:, 0:K2], d_neg, d_mb[j][:, 0:K2], start=False, stop=True)
                ins.then_inc(sem("d_s"), 1)

            def transposed(b, j, c):
                if c % 2 == 0:
                    pe.wait_ge(sem("d_pn"), b * 2 + 1 + c // 2)
                if c >= 2:
                    pe.wait_ge(sem(("d_pTv", "d_pTa")[c % 2]), b * 2 + 1)
                for k in range(3):
                    ins = pe.transpose(bank[4 + c % 2][0:KW, k * P:(k + 1) * P],
                                       d_p[j % 2][:, c, k * KW:(k + 1) * KW], ident)
                ins.then_inc(sem("d_t"), 1)

            def averages(b, j, last=False):
                if not last:
                    pe.wait_ge(sem("d_kT"), b + 3)
                pe.wait_ge(sem("d_v"), b + 1)
                pe.wait_ge(sem("d_pTv"), b * 2 + 2)
                pe.wait_ge(sem("d_pTa"), b * 2 + 2)
                pe.wait_ge(sem("d_diag"), b + 1)
                for k in range(3):
                    for c in range(4):
                        ins = pe.matmul(bank[6][32 * c:32 * c + 32, 0:P], d_v[j % 2][0:KW, k, 32 * c:32 * c + 32],
                                        d_pT[j % 2][0:KW, c, k, :], start=(k == 0), stop=(k == 2))
                ins.then_inc(sem("d_pv"), 1)

            def step(b, j, r, left=3, first=False):
                n, jn = b + 1, (j + 1) % 4
                if left > 0:
                    scores(n, jn, 0)
                if not first:
                    averages(b - 1, j - 1, last=(left == 0))
                transposed(b, j, 0)
                transposed(b, j, 1)
                if left > 0:
                    scores(n, jn, 1)
                if left > 1:
                    project_k(b + 2, (j + 2) % 4, r + (j + 2) // 4)
                if left > 0:
                    project_v(n, jn)
                transposed(b, j, 2)
                transposed(b, j, 3)

            project_k(0, 0, 0, first=True)
            project_v(0, 0, first=True)
            scores(0, 0, 0, first=True)
            scores(0, 0, 1, first=True)
            project_k(1, 1, 0, first=True)
            step(0, 0, 0, first=True)
            with pe.Fori(0, STEPS) as r:
                for j in range(1, 5):
                    step(r * 4 + j, j, r)
            for j in range(1, 4):
                step(STEPS * 4 + j, j, STEPS, left=3 - j)
            averages(B - 1, 3, last=True)
            pe.wait_ge(sem("d_aT"), B)
            for c in range(NC):
                for t in range(4):
                    tt = 4 * c + t
                    ins = pe.matmul(bank[c][:, t * P:(t + 1) * P], d_aT[:, tt * P:(tt + 1) * P], w("xo"),
                                    start=True, stop=True)
                ins.then_inc(sem("d_out"), 1)

        def d_act(act):
            ln_act(act, 2)

            def keys(b, j):
                act.wait_ge(sem("d_kp"), b + 1)
                act.activation(d_kT[j % 2], d_keys, ACT.Identity, bias=vec("xbk")).then_inc(sem("d_kT"), 1)

            def values(b, j):
                act.wait_ge(sem("d_vp"), b + 1)
                act.activation(d_v[j % 2][0:KW], bank[7][0:KW, 0:3 * P].rearrange("p (k n) -> p k n", k=3), ACT.Copy)\
                   .then_inc(sem("d_v"), 1)

            def exps(b, j, half):
                act.wait_ge(sem("d_max"), b * 2 + 1 + half)
                for c in (2 * half, 2 * half + 1):
                    ins = act.activation(d_p[j % 2][:, c, 0:K2], bank[c][:, 0:K2], ACT.Exp,
                                         bias=d_nmax[j % 2][:, c:c + 1], accum_out=d_sum[j % 2][:, c:c + 1])
                ins.then_inc(sem("d_exp"), 1)

            def out_of_bank_5(b, j, c):
                act.wait_ge(sem("d_t"), b * 4 + c + 1)
                act.activation(d_pT[j % 2][0:KW, c], bank[5][0:KW, 0:3 * P].rearrange("p (k n) -> p k n", k=3), ACT.Copy)\
                   .then_inc(sem("d_pTa"), 1)

            def step(b, j, left=3):
                jn = (j + 1) % 4
                if left > 0:
                    exps(b + 1, jn, 0)
                out_of_bank_5(b, j, 1)
                if left > 1:
                    keys(b + 2, (j + 2) % 4)
                if left > 0:
                    exps(b + 1, jn, 1)
                    values(b + 1, jn)
                out_of_bank_5(b, j, 3)

            keys(0, 0)
            values(0, 0)
            exps(0, 0, 0)
            exps(0, 0, 1)
            keys(1, 1)
            step(0, 0)
            with act.Fori(0, STEPS) as r:
                for j in range(1, 5):
                    step(r * 4 + j, j)
            for j in range(1, 4):
                step(STEPS * 4 + j, j, left=3 - j)

        def d_dve(dve):
            ln_dve(dve, 4, x_tok, lambda c: dve.wait_ge(sem("x_done"), NC + c + 1))
            dve.tensor_copy(d_neg, const("negsel")).then_inc(sem("d_neg"), 1)
            for u in range(2):
                ins = dve.memset(d_p[u][:, :, K2], 0.0)
            link(dve, "dve", ins)
            for c in range(NC):
                dve.wait_ge(sem("d_qp"), c + 1)
                dve.tensor_scalar(d_qT[:, c * CH:(c + 1) * CH], bank[c], vec("xbq"), float(DK) ** -0.5,
                                  ALU.add, ALU.mult).then_inc(sem("d_qT"), 1)

            def maxima(b, j, half):
                dve.wait_ge(sem("d_s"), b * 2 + 1 + half)
                cs = slice(2 * half, 2 * half + 2)
                dve.tensor_reduce(d_nmax[j % 2][:, cs],
                                  banks(2 * half, 2).rearrange("p (c k) -> p c k", c=2)[:, :, 0:K2],
                                  AX.X, ALU.max, negate=True).then_inc(sem("d_max"), 1)

            def normalised(b, j, half):
                cs = slice(2 * half, 2 * half + 2)
                dve.wait_ge(sem("d_exp"), b * 2 + 1 + half)
                dve.reciprocal(d_rs[j % 2][:, cs], d_sum[j % 2][:, cs]).then_inc(sem("d_rs"), 1)
                dve.wait_ge(sem("d_rs"), b * 2 + 1 + half)
                for c in (2 * half, 2 * half + 1):
                    ins = dve.tensor_scalar(d_p[j % 2][:, c, 0:K2], d_p[j % 2][:, c, 0:K2],
                                            d_rs[j % 2][:, c:c + 1], None, ALU.mult)
                ins.then_inc(sem("d_pn"), 1)

            def out_of_bank_4(b, j, c):
                dve.wait_ge(sem("d_t"), b * 4 + c + 1)
                dve.tensor_copy(d_pT[j % 2][0:KW, c], bank[4][0:KW, 0:3 * P].rearrange("p (k n) -> p k n", k=3))\
                   .then_inc(sem("d_pTv"), 1)

            def own_blocks(b):
                dve.wait_ge(sem("d_pv"), b + 1)
                dve.scalar_tensor_tensor(out=d_tmp, in0=bank[6][:, 0:P], scalar=vec("xbv"), in1=const("headsel"),
                                         op0=ALU.add, op1=ALU.mult).then_inc(sem("d_diag"), 1)

            def folded(b):
                dve.wait_ge(sem("d_diag"), b + 2)
                dve.tensor_reduce(d_aT[:, bass.ds(b * S, S)], d_tmp.rearrange("p (h s) -> p s h", h=4),
                                  AX.X, ALU.add).then_inc(sem("d_aT"), 1)

            def step(b, j, first=False, last=False):
                jn = (j + 1) % 4
                if not last:
                    maxima(b + 1, jn, 0)
                if not first:
                    own_blocks(b - 1)
                out_of_bank_4(b, j, 0)
                if not first:
                    folded(b - 1)
                if not last:
                    maxima(b + 1, jn, 1)
                    normalised(b + 1, jn, 0)
                out_of_bank_4(b, j, 2)
                if not last:
                    normalised(b + 1, jn, 1)

            dve.nop().then_inc(sem("d_diag"), 1)
            maxima(0, 0, 0)
            maxima(0, 0, 1)
            normalised(0, 0, 0)
            normalised(0, 0, 1)
            step(0, 0, first=True)
            with dve.Fori(0, STEPS) as r:
                for j in range(1, 5):
                    step(r * 4 + j, j)
            for j in range(1, 4):
                step(STEPS * 4 + j, j, last=(j == 3))
            own_blocks(B - 1)
            folded(B - 1)
            dve.wait_ge(sem("d_xbo"), 1)
            for c in range(NC):
                dve.wait_ge(sem("d_out"), c + 1)
                dve.tensor_tensor(x_tok[:, 4 * c:4 * c + 4, :], bank[c].rearrange("p (t d) -> p t d", d=D),
                                  x_tok[:, 4 * c:4 * c + 4, :], ALU.add).then_inc(sem("x_done"), 1)

        re_ = Room()
        e_r, e_k, e_e = (re_.take(RH * T) for _ in range(3))
        e_vT, e_sg = re_.take(T), re_.take(T)
        flat = ring[:, :, :].rearrange("p a b -> p (a b)")
        e_delta, e_xlA = flat[:, 0:T], flat[:, T:2 * T]
        e_xi = [flat[:, 2 * T + i * CH:2 * T + (i + 1) * CH] for i in range(2)]
        e_tan = [flat[0:64, 2 * T + (2 + i) * CH:2 * T + (3 + i) * CH] for i in range(2)]
        e_xlB = xn_tok[:, :, :].rearrange("p t d -> p (t d)")
        e_at = [flat[:, i * HT:(i + 1) * HT] for i in range(2)]
        e_vt = flat[:, T:2 * T]
        e_ruk = [e_xlB, flat[:, 2 * T:3 * T]]
        e_w = xnT[:, :]
        MIX = ("r", "w", "k", "v", "g")
        units = [(c, n) for c in range(NC) for n in range(5)]
        outs = []
        for q, (c, n) in enumerate(units):
            if MIX[n] == "r":
                outs += [(q, "r", h, "act") for h in range(RH)]
            elif MIX[n] == "k":
                outs += [(q, "k", h, "dve") for h in range(RH)]
            elif MIX[n] == "w":
                outs += [(q, "wA", 0, "act")] + [(q, "w", h, "act") for h in range(RH)]
            elif MIX[n] == "v":
                outs += [(q, "v", 0, "dve")]
            else:
                outs += [(q, "gA", 0, "act"), (q, "g", 0, "act")]
        out_count = []
        seen = {"act": 0, "dve": 0}
        for o in outs:
            seen[o[3]] += 1
            out_count.append((o[3], seen[o[3]]))
        tan_index = {}
        for q, kind, _, _ in outs:
            if kind in ("wA", "gA"):
                tan_index[q] = len(tan_index)

        def chunk(a, c):
            return a[:, c * CH:(c + 1) * CH]

        def head_chunk(a, h, c):
            return a[:, h * T + c * CH:h * T + (c + 1) * CH]

        def sides(a, n):
            return a.rearrange("p (b s n) -> p b s n", s=2, n=n)

        jobs = [(l, h) for l in range(len(LEVELS)) for h in range(RH)]

        def e_pool(pool):
            ln_pool(pool, 5)
            for l in range(len(LEVELS) - 1):
                n = LEVELS[l]
                for h in range(RH):
                    i = l * RH + h
                    k = sides(e_k[:, h * T:(h + 1) * T], n)
                    e = sides(e_e[:, h * T:(h + 1) * T], n)
                    pool.wait_ge(sem("e_a"), i + 1)
                    if l:
                        pool.wait_ge(sem("e_T"), i - RH + 1)
                        pool.wait_ge(sem("e_K"), i - RH + 1)
                    pool.tensor_tensor(k[:, :, 0, :], k[:, :, 0, :],
                                       e[:, :, 1, 0:1].broadcast_to([P, T // 2 // n, n]), ALU.mult)\
                        .then_inc(sem("e_K"), 1)
                    pool.wait_ge(sem("e_R"), i + 1)
                    pool.wait_ge(sem("e_K"), i + 1)
                    pool.tensor_tensor(e[:, :, 0, 0], e[:, :, 0, 0], e[:, :, 1, 0], ALU.mult)\
                        .then_inc(sem("e_T"), 1)
            ln_pool(pool, 6)

        def e_pe(pe):
            ln_pe(pe, 5, 3)
            o = [0]

            def product(lhsT, rhs, m=P):
                if o[0] >= 6:
                    e, n = out_count[o[0] - 6]
                    pe.wait_ge(sem("e_left_" + e), n)
                ins = pe.matmul(bank[2 + o[0] % 6][0:m, :], lhsT, rhs, start=True, stop=True)
                ins.then_inc(sem("e_out"), 1)
                o[0] += 1

            pe.wait_ge(sem("ln_T"), 4 * NC)
            for c in range(NC):
                pe.wait_ge(sem("e_xm"), c + 1)
                if c >= 1:
                    pe.wait_ge(sem("e_xl"), c)
                pe.matmul(bank[0], w("rW1T", 0, P), e_xi[c % 2], start=True, stop=True)
                pe.matmul(bank[1][0:32, :], w("rW1T", P, 160), e_xi[c % 2], start=True, stop=True)\
                  .then_inc(sem("e_xlp"), 1)
            pe.wait_ge(sem("e_xl"), NC)

            def mixing(q):
                c, n = units[q]
                if q >= 2:
                    pe.wait_ge(sem("e_m"), q - 1)
                if n < 4:
                    rows = slice(32 * n, 32 * n + 32)
                    pe.matmul(bank[q % 2], W[rows, WAT["rW2Ta"][0]:WAT["rW2Ta"][0] + P], chunk(e_xlA, c)[rows, :],
                              start=True, stop=True).then_inc(sem("e_x5"), 1)
                else:
                    pe.matmul(bank[q % 2], w("rW2Tb", rows=32), chunk(e_xlB, c)[0:32, :],
                              start=True, stop=True).then_inc(sem("e_x5"), 1)

            mixing(0)
            for q, (c, n) in enumerate(units):
                if q + 1 < len(units):
                    mixing(q + 1)
                pe.wait_ge(sem("e_xi"), q + 1)
                xi = e_xi[q % 2]
                kind = MIX[n]
                if kind in "rk":
                    for h in range(RH):
                        product(w("rrT" if kind == "r" else "rkT", h * P, (h + 1) * P), xi)
                elif kind == "v":
                    product(w("rvT"), xi)
                else:
                    product(w("rwAT" if kind == "w" else "rgAT"), xi, 64)
                if kind in "wg":
                    pe.wait_ge(sem("e_left_act"), out_count[o[0] - 1][1])
                    tan = e_tan[tan_index[q] % 2]
                    if kind == "w":
                        for h in range(RH):
                            product(w("rwBT", h * P, (h + 1) * P, rows=64), tan)
                    else:
                        product(w("rgBT", rows=64), tan)
            pe.wait_ge(sem("e_left_act"), seen["act"])
            pe.wait_ge(sem("e_left_dve"), seen["dve"])
            for h in range(RH):
                pe.wait_ge(sem("e_ruk"), h + 1)
                for c in range(NC):
                    ins = pe.matmul(bank[c][32 * h:32 * h + 32, :], const("ones", 0, 32), chunk(e_ruk[h % 2], c),
                                    start=True, stop=True)
                ins.then_inc(sem("e_diag"), 1)
            for tt in range(NT):
                ins = pe.transpose(banks(4, 4)[:, tt * P:(tt + 1) * P], e_vT[:, tt * P:(tt + 1) * P], ident)
            ins.then_inc(sem("e_vtp"), 1)
            pe.wait_ge(sem("zeros"), 1)
            pe.wait_ge(sem("e_vt"), 1)
            for c in range(NC):
                pe.matmul(bank[4 + c], zeros[:, 0:P], zeros[:, :], start=True, stop=False, skip_group_check=True)
            pe.wait_ge(sem("e_dg"), 1)

            def decayed(m):
                l, h = jobs[m]
                if m >= 2:
                    pe.wait_ge(sem("e_at"), m - 1)
                if l:
                    pe.wait_ge(sem("e_K"), m - RH + 1)
                    pe.wait_ge(sem("e_R"), m - RH + 1)
                for g in range(NT):
                    tokens = slice(h * T + g * P, h * T + (g + 1) * P)
                    ins = pe.matmul(banks(2 * (m % 2), 2)[:, g * 64:(g + 1) * 64], e_k[:, tokens],
                                    sides(e_r[:, tokens], LEVELS[l])[:, :, 1, :], start=True, stop=True)
                ins.then_inc(sem("e_a"), 1)

            def outputs(m):
                l, h = jobs[m]
                pe.wait_ge(sem("e_at"), m + 1)
                for g in range(NT):
                    out = sides(banks(4, 4)[32 * h:32 * h + 32, g * P:(g + 1) * P], LEVELS[l])[:, :, 1, :]
                    ins = pe.matmul(out, e_vt[:, g * P + 32 * h:g * P + 32 * h + 32],
                                    e_at[m % 2][:, g * 64:(g + 1) * 64],
                                    start=False, stop=(l == len(LEVELS) - 1), skip_group_check=True)
                ins.then_inc(sem("e_o"), 1)

            for m in range(len(jobs)):
                decayed(m)
                if m >= 1:
                    outputs(m - 1)
            outputs(len(jobs) - 1)
            for c in range(NC):
                pe.wait_ge(sem("e_oT"), c + 1)
                for t in range(4):
                    tt = 4 * c + t
                    ins = pe.transpose(bank[c][:, t * P:(t + 1) * P], e_w[:, tt * P:(tt + 1) * P], ident)
                ins.then_inc(sem("e_ot"), 1)
            pe.wait_ge(sem("e_oT"), NC)
            ln_pe(pe, 6, 4)
            for c in range(NC):
                pe.wait_ge(sem("e_gated"), c + 1)
                for t in range(4):
                    tt = 4 * c + t
                    ins = pe.matmul(bank[c][:, t * P:(t + 1) * P], e_w[:, tt * P:(tt + 1) * P], w("roT"),
                                    start=True, stop=True)
                ins.then_inc(sem("e_proj"), 1)

        def e_act(act):
            ln_act(act, 3)
            for c in range(NC):
                act.wait_ge(sem("e_xlp"), c + 1)
                act.activation(chunk(e_xlA, c), bank[0], ACT.Tanh)
                act.activation(chunk(e_xlB, c)[0:32, :], bank[1][0:32, :], ACT.Tanh).then_inc(sem("e_xl"), 1)
            for o, (q, kind, h, e) in enumerate(outs):
                if e != "act":
                    continue
                c = units[q][0]
                src = bank[2 + o % 6]
                act.wait_ge(sem("e_out"), o + 1)
                if kind == "r":
                    act.activation(head_chunk(e_r, h, c), src, ACT.Copy).then_inc(sem("e_left_act"), 1)
                elif kind in ("wA", "gA"):
                    act.activation(e_tan[tan_index[q] % 2], src[0:64, :], ACT.Tanh).then_inc(sem("e_left_act"), 1)
                elif kind == "w":
                    act.activation(head_chunk(e_e, h, c), src, ACT.Exp, bias=vec("wb", h))\
                       .then_inc(sem("e_left_act"), 1)
                else:
                    act.activation(chunk(e_sg, c), src, ACT.Identity, bias=vec("gb")).then_inc(sem("e_left_act"), 1)
            act.wait_ge(sem("e_left_act"), seen["act"])
            for h in range(RH):
                act.activation(e_e[:, h * T:(h + 1) * T], e_e[:, h * T:(h + 1) * T], ACT.Exp, scale=-1.0)\
                   .then_inc(sem("e_decay"), 1)
            act.activation(e_sg, e_sg, ACT.Silu).then_inc(sem("e_sg"), 1)
            act.wait_ge(sem("e_vtp"), 1)
            act.activation(e_vt, banks(4, 4), ACT.Copy).then_inc(sem("e_vt"), 1)
            for c in range(NC):
                act.wait_ge(sem("ln_tr"), 4 * NC + c + 1)
                act.activation(chunk(e_w, c), bank[6 + c % 2], ACT.Identity, scale=vec("gnw"), bias=vec("gnb"))\
                   .then_inc(sem("ln_T"), 1)

        def e_dve(dve):
            dve.memset(zeros[:, :], 0.0).then_inc(sem("zeros"), 1)
            ln_dve(dve, 5, x_tok, lambda c: dve.wait_ge(sem("x_done"), 2 * NC + c + 1))
            dve.wait_ge(sem("ln_T"), 4 * NC)
            xs_, ds_ = steps(xnT[:, :]), steps(e_delta)
            dve.tensor_tensor(ds_[:, :, 1:S], xs_[:, :, 0:S - 1], xs_[:, :, 1:S], ALU.subtract)
            link(dve, "dve", dve.tensor_scalar(ds_[:, :, 0], xs_[:, :, 0], -1.0, None, ALU.mult))
            for c in range(NC):
                if c >= 2:
                    dve.wait_ge(sem("e_xlp"), c - 1)
                dve.scalar_tensor_tensor(out=e_xi[c % 2], in0=chunk(e_delta, c), scalar=vec("mu"),
                                         in1=chunk(xnT, c), op0=ALU.mult, op1=ALU.add).then_inc(sem("e_xm"), 1)
            dve.wait_ge(sem("e_xlp"), NC)
            last_out = {q: o for o, (q, kind, _, _) in enumerate(outs) if kind not in ("w", "g")}

            def evacuate(q):
                for o, (q2, kind, h, e) in enumerate(outs):
                    if q2 != q or e != "dve":
                        continue
                    c = units[q][0]
                    dve.wait_ge(sem("e_out"), o + 1)
                    dst = head_chunk(e_k, h, c) if kind == "k" else chunk(e_vT, c)
                    dve.tensor_copy(dst, bank[2 + o % 6]).then_inc(sem("e_left_dve"), 1)

            for q, (c, n) in enumerate(units):
                dve.wait_ge(sem("e_x5"), q + 1)
                if q >= 2:
                    dve.wait_ge(sem("e_out"), last_out[q - 2] + 1)
                dve.scalar_tensor_tensor(out=e_xi[q % 2], in0=bank[q % 2], scalar=vec("xbias", n),
                                         in1=chunk(e_delta, c), op0=ALU.add, op1=ALU.mult).then_inc(sem("e_m"), 1)
                dve.wait_ge(sem("e_m"), q + 1)
                dve.tensor_tensor(e_xi[q % 2], e_xi[q % 2], chunk(xnT, c), ALU.add).then_inc(sem("e_xi"), 1)
                if q >= 1:
                    evacuate(q - 1)
            evacuate(len(units) - 1)
            dve.wait_ge(sem("e_left_dve"), seen["dve"])
            dve.wait_ge(sem("e_left_act"), seen["act"])
            dve.wait_ge(sem("e_out"), len(outs))
            for h in range(RH):
                if h >= 2:
                    dve.wait_ge(sem("e_diag"), h - 1)
                dve.scalar_tensor_tensor(out=e_ruk[h % 2], in0=e_r[:, h * T:(h + 1) * T], scalar=vec("bonus", h),
                                         in1=e_k[:, h * T:(h + 1) * T], op0=ALU.mult, op1=ALU.mult)\
                   .then_inc(sem("e_ruk"), 1)
            dve.wait_ge(sem("e_diag"), RH)
            dve.tensor_tensor(e_w, banks(0, 4), e_vT, ALU.mult).then_inc(sem("e_dg"), 1)
            dve.wait_ge(sem("e_decay"), RH)
            for m, (l, h) in enumerate(jobs):
                i, n = m, LEVELS[l]
                dve.wait_ge(sem("e_a"), i + 1)
                if i >= 2:
                    dve.wait_ge(sem("e_o"), i - 1)
                mask = const("levels", l * 64, (l + 1) * 64).unsqueeze(1).broadcast_to([P, NT, 64])
                dve.tensor_tensor(e_at[i % 2].rearrange("p (g t) -> p g t", g=NT),
                                  banks(2 * (m % 2), 2).rearrange("p (g t) -> p g t", g=NT), mask, ALU.mult)\
                   .then_inc(sem("e_at"), 1)
                if l < len(LEVELS) - 1:
                    r = sides(e_r[:, h * T:(h + 1) * T], n)
                    e = sides(e_e[:, h * T:(h + 1) * T], n)
                    if l:
                        dve.wait_ge(sem("e_T"), i - RH + 1)
                        dve.wait_ge(sem("e_R"), i - RH + 1)
                    dve.tensor_tensor(r[:, :, 1, :], r[:, :, 1, :],
                                      e[:, :, 0, 0:1].broadcast_to([P, T // 2 // n, n]), ALU.mult)\
                       .then_inc(sem("e_R"), 1)
            dve.wait_ge(sem("e_o"), len(LEVELS) * RH)
            for c in range(NC):
                dve.tensor_tensor(chunk(e_w, c), bank[4 + c], chunk(e_w, c), ALU.add).then_inc(sem("e_oT"), 1)
            ln_dve(dve, 6, banks(0, 4).rearrange("p (t d) -> p t d", d=D), lambda c: dve.wait_ge(sem("e_ot"), c + 1))
            dve.wait_ge(sem("e_sg"), 1)
            for c in range(NC):
                dve.wait_ge(sem("ln_T"), 4 * NC + c + 1)
                dve.tensor_tensor(chunk(e_w, c), chunk(e_w, c), chunk(e_sg, c), ALU.mult).then_inc(sem("e_gated"), 1)
            for c in range(NC):
                dve.wait_ge(sem("e_proj"), c + 1)
                dve.tensor_tensor(x_tok[:, 4 * c:4 * c + 4, :], bank[c].rearrange("p (t d) -> p t d", d=D),
                                  x_tok[:, 4 * c:4 * c + 4, :], ALU.add).then_inc(sem("x_done"), 1)

        rf = Room()
        f_ind = rf.take(NT * NE).rearrange("p (t e) -> p t e", e=NE)
        f_lg = rf.take(NT * NE).rearrange("p (t e) -> p t e", e=NE)
        f_ex = rf.take(NT * NE).rearrange("p (t e) -> p t e", e=NE)
        f_mx, f_se, f_mp, f_top = (rf.take(NT) for _ in range(4))
        f_indT = rf.take(T, BF16)
        f_sel = rf.take((NE + 1) * P, BF16)
        f_xe = [rf.take(CH) for _ in range(2)]
        f_sa = [rf.take(CH) for _ in range(4)]
        f_h = [rf.take(CH) for _ in range(4)]
        JOBS = 5
        TURNS = NE // 2

        def over_experts(a):
            return a.unsqueeze(2).broadcast_to([P, NT, NE])

        def f_sp(sp):
            sp.wait_ge(sem("e_o"), len(LEVELS) * RH)
            for s in range(2):
                sp.dma_start(ring[:, s, :], we_d[s, :, :]).then_inc(sem(f"f_w{s}"), 16)
            with sp.Fori(0, TURNS - 1) as r:
                for s in range(2):
                    sp.wait_ge(sem("f_y"), r * 8 + 4 * s + 4)
                    sp.dma_start(ring[:, s, :], we_d[bass.ds(r * 2 + 2 + s, 1), :, :]
                                 .rearrange("e p n -> p (e n)")).then_inc(sem(f"f_w{s}"), 16)

        def f_pool(pool):
            ln_pool(pool, 7)

        def f_pe(pe):
            ln_pe(pe, 7, 5)
            for c in range(NC):
                pe.wait_ge(sem("ln_T"), 5 * NC + c + 1)
                for t in range(4):
                    tt = 4 * c + t
                    ins = pe.matmul(bank[0][:, tt * NE:(tt + 1) * NE], xnT[:, tt * P:(tt + 1) * P], w("router"),
                                    start=True, stop=True)
            ins.then_inc(sem("f_logits"), 1)
            for c in range(NC):
                pe.matmul(bank[4 + c], zeros[:, 0:P], zeros[:, :], start=True, stop=False, skip_group_check=True)
            pe.wait_ge(sem("f_ind"), 1)
            for tt in range(NT):
                ins = pe.transpose(banks(0, 4)[0:NE, tt * P:(tt + 1) * P], f_ind[:, tt, :], ident)
            ins.then_inc(sem("f_indp"), 1)
            pe.wait_ge(sem("f_indT"), 1)

            def token_mask(e, c, pair):
                pe.matmul(bank[2 * pair], f_sel[:, bass.ds(e * P, P)], chunk(f_indT, c), start=True, stop=True)\
                  .then_inc(sem("f_bc"), 1)

            def hidden(u, v, c, slot, j, pair):
                m = u * JOBS + 1 + j
                pe.wait_ge(sem("f_left"), m)
                weights = ring[:, slot, :]
                pe.matmul(bank[2 * pair], weights[:, j * P:(j + 1) * P], f_xe[v % 2], start=True, stop=True)\
                  .then_inc(sem("f_A"), 1)
                pe.matmul(bank[2 * pair + 1], weights[:, HID + j * P:HID + (j + 1) * P], f_xe[v % 2],
                          start=True, stop=True).then_inc(sem("f_G"), 1)

            def down(u, c, slot, j, last=False):
                pe.wait_ge(sem("f_left"), u * JOBS + 3 + j)
                for t in range(4):
                    ins = pe.matmul(bank[4 + c][:, t * P:(t + 1) * P], f_h[j][:, t * P:(t + 1) * P],
                                    ring[:, slot, 2 * HID + j * P:2 * HID + (j + 1) * P],
                                    start=False, stop=(j == 3), skip_group_check=True)
                if j == 3:
                    ins.then_inc(sem("f_y"), 1)

            token_mask(0, 0, 0)
            with pe.Fori(0, TURNS) as r:
                for v in range(8):
                    slot, c = v // 4, v % 4
                    u = r * 8 + v
                    pair = lambda j: (v * JOBS + 1 + j) % 2
                    if c == 0:
                        pe.wait_ge(sem(f"f_w{slot}"), r * 16 + 16)
                    pe.wait_ge(sem("f_left"), u * JOBS + 2)
                    hidden(u, v, c, slot, 0, pair(0))
                    for j in range(1, 4):
                        hidden(u, v, c, slot, j, pair(j))
                        down(u, c, slot, j - 1)
                    pe.wait_ge(sem("f_left"), u * JOBS + 5)
                    token_mask(r * 2 + (v + 1) // 4, (c + 1) % 4, pair(4))
                    down(u, c, slot, 3)

        def f_act(act):
            ln_act(act, 5)
            act.wait_ge(sem("f_rel"), 1)
            act.activation(f_ex, f_lg, ACT.Exp).then_inc(sem("f_ex"), 1)
            with act.Fori(0, TURNS * 4) as r:
                for v in range(2):
                    for j in range(4):
                        act.wait_ge(sem("f_A"), r * 8 + 4 * v + j + 1)
                        act.activation(f_sa[j], bank[2 * ((v * JOBS + 1 + j) % 2)], ACT.Silu)\
                           .then_inc(sem("f_sa"), 1)

        def f_dve(dve):
            dve.tensor_copy(f_sel, const("expert")).then_inc(sem("f_sel"), 1)
            link(dve, "dve", dve.memset(f_indT, 0.0))
            ln_dve(dve, 7, x_tok, lambda c: dve.wait_ge(sem("x_done"), 3 * NC + c + 1))
            dve.wait_ge(sem("f_logits"), 1)
            logits = bank[0][:, 0:NT * NE].rearrange("p (t e) -> p t e", e=NE)
            link(dve, "dve", dve.tensor_tensor(f_lg, logits, row("rb").unsqueeze(1).broadcast_to([P, NT, NE]), ALU.add))
            link(dve, "dve", dve.tensor_reduce(f_mx, f_lg, AX.X, ALU.max))
            dve.tensor_tensor(f_lg, f_lg, over_experts(f_mx), ALU.subtract).then_inc(sem("f_rel"), 1)
            dve.wait_ge(sem("f_ex"), 1)
            dve.tensor_reduce(f_se, f_ex, AX.X, ALU.add)
            link(dve, "dve", dve.tensor_reduce(f_top, f_ex, AX.X, ALU.max))
            link(dve, "dve", dve.reciprocal(f_se, f_se))
            link(dve, "dve", dve.tensor_tensor(f_mp, f_top, f_se, ALU.mult))
            link(dve, "dve", dve.tensor_tensor(f_lg, f_ex, over_experts(f_top), ALU.is_equal))
            link(dve, "dve", dve.tensor_tensor(f_lg, f_lg, const("evals").unsqueeze(1).broadcast_to([P, NT, NE]),
                                               ALU.mult))
            link(dve, "dve", dve.tensor_reduce(f_mx, f_lg, AX.X, ALU.max))
            dve.tensor_tensor(f_ind, f_lg, over_experts(f_mx), ALU.is_equal).then_inc(sem("f_ind"), 1)
            dve.wait_ge(sem("f_indp"), 1)
            dve.tensor_copy(f_indT[0:NE, :], banks(0, 4)[0:NE, :]).then_inc(sem("f_indT"), 1)

            def tokens(count, c, v, pair):
                dve.wait_ge(sem("f_bc"), count)
                dve.tensor_tensor(f_xe[v % 2], bank[2 * pair], chunk(xnT, c), ALU.mult).then_inc(sem("f_left"), 1)

            dve.nop().then_inc(sem("f_left"), 1)
            tokens(1, 0, 0, 0)
            with dve.Fori(0, TURNS) as r:
                for v in range(8):
                    u = r * 8 + v
                    for j in range(4):
                        dve.wait_ge(sem("f_G"), u * 4 + j + 1)
                        dve.wait_ge(sem("f_sa"), u * 4 + j + 1)
                        dve.tensor_tensor(f_h[j], bank[2 * ((v * JOBS + 1 + j) % 2) + 1], f_sa[j], ALU.mult)\
                           .then_inc(sem("f_left"), 1)
                    tokens(u + 2, (v + 1) % 4, v + 1, (v * JOBS + 5) % 2)
            dve.wait_ge(sem("f_y"), TURNS * 8)
            for c in range(NC):
                for t in range(4):
                    tt = 4 * c + t
                    ins = dve.scalar_tensor_tensor(out=x_tok[:, tt, :], in0=bank[4 + c][:, t * P:(t + 1) * P],
                                                   scalar=f_mp[:, tt:tt + 1], in1=x_tok[:, tt, :],
                                                   op0=ALU.mult, op1=ALU.add)
                ins.then_inc(sem("x_done"), 1)

        stages = "ABCDEF"[:"ABCDEF".index(stop) + 1]
        programs = {k: v for k, v in locals().items()}

        def run(eng, name):
            for s in stages:
                f = programs.get(f"{s.lower()}_{name}")
                if s == "B" and name != "sp":
                    eng.wait_ge(sem("w_load"), 32)
                if f is not None:
                    f(eng)

        block = ctx.enter_context(nc.Block())

        @block.sync
        def _(sp):
            for c in range(NC):
                sp.dma_start(x_tok[:, 4 * c:4 * c + 4, :], x_d[c * CH:(c + 1) * CH, :].rearrange("(t p) d -> p t d", p=P))\
                  .then_inc(sem(f"x_load{c}"), 16)
            sp.dma_start(C[:, 0:P], c_d[:, 0:P]).then_inc(sem("ident_load"), 16)
            sp.dma_start(W[:, 0:512], w_d[:, 0:512]).then_inc(sem("wa_load"), 16)
            sp.dma_start(V[:, :], v_d).then_inc(sem("wa_load"), 16)
            sp.dma_start(R[:, :], r_d.broadcast_to([P, RN])).then_inc(sem("row_load"), 16)
            for j in range(4):
                a_load(sp, j, j)
            sp.dma_start(C[:, P:CN], c_d[:, P:CN]).then_inc(sem("w_load"), 16)
            sp.dma_start(W[:, 512:WN], w_d[:, 512:WN]).then_inc(sem("w_load"), 16)
            run(sp, "sp")
            sp.wait_ge(sem("a_x"), NT)
            sp.wait_ge(sem("x_done"), NC * (len(stages) - 1))
            sp.dma_start(out_d.rearrange("(t p) d -> p t d", p=P), x_tok[:, :, :]).then_inc(sem("stored"), 16)
            sp.wait_ge(sem("stored"), 16)

        @block.tensor
        def _(pe):
            run(pe, "pe")

        @block.scalar
        def _(act):
            run(act, "act")

        @block.vector
        def _(dve):
            dve.memset(neg_half[:, :], -0.5).then_inc(sem("half"), 1)
            run(dve, "dve")

        @block.gpsimd
        def _(pool):
            pool.wait_ge(sem("half"), 1)
            run(pool, "pool")


def packed(cols, rows, parts):
    at, n = columns(cols)
    out = np.zeros((rows, n), np.float32)
    for name, a in parts.items():
        lo, k = at[name]
        out[:a.shape[0], lo:lo + k] = a
    assert set(parts) == {c for c, _ in cols}
    return out


def arranged(i):
    g = {k: np.asarray(v) for k, v in i.items()}
    col = lambda a, n=1: a.reshape(n, P).T
    W = packed(WCOLS, P, {
        "wq": g["L0_xattn_Wq"], "wk": g["L0_xattn_Wk"], "wv": g["L0_xattn_Wv"], "woT": g["L0_xattn_Wo"].T,
        "winT": g["L0_attn_w_in"].T, "wdtT": g["L0_attn_w_dt"].T, "wBT": g["L0_attn_w_B"].T,
        "wCT": g["L0_attn_w_C"].T, "woutT": g["L0_attn_w_out"].T,
        "w1T": g["L0_ffn_w1"].T, "w2T": g["L0_ffn_w2"].T.reshape(4, P, D).transpose(1, 0, 2).reshape(P, 512),
        "xq": g["L1_xattn_w_q"], "xk": g["L1_xattn_w_k"], "xv": g["L1_xattn_w_v"], "xo": g["L1_xattn_w_o"],
        "rW1T": g["L1_attn_xp_W1"].T, "rW2Ta": g["L1_attn_xp_W2"].T[0:128], "rW2Tb": g["L1_attn_xp_W2"].T[128:160],
        "rrT": g["L1_attn_r_W"].T, "rwAT": g["L1_attn_w_A"].T, "rwBT": g["L1_attn_w_B"].T,
        "rkT": g["L1_attn_k_W"].T, "rvT": g["L1_attn_v_W"].T, "rgAT": g["L1_attn_g_A"].T,
        "rgBT": g["L1_attn_g_B"].T, "roT": g["L1_attn_o_W"].T, "router": g["L1_ffn_router_w"]})
    V = packed(VCOLS, P, {
        "bq": col(g["L0_xattn_bq"]), "bv": col(g["L0_xattn_bv"]), "bin": col(g["L0_attn_b_in"], 2),
        "bdt": col(g["L0_attn_b_dt"]), "alog": g["L0_attn_A_log"], "Dskip": col(g["L0_attn_D"]),
        "convw": g["L0_ffn_conv_w"].reshape(4, P, 3).transpose(1, 0, 2).reshape(P, 12),
        "convb": col(g["L0_ffn_conv_b"], 4),
        "xbq": col(g["L1_xattn_b_q"]), "xbk": col(g["L1_xattn_b_k"]), "xbv": col(g["L1_xattn_b_v"]),
        "mu": col(g["L1_attn_xp_mu"]), "xbias": g["L1_attn_x_bias"].T, "wb": col(g["L1_attn_w_b"], 4),
        "gb": col(g["L1_attn_g_b"]), "bonus": g["L1_attn_bonus"].T, "gnw": col(g["L1_attn_gn_w"]),
        "gnb": col(g["L1_attn_gn_b"])})
    R = packed(RCOLS, 1, {n: g[k].reshape(1, -1) for n, k in (
        ("bo", "L0_xattn_bo"), ("bout", "L0_attn_b_out"), ("gamma", "L0_attn_gamma"), ("beta", "L0_attn_beta"),
        ("xbo", "L1_xattn_b_o"), ("bB", "L0_attn_b_B"), ("bC", "L0_attn_b_C"), ("rb", "L1_ffn_router_b"))})
    ctxn = np.zeros((B, 3 * KW, D), np.float32)
    ctxn[:, 0:K2] = g["ctx_1024"]
    ctxT = ctxn.reshape(NT, 4, K2P, D).transpose(0, 3, 1, 2).reshape(NT, D, 4 * K2P)
    ctxn = ctxn.reshape(NT, 4, 3, KW, D).transpose(0, 3, 1, 2, 4).reshape(NT, KW, 4 * 3 * D)
    return {
        "x": g["x"].reshape(T, D), "ctxn": ctxn, "ctxT": ctxT,
        "mask": g["mask_Bx1xSxS2_bk1"].reshape(B, S, K2),
        "w": W, "v": V, "r": R, "c": shape_constants(),
        "we": np.concatenate([g["L1_ffn_w1"], g["L1_ffn_w2"].reshape(NE, 4, P, D).transpose(0, 2, 1, 3)
                              .reshape(NE, P, HID)], 2)}


def kernel(**inputs):
    import concourse.bacc as bacc
    from concourse.bass_utils import run_bass_kernel_spmd

    nc = bacc.Bacc("TRN2", target_bir_lowering=False, num_devices=1)
    arrays, args = {}, []
    for name, a in arranged(inputs).items():
        a = np.ascontiguousarray(a)
        arrays[f"in_{name}"] = a
        args.append(nc.dram_tensor(f"in_{name}", a.shape, mybir.dt.from_np(a.dtype), kind="ExternalInput").ap())
    args.append(nc.dram_tensor("out", (T, D), F32, kind="ExternalOutput").ap())
    build_program(nc, *args)
    r = run_bass_kernel_spmd(nc, [arrays], core_ids=[0])
    return r.results[0]["out"].reshape(B, S, D)
```
